# Optimizing a Trainium2 kernel written in Bass

```python
import numpy as np
import jax
import jax.numpy as jnp

def _softmax(x, axis=-1):
    return jax.nn.softmax(x, axis=axis)

def _gelu(x):
    return jax.nn.gelu(x, approximate=True)

def _silu(x):
    return jax.nn.silu(x)

def _sigmoid(x):
    return jax.nn.sigmoid(x)

def _layernorm(x, axis=-1, eps=1e-05):
    m = jnp.mean(x, axis=axis, keepdims=True)
    v = jnp.var(x, axis=axis, keepdims=True)
    return (x - m) / jnp.sqrt(v + eps)

def _scatter_add(tgt, idx, src, axis=0):
    return tgt.at[idx].add(src)

def _segment_sum(src, seg, n):
    return jax.ops.segment_sum(src, seg, n)
kernel_name = 'mk_flamingo_gated_d1_seqx_r4_15021d'

def setup_inputs(seed: int=0):
    np.random.seed(seed)
    _w = jnp.asarray

    def _rec_inputs():
        import jax
        import jax.numpy as jnp
        _rk = jax.random.key(seed)
        x = -7.109e-05 + 0.9999 * jax.random.normal(jax.random.fold_in(_rk, 1), (4, 512, 512), jnp.float32)
        _lenS = 512 - jax.random.randint(jax.random.fold_in(_rk, 7), (4,), 0, max(1, 512 // 4) + 1, jnp.int32)
        _lenS2 = 512 - jax.random.randint(jax.random.fold_in(_rk, 8), (4,), 0, max(1, 512 // 4) + 1, jnp.int32)
        _ctx_2048P = jax.random.normal(jax.random.fold_in(_rk, 11), (4, 16, 512), jnp.float32)
        _ctx_2048c = jax.random.dirichlet(jax.random.fold_in(_rk, 511), 0.3 * jnp.ones((16,), jnp.float32), (4, 512))
        _ctx_2048t = jnp.einsum('bsk,bkd->bsd', _ctx_2048c, _ctx_2048P)
        _ctx_2048t = _ctx_2048t * jax.lax.rsqrt(jnp.mean(jnp.square(_ctx_2048t)) + 1e-12) * 0.953939
        ctx_2048 = -3.05549e-07 + 0.0199987 * (_ctx_2048t + 0.3 * jax.random.normal(jax.random.fold_in(_rk, 611), (4, 512, 512), jnp.float32))
        _g = jax.random.normal(jax.random.fold_in(_rk, 9001), (2, 1), jnp.float32)
        _g = jnp.sign(_g) * jnp.maximum(jnp.abs(_g), 1.0) + (_g == 0) * 1.0
        g_xattn = _g[0]
        g_ffn = _g[1]
        return (x, ctx_2048, g_xattn, g_ffn)
    x, ctx_2048, g_xattn, g_ffn = _rec_inputs()

    def _L0_xattn_setup():
        import jax, jax.numpy as jnp
        import numpy as np
        FP8_MAX = 448.0
        ACT_EPS = 0.0001
        W_EPS = 1e-06
        BLK = 128

        def quant_dequant_act_1x128(x):
            E, M, K = x.shape
            xb = x.reshape(E, M, K // BLK, BLK)
            amax = jnp.max(jnp.abs(xb), axis=-1, keepdims=True)
            safe = jnp.maximum(amax, ACT_EPS)
            q = (xb * (FP8_MAX / safe)).astype(jnp.float8_e4m3fn)
            return (q.astype(jnp.float32) * (safe / FP8_MAX)).reshape(E, M, K)

        def quant_dequant_weight_128x128(w):
            E, N, K = w.shape
            wb = w.reshape(E, N // BLK, BLK, K // BLK, BLK)
            amax = jnp.max(jnp.abs(wb), axis=(2, 4), keepdims=True)
            safe = jnp.maximum(amax, W_EPS)
            q = (wb * (FP8_MAX / safe)).astype(jnp.float8_e4m3fn)
            return (q.astype(jnp.float32) * (safe / FP8_MAX)).reshape(E, N, K)
        key = jax.random.key(seed)
        kx, kw = jax.random.split(key)
        E, M, K, N = (8, 1024, 512, 512)
        x = jax.random.normal(kx, (E, M, K), dtype=jnp.float32)
        weight = jax.random.normal(kw, (E, N, K), dtype=jnp.float32) * 0.02
        return {'x': x, 'weight': weight}
    _L0_xattn_all = _L0_xattn_setup()
    _L0_xattn_in = {k: v for k, v in _L0_xattn_all.items() if k in ()}
    del _L0_xattn_all

    def _L0_ffn_setup():
        import jax, jax.numpy as jnp
        import numpy as np
        LN_EPS = 1e-05
        L2_EPS = 1e-12

        def _l2norm(v, axis):
            n = jnp.sqrt(jnp.sum(v * v, axis=axis, keepdims=True))
            return v / jnp.maximum(n, L2_EPS)
        key = jax.random.key(seed)
        ks = jax.random.split(key, 4)
        B, N, D, E, S, H = (8, 512, 512, 16, 128, 128)
        x = jax.random.normal(ks[0], (B, N, D), dtype=jnp.float32)
        mu = jax.random.normal(ks[1], (D, E, S), dtype=jnp.float32) / np.sqrt(D)
        W1 = jax.random.normal(ks[2], (E, D, H), dtype=jnp.float32) * np.sqrt(2.0 / D)
        W2 = jax.random.normal(ks[3], (E, H, D), dtype=jnp.float32) * np.sqrt(2.0 / (H + D))
        return {'x': x, 'gamma': jnp.ones((D,), jnp.float32), 'beta': jnp.zeros((D,), jnp.float32), 'mu': mu, 'scale': jnp.ones((1,), jnp.float32), 'W1': W1, 'b1': jnp.zeros((E, H), jnp.float32), 'W2': W2, 'b2': jnp.zeros((E, D), jnp.float32)}
    _L0_ffn_all = _L0_ffn_setup()
    _L0_ffn_in = {k: v for k, v in _L0_ffn_all.items() if k in ('gamma', 'beta', 'mu', 'scale', 'W1', 'b1', 'W2', 'b2')}
    del _L0_ffn_all
    return {'x': x, 'ctx_2048': ctx_2048, 'g_xattn': g_xattn, 'g_ffn': g_ffn, 'L0_ffn_gamma': _L0_ffn_in['gamma'], 'L0_ffn_beta': _L0_ffn_in['beta'], 'L0_ffn_mu': _L0_ffn_in['mu'], 'L0_ffn_scale': _L0_ffn_in['scale'], 'L0_ffn_W1': _L0_ffn_in['W1'], 'L0_ffn_b1': _L0_ffn_in['b1'], 'L0_ffn_W2': _L0_ffn_in['W2'], 'L0_ffn_b2': _L0_ffn_in['b2']}

def reference(x, ctx_2048, g_xattn, g_ffn, L0_ffn_gamma, L0_ffn_beta, L0_ffn_mu, L0_ffn_scale, L0_ffn_W1, L0_ffn_b1, L0_ffn_W2, L0_ffn_b2):
    import jax
    import jax.numpy as jnp

    def _L0_xattn_ref(x, weight):
        import jax, jax.numpy as jnp
        import numpy as np
        FP8_MAX = 448.0
        ACT_EPS = 0.0001
        W_EPS = 1e-06
        BLK = 128

        def quant_dequant_act_1x128(x):
            E, M, K = x.shape
            xb = x.reshape(E, M, K // BLK, BLK)
            amax = jnp.max(jnp.abs(xb), axis=-1, keepdims=True)
            safe = jnp.maximum(amax, ACT_EPS)
            q = (xb * (FP8_MAX / safe)).astype(jnp.float8_e4m3fn)
            return (q.astype(jnp.float32) * (safe / FP8_MAX)).reshape(E, M, K)

        def quant_dequant_weight_128x128(w):
            E, N, K = w.shape
            wb = w.reshape(E, N // BLK, BLK, K // BLK, BLK)
            amax = jnp.max(jnp.abs(wb), axis=(2, 4), keepdims=True)
            safe = jnp.maximum(amax, W_EPS)
            q = (wb * (FP8_MAX / safe)).astype(jnp.float8_e4m3fn)
            return (q.astype(jnp.float32) * (safe / FP8_MAX)).reshape(E, N, K)
        xq = quant_dequant_act_1x128(x)
        wq = quant_dequant_weight_128x128(weight)
        return jnp.einsum('emk,enk->emn', xq, wq)

    def _L0_ffn_ref(x, gamma, beta, mu, scale, W1, b1, W2, b2):
        import jax, jax.numpy as jnp
        import numpy as np
        LN_EPS = 1e-05
        L2_EPS = 1e-12

        def _l2norm(v, axis):
            n = jnp.sqrt(jnp.sum(v * v, axis=axis, keepdims=True))
            return v / jnp.maximum(n, L2_EPS)
        B, N, D = x.shape
        _, E, S = mu.shape
        mean = jnp.mean(x, axis=-1, keepdims=True)
        var = jnp.mean(jnp.square(x - mean), axis=-1, keepdims=True)
        x_ln = (x - mean) / jnp.sqrt(var + LN_EPS) * gamma + beta
        x_n = _l2norm(x_ln, -1) * scale
        mu_n = _l2norm(mu, 0)
        logits = jnp.einsum('bnd,des->bnes', x_n, mu_n)
        dispatch = jax.nn.softmax(logits, axis=1)
        combine = jax.nn.softmax(logits.reshape(B, N, E * S), axis=-1)
        slot_in = jnp.einsum('bnd,bnes->besd', x_ln, dispatch)
        h = jax.nn.gelu(jnp.einsum('besd,edh->besh', slot_in, W1) + b1[None, :, None, :], approximate=False)
        slot_out = jnp.einsum('besh,ehd->besd', h, W2) + b2[None, :, None, :]
        out = jnp.einsum('bsd,bns->bnd', slot_out.reshape(B, E * S, D), combine)
        return out
    x = x + jnp.tanh(g_xattn[0]) * _L0_xattn_ref(_layernorm(x, axis=-1), ctx_2048)
    x = x + jnp.tanh(g_ffn[0]) * _L0_ffn_ref(_layernorm(x, axis=-1), L0_ffn_gamma, L0_ffn_beta, L0_ffn_mu, L0_ffn_scale, L0_ffn_W1, L0_ffn_b1, L0_ffn_W2, L0_ffn_b2)
    return x

_drawn_inputs = setup_inputs


def setup_inputs(seed=0):
    import zlib

    import numpy as np

    out = dict(_drawn_inputs(seed))
    spreads = {'L0_ffn_gamma': (1.0, 0.6),
     'L0_ffn_beta': (0.0, 0.8),
     'L0_ffn_b1': (0.0, 0.8),
     'L0_ffn_b2': (0.0, 0.372)}
    factors = {'L0_ffn_mu': 8.0, 'L0_ffn_W1': 5.27, 'L0_ffn_W2': 4.446}
    for name, (base, spread) in spreads.items():
        noise = np.random.default_rng([zlib.crc32(name.encode()), seed]).standard_normal(out[name].shape)
        drawn = base * np.exp(spread * noise) if base else spread * noise
        out[name] = jnp.asarray(drawn.astype(out[name].dtype))
    for name, factor in factors.items():
        out[name] = (out[name] * factor).astype(out[name].dtype)
    return out
```

```python
from contextlib import ExitStack

import concourse.bass as bass
from concourse import mybir

ALU = mybir.AluOpType
ACT = mybir.ActivationFunctionType
AX_X = mybir.AxisListType.X
F32 = mybir.dt.float32
F32R = mybir.dt.float32r
F16 = mybir.dt.float16
BF16 = mybir.dt.bfloat16
I32 = mybir.dt.int32

P = 128
FP8_MAX = 448.0
ACT_EPS, W_EPS = 1e-4, 1e-6
LN_EPS, L2_EPS = 1e-5, 1e-12
EXP_MASK = 0x7F800000
UNIT = 2.0 ** 13
LOGIT_ROOM = 60.0


def flamingo_block(nc, x, ctx_w, g_xattn, g_ffn, gamma, beta, mu, scale, w1, b1, w2, b2, out):
    B, N, D = x.shape
    _, E, S = mu.shape
    H = w1.shape[2]
    KD = D // P
    NT = N // P
    G = 4
    NG = E // G
    W = G * S
    assert S == P and H == P and N == 512 and D == 512 and W == 512 and NG == 4 and NT == 4 and KD == 4

    x_rows = x.rearrange("b n d -> (b n) d")
    ctx_rows = ctx_w.rearrange("b n d -> (b n) d")
    out_rows = out.rearrange("b n d -> (b n) d")
    mu_dram = mu.rearrange("(k p) e s -> p k (e s)", p=P)
    w1_dram = w1.rearrange("e (k p) h -> p k e h", p=P)
    w2_dram = w2.rearrange("e h d -> h e d")
    b1_flat = b1.rearrange("e h -> (e h)")

    with ExitStack() as es:
        def sb(name, shape, dt=F32):
            return es.enter_context(nc.sbuf_tensor(name, shape, dt))

        def sem(name):
            return es.enter_context(nc.semaphore(name))

        acc = [es.enter_context(nc.psum_tensor(f"acc{t}", [P, D], F32)) for t in range(NT)]
        ps_l = es.enter_context(nc.psum_tensor("ps_l", [P, N], F32))
        ps_zh = es.enter_context(nc.psum_tensor("ps_zh", [P, N], F32))
        ps_t = es.enter_context(nc.psum_tensor("ps_t", [P, N], F32))
        ps_y = es.enter_context(nc.psum_tensor("ps_y", [P, N], F32))

        ident = sb("ident", [P, P])
        ident16 = sb("ident16", [P, P], BF16)
        gx = sb("gx", [P, 1])
        gf = sb("gf", [P, 1])
        sc_in = sb("sc_in", [P, 1])
        tgx = sb("tgx", [P, 1])
        tgf = sb("tgf", [P, 1])
        half = sb("half", [P, 1])
        mhalf = sb("mhalf", [P, E])
        logit_scale = sb("logit_scale", [P, 1])
        shift = sb("shift", [P, 1])
        gam = sb("gam", [P, D])
        bet = sb("bet", [P, D])
        b1_bc = sb("b1_bc", [P, W])
        b2_hi = sb("b2_hi", [E, D], F32R)
        b2_lo = sb("b2_lo", [E, D], F32R)
        mu_hi = sb("mu_hi", [P, KD, E * S], F16)
        mu_lo = sb("mu_lo", [P, KD, E * S], F16)
        mu_norm = sb("mu_norm", [P, 2, E])
        w1_hi = sb("w1_hi", [P, KD, E * H], F16)
        w1_lo = sb("w1_lo", [P, KD, E * H], F16)
        w1_max = sb("w1_max", [P, KD])
        w1_unit = sb("w1_unit", [P, 5])
        w2_raw = sb("w2_raw", [P, D])
        w2_hi = sb("w2_hi", [P, 2, D], F32R)
        w2_lo = sb("w2_lo", [P, 2, D], F32R)

        work = sb("work", [P, 2, 2, D])
        q16 = sb("q16", [P, 2, D], BF16)
        qT = sb("qT", [P, NT, KD, P], BF16)
        wT = sb("wT", [P, KD, N], BF16)
        x1 = sb("x1", [P, NT, D])
        stat = sb("stat", [P, 2, 8])
        norm = sb("norm", [P, 2, 6])
        amax = sb("amax", [P, 2, 4])
        amax_all = sb("amax_all", [P, 2, 4])
        quant = sb("quant", [P, 2, 4])
        x_dequant = sb("x_dequant", [P, NT, 4])
        w_dequant = sb("w_dequant", [P, KD, NT])
        dequant = sb("dequant", [P, 2, KD, NT])
        uT_hi = sb("uT_hi", [P, 2 * KD * N], F16)
        uT_lo = sb("uT_lo", [P, 2 * KD * N], F16)
        y_scale = sb("y_scale", [P, 2 * NT])

        eT = sb("eT", [P, G, N])
        den = sb("den", [P, G])
        rden = sb("rden", [P, G])
        hn = sb("hn", [P, G, H])
        mass = sb("mass", [P, 2 * NT, E])
        mass_sum = sb("mass_sum", [P, NT, E])
        z_row = sb("z_row", [P, NT])
        z_inv = sb("z_inv", [P, NT])
        with nc.sbuf_tensor("prod", [P, 2, D], F32) as prod:
            pass
        massT_hi = sb("massT_hi", [E, N], F32R)
        massT_lo = sb("massT_lo", [E, N], F32R)
        b2_raw, diag, ones = prod[0:E, 0, :], prod[:, 1, 0:2 * P].rearrange("p (a c) -> p a c", c=P), hn[:, 0, :]

        with nc.sbuf_tensor("mu_raw", [P, KD, E * S], F32) as mu_raw, nc.sbuf_tensor("w1_raw", [P, KD, E * H], F32) as w1_raw:
            pass
        e_hi = sb("e_hi", [P, G, NT, S], F32R)
        e_lo = sb("e_lo", [P, G, NT, S], F32R)
        y_hi = sb("y_hi", [P, NT, W], F32R)
        y_lo = sb("y_lo", [P, NT, W], F32R)
        eT_hi = sb("eT_hi", [P, G, N], F32R)
        eT_lo = sb("eT_lo", [P, G, N], F32R)
        h_hi = sb("h_hi", [P, G, H], F32R)
        h_lo = sb("h_lo", [P, G, H], F32R)
        z_hi = sb("z_hi", [P, N], F32R)
        z_lo = sb("z_lo", [P, N], F32R)
        last = sb("last", [P, NT, D])

        x1_dram = nc.dram_tensor("x1_dram", [B * N, D], F32, kind="Internal").ap()

        consts_in, b2_in, b1_in = sem("consts_in"), sem("b2_in"), sem("b1_in")
        mu_in = [sem(f"mu_in{i}") for i in range(KD)]
        w1_in = [sem(f"w1_in{i}") for i in range(KD)]
        w2_in = sem("w2_in")
        x_in = [sem(f"x_in{t}") for t in range(NT)]
        ctx_in = [sem(f"ctx_in{i}") for i in range(2)]
        x1_stored = [sem(f"x1_stored{t}") for t in range(NT)]
        last_in = [sem(f"last_in{t}") for t in range(NT)]
        out_written = [sem(f"out_written{t}") for t in range(NT)]
        pool_const, ones_done = sem("pool_const"), sem("ones_done")
        tanh_done, dve_small, dve_w1 = sem("tanh_done"), sem("dve_small"), sem("dve_w1")
        mu_squared, mu_summed, mu_clamped, mu_rooted = sem("mu_squared"), sem("mu_summed"), sem("mu_clamped"), sem("mu_rooted")
        mu_diag, mu_spread, mu_scaled, mu_hi_done, mu_lo_done = sem("mu_diag"), sem("mu_spread"), sem("mu_scaled"), sem("mu_hi_done"), sem("mu_lo_done")
        w1_all_max, w1_hi_done, w1_lo_done = sem("w1_all_max"), sem("w1_hi_done"), sem("w1_lo_done")
        w_amax_done, w_amax_all = sem("w_amax_done"), sem("w_amax_all")
        x_var_done, x_rstd_done = sem("x_var_done"), sem("x_rstd_done")
        q_scale_done, q_scaled, q_step_done = sem("q_scale_done"), sem("q_scaled"), sem("q_step_done")
        q_done, q_turned, q_copied = sem("q_done"), sem("q_turned"), sem("q_copied")
        prod_done, prod_scaled, prod_added = sem("prod_done"), sem("prod_scaled"), sem("prod_added")
        var1_done, rstd1_done, var2_done, rstd2_done = sem("var1_done"), sem("rstd1_done"), sem("var2_done"), sem("rstd2_done")
        ln_done, affine_done, squares_done, l2_done = sem("ln_done"), sem("affine_done"), sem("squares_done"), sem("l2_done")
        rl2_done, unit_done, unit_turned, uT_hi_done, uT_lo_done = (sem("rl2_done"), sem("unit_done"), sem("unit_turned"),
                                                                    sem("uT_hi_done"), sem("uT_lo_done"))
        dve_early, dve_link, pool_early, pool_link = sem("dve_early"), sem("dve_link"), sem("pool_early"), sem("pool_link")
        w2_half, w2_split, held = sem("w2_half"), sem("w2_split"), sem("held")
        l_done, y_done, h_done, z_done, t_done, f_done = (sem("l_done"), sem("y_done"), sem("h_done"), sem("z_done"),
                                                          sem("t_done"), sem("f_done"))
        exp_done, gelu_done, y_hi_done, z_hi_done, e_hi_done = (sem("exp_done"), sem("gelu_done"), sem("y_hi_done"),
                                                                sem("z_hi_done"), sem("e_hi_done"))
        rden_done, hn_done, hb_done, h_hi_done, h_lo_done = (sem("rden_done"), sem("hn_done"), sem("hb_done"),
                                                             sem("h_hi_done"), sem("h_lo_done"))
        y_lo_done, z_lo_done, eT_hi_done, eT_lo_done = sem("y_lo_done"), sem("z_lo_done"), sem("eT_hi_done"), sem("eT_lo_done")
        e_lo_done, e_sum_done = sem("e_lo_done"), sem("e_sum_done")
        mass_sum_done, mass_turned, mass_split, zr_done = (sem("mass_sum_done"), sem("mass_turned"), sem("mass_split"),
                                                            sem("zr_done"))
        sums_done, out_ready = sem("sums_done"), sem("out_ready")

        W1_LINKS, DVE_LINKS, POOL_LINKS = KD + 5, 72, 12
        EARLY_BANKS = (ps_y, ps_l, ps_zh, ps_t)
        FIRST_Q = 3 * NT

        class Chain:

            def __init__(self, engine, semaphore, start=0):
                self.engine, self.semaphore, self.start, self.count = engine, semaphore, start, 0

            def then(self, instruction):
                self.count += 1
                instruction.then_inc(self.semaphore, 1)
                self.engine.wait_ge(self.semaphore, self.start + self.count)

        def hold(engine):
            engine.sem_inc(held, 1)

        def by_block(ap):
            return ap.rearrange("p (k c) -> p k c", c=P)

        def spread(ap, n=P):
            return ap.rearrange("p (k a) -> p k a", a=1).to_broadcast([P, 4, n])

        def flat(ap):
            return ap.rearrange("p a b -> p (a b)")

        def nth(b, t):
            return b * NT + t

        def nth_product(b, t, kb):
            return b * (NT * KD) + ((t // 2) * 2 * KD + 2 * kb + t % 2)

        def banks16(bank):
            return bank[:, 0:D // 2].bitcast(BF16)

        def u_view(u, par, t):
            return u[:, :].rearrange("p (a k n) -> p a k n", a=2, k=KD)[:, bass.ds(par, 1), :, t * P:(t + 1) * P].rearrange(
                "p a k n -> p (a k) n")

        block = es.enter_context(nc.Block())

        @block.sync
        def _(sp):
            def load_ctx(b, t, n, later):
                if later:
                    sp.wait_ge(q_done, n - 1)
                sp.dma_start(work[:, t % 2, 0, :], ctx_rows[bass.ds((b % B) * N + t * P, P), :]).then_inc(ctx_in[t % 2], 16)

            def load_x(b, t):
                sp.dma_start(x1[:, t, :], x_rows[bass.ds(b * N + t * P, P), :]).then_inc(x_in[t], 16)

            def store_x1(b, t):
                sp.wait_ge(prod_added, nth_product(b, t, KD - 1) + 1)
                sp.dma_start(x1_dram[bass.ds(b * N + t * P, P), :], x1[:, t, :]).then_inc(x1_stored[t], 16)

            def load_b1(n, g):
                if n is not None:
                    sp.wait_ge(hb_done, n)
                sp.dma_start(b1_bc[:, :], b1_flat[bass.ds(g * W, W)].partition_broadcast(P)).then_inc(b1_in, 16)

            def outputs(b):
                for t in range(NT):
                    sp.wait_ge(out_written[t], (b + 1) * 16)
                    sp.wait_ge(x1_stored[t], b * 16 + 16)
                    sp.dma_start(last[:, t, :], x1_dram[bass.ds(b * N + t * P, P), :]).then_inc(last_in[t], 16)
                for t in range(NT):
                    sp.wait_ge(out_ready, nth(b, t) + 1)
                    sp.dma_start(out_rows[bass.ds(b * N + t * P, P), :], last[:, t, :]).then_inc(out_written[t], 16)

            for t in range(NT):
                sp.sem_inc(out_written[t], 16)
            for t in range(2):
                load_ctx(0, t, t, False)
            for t in range(NT):
                load_x(0, t)
            for dst, src in ((gx, g_xattn), (gf, g_ffn), (sc_in, scale), (gam, gamma), (bet, beta)):
                sp.dma_start(dst[:, :], src.partition_broadcast(P)).then_inc(consts_in, 16)
            for k in range(KD):
                sp.dma_start(mu_raw[:, k, :], mu_dram[:, k]).then_inc(mu_in[k], 16)
                sp.dma_start(w1_raw[:, k, :].rearrange("p (c h) -> p c h", h=H), w1_dram[:, k]).then_inc(w1_in[k], 16)
            sp.dma_start(b2_raw, b2).then_inc(b2_in, 16)
            for t in range(2, NT):
                load_ctx(0, t, t, True)
            load_b1(None, 0)
            for t in range(NT):
                store_x1(0, t)
            sp.wait_ge(unit_turned, NT)
            for t in range(NT):
                load_ctx(1, t, 2 * NT + t, True)
            with sp.Fori(0, B - 1) as b:
                for t in range(NT):
                    sp.wait_ge(x1_stored[t], b * 16 + 16)
                    load_x(b + 1, t)
                load_b1(b * NG + 1, 1)
                load_b1(b * NG + 2, 2)
                store_x1(b + 1, 0)
                store_x1(b + 1, 1)
                load_b1(b * NG + 3, 3)
                store_x1(b + 1, 2)
                store_x1(b + 1, 3)
                sp.wait_ge(unit_turned, nth(b + 1, NT - 1) + 1)
                n = b * (2 * NT) + (FIRST_Q + NT)
                load_ctx(b + 2, 0, n, True)
                load_ctx(b + 2, 1, n + 1, True)
                load_b1(b * NG + 4, 0)
                load_ctx(b + 2, 2, n + 2, True)
                load_ctx(b + 2, 3, n + 3, True)
                outputs(b)
            for g in range(1, NG):
                load_b1((B - 1) * NG + g, g)
            outputs(B - 1)
            for t in range(NT):
                sp.wait_ge(out_written[t], 16 * B + 16)

        @block.gpsimd
        def _(pool):
            def reduce_weights(b, t):
                w = t % 2
                pool.wait_ge(w_amax_done, nth(b, t) + 1)
                hold(pool)
                nc.gpsimd.partition_all_reduce(amax_all[:, w, :], amax[:, w, :], P, bass.bass_isa.ReduceOp.max).then_inc(w_amax_all, 1)

            def root(b, t, col_in, waits, col_out, exponent, done):
                w = t % 2
                pool.wait_ge(waits, nth(b, t) + 1)
                src = stat[:, w, 7:8] if col_in is None else norm[:, w, col_in:col_in + 1]
                nc.gpsimd.tensor_tensor(norm[:, w, col_out:col_out + 1], src, exponent, ALU.pow).then_inc(done, 1)

            def x_rstd(b, t):
                root(b, t, None, x_var_done, 0, mhalf[:, 0:1], x_rstd_done)

            def rstd1(b, t):
                root(b, t, None, var1_done, 1, mhalf[:, 0:1], rstd1_done)

            def rstd2(b, t):
                root(b, t, None, var2_done, 2, mhalf[:, 0:1], rstd2_done)

            def l2(b, t):
                root(b, t, 3, squares_done, 4, half[:, :], l2_done)

            def round_(n, w, link, first=False):
                a, m = work[:, w, 0, :], work[:, w, 1, :]
                pool.wait_ge(q_step_done, n + 1)
                link.then(nc.gpsimd.tensor_tensor(a, a, m, ALU.add))
                if not first:
                    pool.wait_ge(q_turned, n - 1)
                nc.gpsimd.tensor_tensor(q16[:, w, :], a, m, ALU.subtract).then_inc(q_done, 1)

            def add(b, t, kb):
                pool.wait_ge(prod_scaled, nth_product(b, t, kb) + 1)
                nc.gpsimd.tensor_tensor(x1[:, t, :], x1[:, t, :], prod[:, t % 2, :], ALU.add).then_inc(prod_added, 1)

            def affine(b, t, link):
                y = work[:, t % 2, 0, :]
                pool.wait_ge(ln_done, nth(b, t) + 1)
                link.then(nc.gpsimd.tensor_tensor(y, y, gam[:, :], ALU.mult))
                nc.gpsimd.tensor_tensor(y, y, bet[:, :], ALU.add).then_inc(affine_done, 1)

            def load_w2(b, e):
                hold(pool)
                pool.dma_start(w2_raw[:, :], w2_dram[:, e, :]).then_inc(w2_in, 16)

            def split_w2(b, e):
                i, s = b * E + e, e % 2
                pool.wait_ge(w2_in, i * 16 + 16)
                pool.wait_ge(f_done, i + 1)
                hold(pool)
                nc.gpsimd.tensor_scalar(w2_hi[:, s, :], w2_raw[:, :], 1.0, 1.0, ALU.mult, ALU.mult).then_inc(w2_half, 1)
                pool.wait_ge(w2_half, i + 1)
                nc.gpsimd.tensor_tensor(w2_lo[:, s, :], w2_raw[:, :], w2_hi[:, s, :].bitcast(F32), ALU.subtract).then_inc(w2_split, 1)
                pool.wait_ge(w2_split, i + 1)
                load_w2(b, (e + 1) % E)

            c = Chain(pool, pool_const)
            c.then(nc.gpsimd.memset(mhalf[:, :], -0.5))
            c.then(nc.gpsimd.memset(half[:, :], 0.5))
            c.then(nc.gpsimd.memset(ident[:, :], 0.0))
            c.then(nc.gpsimd.affine_select(out=ident[:, :], in_=ident[:, :], compare_op=ALU.not_equal, fill=1.0,
                                           base=0, pattern=[[-1, P]], channel_multiplier=1))
            c.then(nc.gpsimd.tensor_copy(ident16[:, :], ident[:, :]))
            nc.gpsimd.memset(ones, 1.0).then_inc(ones_done, 1)
            load_w2(0, 0)
            link = Chain(pool, pool_early)
            for t in range(0, NT, 2):
                for i in (t, t + 1):
                    reduce_weights(0, i)
                for i in (t, t + 1):
                    round_(i, i % 2, link, first=(i < 2))
            for t in range(0, NT, 2):
                for i in (t, t + 1):
                    x_rstd(0, i)
                for i in (t, t + 1):
                    round_(NT + i, i % 2, link)
            pool.wait_ge(dve_w1, KD + 1)
            nc.gpsimd.partition_all_reduce(w1_unit[:, 1:2], w1_unit[:, 0:1], P, bass.bass_isa.ReduceOp.max).then_inc(w1_all_max, 1)
            pool.wait_ge(mu_clamped, 1)
            nc.gpsimd.tensor_tensor(mu_norm[:, 1, :], mu_norm[:, 0, :], mhalf[:, :], ALU.pow).then_inc(mu_rooted, 1)
            for k in range(KD):
                pool.wait_ge(mu_hi_done, k + 1)
                nc.gpsimd.tensor_tensor(mu_lo[:, k, :], mu_raw[:, k, :], mu_hi[:, k, :], ALU.subtract).then_inc(mu_lo_done, 1)
            for t in range(0, NT, 2):
                for kb in range(KD):
                    for i in (t, t + 1):
                        add(0, i, kb)
                for stage in (rstd1, rstd2, lambda b, i: affine(b, i, link), l2):
                    for i in (t, t + 1):
                        stage(0, i)
            for t in range(0, NT, 2):
                for i in (t, t + 1):
                    reduce_weights(1, i)
                for i in (t, t + 1):
                    round_(2 * NT + i, i % 2, link)

            def batch(b, aside):
                link = Chain(pool, pool_link, b * POOL_LINKS)
                n_x, n_w = b * (2 * NT) + FIRST_Q, b * (2 * NT) + (FIRST_Q + NT)
                for g in range(NG):
                    e = g * G
                    split_w2(b, e)
                    split_w2(b, e + 1)
                    if not aside:
                        split_w2(b, e + 2)
                        split_w2(b, e + 3)
                    elif g == 0:
                        x_rstd(b + 1, 0)
                        x_rstd(b + 1, 1)
                        split_w2(b, e + 2)
                        round_(n_x, 0, link)
                        round_(n_x + 1, 1, link)
                        x_rstd(b + 1, 2)
                        x_rstd(b + 1, 3)
                        split_w2(b, e + 3)
                        add(b + 1, 0, 0)
                        add(b + 1, 1, 0)
                        round_(n_x + 2, 0, link)
                        add(b + 1, 0, 1)
                        round_(n_x + 3, 1, link)
                        add(b + 1, 1, 1)
                        add(b + 1, 0, 2)
                    elif g == 1:
                        split_w2(b, e + 2)
                        add(b + 1, 1, 2)
                        add(b + 1, 0, 3)
                        add(b + 1, 1, 3)
                        rstd1(b + 1, 0)
                        split_w2(b, e + 3)
                        add(b + 1, 2, 0)
                        rstd1(b + 1, 1)
                        add(b + 1, 3, 0)
                        rstd2(b + 1, 0)
                        add(b + 1, 2, 1)
                        rstd2(b + 1, 1)
                        add(b + 1, 3, 1)
                        affine(b + 1, 0, link)
                        add(b + 1, 2, 2)
                        affine(b + 1, 1, link)
                        add(b + 1, 3, 2)
                    elif g == 2:
                        l2(b + 1, 0)
                        l2(b + 1, 1)
                        add(b + 1, 2, 3)
                        add(b + 1, 3, 3)
                        split_w2(b, e + 2)
                        rstd1(b + 1, 2)
                        rstd1(b + 1, 3)
                        rstd2(b + 1, 2)
                        rstd2(b + 1, 3)
                        affine(b + 1, 2, link)
                        affine(b + 1, 3, link)
                        l2(b + 1, 2)
                        l2(b + 1, 3)
                        split_w2(b, e + 3)
                    else:
                        reduce_weights(b + 2, 0)
                        reduce_weights(b + 2, 1)
                        round_(n_w, 0, link)
                        split_w2(b, e + 2)
                        round_(n_w + 1, 1, link)
                        reduce_weights(b + 2, 2)
                        reduce_weights(b + 2, 3)
                        split_w2(b, e + 3)
                        round_(n_w + 2, 0, link)
                        round_(n_w + 3, 1, link)
                assert link.count in (0, POOL_LINKS), link.count

            with pool.Fori(0, B - 1) as b:
                batch(b, True)
            batch(B - 1, False)

        @block.scalar
        def _(act):
            def scale_blocks(n, w):
                act.wait_ge(q_scale_done, n + 1)
                a = work[:, w, 0, :]
                for kb in range(KD):
                    cols = slice(kb * P, (kb + 1) * P)
                    ins = nc.scalar.activation(a[:, cols], a[:, cols], ACT.Copy, scale=quant[:, w, kb:kb + 1])
                ins.then_inc(q_scaled, 1)

            def keep_w(n, t, bank):
                act.wait_ge(q_turned, n + 1)
                nc.scalar.activation(wT[:, :, t * P:(t + 1) * P], by_block(banks16(bank)), ACT.Copy).then_inc(q_copied, 1)

            def keep_x(n, t, bank):
                act.wait_ge(q_turned, n + 1)
                nc.scalar.activation(qT[:, t, :, :], by_block(banks16(bank)), ACT.Copy).then_inc(q_copied, 1)

            def squares(b, t):
                act.wait_ge(affine_done, nth(b, t) + 1)
                w = t % 2
                nc.scalar.activation(work[:, w, 1, :], work[:, w, 0, :], ACT.Square, accum_out=norm[:, w, 3:4]).then_inc(squares_done, 1)

            def unit(b, t):
                act.wait_ge(rl2_done, nth(b, t) + 1)
                w = t % 2
                nc.scalar.activation(work[:, w, 0, :], work[:, w, 0, :], ACT.Copy, scale=norm[:, w, 5:6]).then_inc(unit_done, 1)

            def keep_u(b, t, par, bank):
                act.wait_ge(unit_turned, nth(b, t) + 1)
                hold(act)
                nc.scalar.activation(u_view(uT_hi, par, t), by_block(bank[:, :]), ACT.Copy).then_inc(uT_hi_done, 1)

            def exp(i, j, reused):
                act.wait_ge(l_done, i + j + 1)
                if reused:
                    act.wait_ge(t_done, i + j - 3)
                    act.wait_ge(eT_lo_done, i + j - 3)
                nc.scalar.activation(eT[:, j, :], ps_l[:, :], ACT.Exp, bias=shift[:, :], scale=logit_scale[:, :],
                                     accum_out=den[:, j:j + 1]).then_inc(exp_done, 1)

            def split_y(i, j, par):
                act.wait_ge(y_done, i + j + 1)
                hold(act)
                nc.scalar.activation(y_hi[:, j, :], ps_y[:, :], ACT.Copy, scale=y_scale[:, bass.ds(par * NT + j, 1)]).then_inc(y_hi_done, 1)

            def split_e(i, j):
                act.wait_ge(t_done, i + j + 1)
                nc.scalar.activation(e_hi[:, j, :, :], ps_t[:, :].rearrange("p (t s) -> p t s", s=S), ACT.Copy).then_inc(e_hi_done, 1)

            def split_z(i, j):
                act.wait_ge(z_done, i + j + 1)
                nc.scalar.activation(z_hi[:, :], ps_zh[:, :], ACT.Copy).then_inc(z_hi_done, 1)

            def group(b, g, follows, par, aside):
                i = b * E + g * G
                act.wait_ge(hb_done, b * NG + g + 1)
                nc.scalar.activation(hn[:, :, :], hn[:, :, :], ACT.Gelu).then_inc(gelu_done, 1)
                aside(g, "h")
                for j in range(G):
                    if follows and j == 0:
                        exp(i + G, 0, True)
                        split_y(i + G, 0, par)
                    split_z(i, j)
                    if follows and j + 1 < G:
                        exp(i + G, j + 1, True)
                    aside(g, f"z{j}")
                    if follows and j + 1 < G:
                        split_y(i + G, j + 1, par)
                    aside(g, f"y{j}")
                    if follows:
                        split_e(i + G, j)
                    aside(g, f"e{j}")

            def batch(b, follows):
                n_x, n_w = b * (2 * NT) + FIRST_Q, b * (2 * NT) + (FIRST_Q + NT)
                this, after = b % 2, (b + 1) % 2

                def aside(g, at):
                    if not follows:
                        return
                    at = (g, at)
                    if at == (0, "y0"):
                        scale_blocks(n_x, 0)
                        scale_blocks(n_x + 1, 1)
                    elif at == (0, "y1"):
                        keep_x(n_x, 0, ps_l)
                    elif at == (0, "e1"):
                        keep_x(n_x + 1, 1, ps_y)
                    elif at == (0, "z2"):
                        scale_blocks(n_x + 2, 0)
                        scale_blocks(n_x + 3, 1)
                    elif at == (1, "z0"):
                        keep_x(n_x + 2, 2, ps_t)
                    elif at == (1, "y0"):
                        keep_x(n_x + 3, 3, ps_l)
                    elif at == (2, "h"):
                        squares(b + 1, 0)
                        squares(b + 1, 1)
                    elif at == (2, "y0"):
                        unit(b + 1, 0)
                        unit(b + 1, 1)
                    elif at == (2, "e0"):
                        keep_u(b + 1, 0, after, ps_y)
                    elif at == (2, "y1"):
                        keep_u(b + 1, 1, after, ps_t)
                        squares(b + 1, 2)
                    elif at == (2, "e1"):
                        squares(b + 1, 3)
                        unit(b + 1, 2)
                        unit(b + 1, 3)
                    elif at == (2, "y2"):
                        keep_u(b + 1, 2, after, ps_t)
                    elif at == (2, "e2"):
                        keep_u(b + 1, 3, after, ps_l)
                    elif at == (3, "z0"):
                        scale_blocks(n_w, 0)
                        scale_blocks(n_w + 1, 1)
                    elif at == (3, "y1"):
                        keep_w(n_w, 0, ps_l)
                        scale_blocks(n_w + 2, 0)
                        scale_blocks(n_w + 3, 1)
                    elif at == (3, "e1"):
                        keep_w(n_w + 1, 1, ps_y)
                    elif at == (3, "y2"):
                        keep_w(n_w + 2, 2, ps_l)
                    elif at == (3, "e2"):
                        keep_w(n_w + 3, 3, ps_y)

                for g in range(NG):
                    group(b, g, follows or g < NG - 1, after if g == NG - 1 else this, aside)

            act.wait_ge(consts_in, 16 * 5)
            nc.scalar.activation(tgx[:, :], gx[:, :], ACT.Tanh).then_inc(tanh_done, 1)
            nc.scalar.activation(tgf[:, :], gf[:, :], ACT.Tanh).then_inc(tanh_done, 1)
            for n in range(0, 2 * NT, 2):
                keep = keep_w if n < NT else keep_x
                scale_blocks(n, 0)
                scale_blocks(n + 1, 1)
                keep(n, n % NT, ps_t)
                keep(n + 1, n % NT + 1, ps_y)
            for k in range(KD):
                act.wait_ge(mu_in[k], 16)
                if k >= 1:
                    act.wait_ge(mu_summed, k)
                nc.scalar.activation(flat(eT[:, :, :]), mu_raw[:, k, :], ACT.Square).then_inc(mu_squared, 1)
            for k in range(KD):
                act.wait_ge(w1_in[k], 16)
                if k == 0:
                    act.wait_ge(dve_w1, W1_LINKS)
                nc.scalar.activation(w1_hi[:, k, :], w1_raw[:, k, :], ACT.Copy, scale=w1_unit[:, 3:4]).then_inc(w1_hi_done, 1)
                act.wait_ge(mu_scaled, k + 1)
                nc.scalar.activation(mu_hi[:, k, :], mu_raw[:, k, :], ACT.Copy).then_inc(mu_hi_done, 1)
            for t in range(0, NT, 2):
                for stage in (squares, unit):
                    for i in (t, t + 1):
                        stage(0, i)
                keep_u(0, t, 0, ps_t)
                keep_u(0, t + 1, 0, ps_y)
            for j in range(G):
                exp(0, j, False)
                split_y(0, j, 0)
                split_e(0, j)
            for n in range(2 * NT, 3 * NT, 2):
                scale_blocks(n, 0)
                scale_blocks(n + 1, 1)
                keep_w(n, n % NT, ps_l)
                keep_w(n + 1, n % NT + 1, ps_y)
            with act.Fori(0, B - 1) as b:
                batch(b, True)
            batch(B - 1, False)

        @block.vector
        def _(dve):
            def statistics(src, w, link, done):
                link.then(nc.vector.bn_stats(stat[:, w, 0:6], src))
                hold(dve)
                link.then(nc.vector.bn_aggr(stat[:, w, 6:8], stat[:, w, 0:6]))
                nc.vector.tensor_scalar(stat[:, w, 7:8], stat[:, w, 7:8], LN_EPS, None, ALU.add).then_inc(done, 1)

            def standardise(dst, src, w, col, waits, n):
                dve.wait_ge(waits, n + 1)
                return nc.vector.tensor_scalar(dst, src, stat[:, w, 6:7], norm[:, w, col:col + 1], ALU.subtract, ALU.mult)

            def w_amax(b, t):
                dve.wait_ge(ctx_in[t % 2], b * 32 + (t // 2) * 16 + 16)
                nc.vector.tensor_reduce(amax[:, t % 2, :], by_block(work[:, t % 2, 0, :]), AX_X, ALU.max,
                                        apply_absolute_value=True).then_inc(w_amax_done, 1)

            def w_scale(b, t, n, link):
                w = t % 2
                dve.wait_ge(w_amax_all, nth(b, t) + 1)
                link.then(nc.vector.tensor_scalar(w_dequant[:, :, t], amax_all[:, w, :], W_EPS, 1.0 / FP8_MAX, ALU.max, ALU.mult))
                nc.vector.reciprocal(quant[:, w, :], w_dequant[:, :, t]).then_inc(q_scale_done, 1)

            def x_stats(b, t, link):
                dve.wait_ge(x_in[t], b * 16 + 16)
                statistics(x1[:, t, :], t % 2, link, x_var_done)

            def x_scale(b, t, n, link, first=False):
                w = t % 2
                a = work[:, w, 0, :]
                dve.wait_ge(q_done, n - 1)
                link.then(standardise(a, x1[:, t, :], w, 0, x_rstd_done, nth(b, t)))
                link.then(nc.vector.tensor_reduce(amax[:, w, :], by_block(a), AX_X, ALU.max, apply_absolute_value=True))
                link.then(nc.vector.tensor_scalar(x_dequant[:, t, :], amax[:, w, :], ACT_EPS, 1.0 / FP8_MAX, ALU.max, ALU.mult))
                link.then(nc.vector.reciprocal(quant[:, w, :], x_dequant[:, t, :]))
                nc.vector.tensor_scalar(x_dequant[:, t, :], x_dequant[:, t, :], tgx[:, :], None, ALU.mult).then_inc(q_scale_done, 1)

            def step(n, w, link):
                a, m = work[:, w, 0, :], work[:, w, 1, :]
                dve.wait_ge(q_scaled, n + 1)
                link.then(nc.vector.tensor_scalar(m.bitcast(I32), a.bitcast(I32), EXP_MASK, None, ALU.bitwise_and))
                nc.vector.tensor_scalar(m, m, 2.0 ** -6, 1.5 * 2.0 ** 20, ALU.max, ALU.mult).then_inc(q_step_done, 1)

            def dequants(t, link):
                link.then(nc.vector.tensor_tensor(dequant[:, t % 2, :, :], spread(x_dequant[:, t, :], NT), w_dequant[:, :, :], ALU.mult))

            def scale_product(b, t, kb, bank, first=False):
                n, w = nth_product(b, t, kb), t % 2
                dve.wait_ge(prod_done, n + 1)
                if not first:
                    dve.wait_ge(prod_added, n - 1)
                nc.vector.tensor_tensor(by_block(prod[:, w, :]), by_block(bank[:, :]), spread(dequant[:, w, kb, :]), ALU.mult).then_inc(prod_scaled, 1)

            def stats1(b, t, link):
                dve.wait_ge(prod_added, nth_product(b, t, KD - 1) + 1)
                statistics(x1[:, t, :], t % 2, link, var1_done)

            def stats2(b, t, link):
                y = work[:, t % 2, 0, :]
                if t >= 2:
                    dve.wait_ge(unit_turned, nth(b, t) - 1)
                link.then(standardise(y, x1[:, t, :], t % 2, 1, rstd1_done, nth(b, t)))
                statistics(y, t % 2, link, var2_done)

            def layernorm(b, t):
                y = work[:, t % 2, 0, :]
                standardise(y, y, t % 2, 2, rstd2_done, nth(b, t)).then_inc(ln_done, 1)

            def rl2(b, t, par, link):
                w = t % 2
                dve.wait_ge(l2_done, nth(b, t) + 1)
                link.then(nc.vector.tensor_scalar(norm[:, w, 4:5], norm[:, w, 4:5], L2_EPS, None, ALU.max))
                link.then(nc.vector.tensor_scalar(y_scale[:, bass.ds(par * NT + t, 1)], norm[:, w, 4:5], w1_unit[:, 4:5], None, ALU.mult))
                link.then(nc.vector.reciprocal(norm[:, w, 5:6], norm[:, w, 4:5]))
                nc.vector.tensor_scalar(norm[:, w, 5:6], norm[:, w, 5:6], UNIT, None, ALU.mult).then_inc(rl2_done, 1)

            def split_u(b, t, par, bank):
                dve.wait_ge(uT_hi_done, nth(b, t) + 1)
                nc.vector.tensor_tensor(u_view(uT_lo, par, t), by_block(bank[:, :]), u_view(uT_hi, par, t), ALU.subtract).then_inc(uT_lo_done, 1)

            def split_y(i, j, par):
                dve.wait_ge(y_hi_done, i + j + 1)
                nc.vector.scalar_tensor_tensor(y_lo[:, j, :], ps_y[:, :], y_scale[:, bass.ds(par * NT + j, 1)], y_hi[:, j, :].bitcast(F32),
                                               ALU.mult, ALU.subtract).then_inc(y_lo_done, 1)

            def split_z(i, j):
                dve.wait_ge(z_hi_done, i + j + 1)
                nc.vector.tensor_tensor(z_lo[:, :], ps_zh[:, :], z_hi[:, :].bitcast(F32), ALU.subtract).then_inc(z_lo_done, 1)

            def split_eT(i, j, reused):
                dve.wait_ge(exp_done, i + j + 1)
                if reused:
                    dve.wait_ge(z_done, i + j - 3)
                nc.vector.tensor_copy(eT_hi[:, j, :], eT[:, j, :]).then_inc(eT_hi_done, 1)
                dve.wait_ge(eT_hi_done, i + j + 1)
                nc.vector.tensor_tensor(eT_lo[:, j, :], eT[:, j, :], eT_hi[:, j, :].bitcast(F32), ALU.subtract).then_inc(eT_lo_done, 1)

            def split_e(i, e, j, par):
                dve.wait_ge(e_hi_done, i + j + 1)
                nc.vector.tensor_tensor(e_lo[:, j, :, :].rearrange("p t s -> p (t s)"), ps_t[:, :],
                                        e_hi[:, j, :, :].rearrange("p t s -> p (t s)").bitcast(F32), ALU.subtract).then_inc(e_lo_done, 1)
                nc.vector.tensor_reduce(mass[:, bass.ds(par * NT, NT), e + j], ps_t[:, :].rearrange("p (t s) -> p t s", s=S), AX_X,
                                        ALU.add).then_inc(e_sum_done, 1)

            def group(b, g, follows, par, aside):
                i, n = b * E + g * G, b * NG + g + 1
                dve.wait_ge(exp_done, i + G)
                nc.vector.reciprocal(rden[:, :], den[:, :]).then_inc(rden_done, 1)
                dve.wait_ge(rden_done, n)
                dve.wait_ge(h_done, n)
                nc.vector.tensor_tensor(hn[:, :, :], by_block(ps_zh[:, :]), spread(rden[:, :]), ALU.mult).then_inc(hn_done, 1)
                dve.wait_ge(hn_done, n)
                dve.wait_ge(b1_in, n * 16)
                nc.vector.tensor_tensor(hn[:, :, :], hn[:, :, :], by_block(b1_bc[:, :]), ALU.add).then_inc(hb_done, 1)
                dve.wait_ge(gelu_done, n)
                nc.vector.tensor_copy(h_hi[:, :, :], hn[:, :, :]).then_inc(h_hi_done, 1)
                dve.wait_ge(h_hi_done, n)
                nc.vector.tensor_tensor(h_lo[:, :, :], hn[:, :, :], h_hi[:, :, :].bitcast(F32), ALU.subtract).then_inc(h_lo_done, 1)
                aside(g, "h")
                if follows:
                    split_y(i + G, 0, par)
                for j in range(G):
                    split_z(i, j)
                    if follows:
                        split_eT(i + G, j, True)
                    aside(g, f"z{j}")
                    if follows and j + 1 < G:
                        split_y(i + G, j + 1, par)
                    aside(g, f"y{j}")
                    if follows:
                        split_e(i + G, (g + 1) % NG * G, j, par)
                    aside(g, f"e{j}")

            def batch(b, follows):
                n_x, n_w = b * (2 * NT) + FIRST_Q, b * (2 * NT) + (FIRST_Q + NT)
                this, after = b % 2, (b + 1) % 2
                link = Chain(dve, dve_link, b * DVE_LINKS)

                def aside(g, at):
                    at = (g, at)
                    if at == (NG - 1, "z1"):
                        dve.wait_ge(mass_turned, b + 1)
                        nc.vector.tensor_copy(massT_hi[:, :], ps_t[0:E, :]).then_inc(mass_split, 1)
                        dve.wait_ge(mass_split, b * 2 + 1)
                        nc.vector.tensor_tensor(massT_lo[:, :], ps_t[0:E, :], massT_hi[:, :].bitcast(F32), ALU.subtract).then_inc(mass_split, 1)
                    if not follows:
                        return
                    if at == (0, "h"):
                        x_stats(b + 1, 0, link)
                        x_stats(b + 1, 1, link)
                    elif at == (0, "z0"):
                        x_scale(b + 1, 0, n_x, link)
                        x_scale(b + 1, 1, n_x + 1, link)
                    elif at == (0, "e0"):
                        step(n_x, 0, link)
                        step(n_x + 1, 1, link)
                    elif at == (0, "z1"):
                        x_stats(b + 1, 2, link)
                        x_stats(b + 1, 3, link)
                    elif at == (0, "e1"):
                        x_scale(b + 1, 2, n_x + 2, link)
                        x_scale(b + 1, 3, n_x + 3, link)
                    elif at == (0, "z2"):
                        dequants(0, link)
                        dequants(1, link)
                        scale_product(b + 1, 0, 0, ps_t)
                    elif at == (0, "y2"):
                        step(n_x + 2, 0, link)
                        step(n_x + 3, 1, link)
                        scale_product(b + 1, 1, 0, ps_l)
                    elif at == (0, "e2"):
                        scale_product(b + 1, 0, 1, ps_y)
                    elif at == (0, "z3"):
                        scale_product(b + 1, 1, 1, ps_y)
                    elif at == (0, "e3"):
                        scale_product(b + 1, 0, 2, ps_l)
                    elif at == (1, "e0"):
                        scale_product(b + 1, 1, 2, ps_y)
                    elif at == (1, "z1"):
                        scale_product(b + 1, 0, 3, ps_t)
                    elif at == (1, "y1"):
                        scale_product(b + 1, 1, 3, ps_l)
                        stats1(b + 1, 0, link)
                    elif at == (1, "e1"):
                        dequants(2, link)
                        dequants(3, link)
                        scale_product(b + 1, 2, 0, ps_y)
                        stats1(b + 1, 1, link)
                    elif at == (1, "z2"):
                        scale_product(b + 1, 3, 0, ps_t)
                        stats2(b + 1, 0, link)
                    elif at == (1, "y2"):
                        scale_product(b + 1, 2, 1, ps_l)
                        stats2(b + 1, 1, link)
                    elif at == (1, "e2"):
                        scale_product(b + 1, 3, 1, ps_y)
                        layernorm(b + 1, 0)
                    elif at == (1, "z3"):
                        scale_product(b + 1, 2, 2, ps_y)
                        layernorm(b + 1, 1)
                    elif at == (1, "e3"):
                        scale_product(b + 1, 3, 2, ps_l)
                    elif at == (2, "h"):
                        rl2(b + 1, 0, after, link)
                        rl2(b + 1, 1, after, link)
                    elif at == (2, "z0"):
                        scale_product(b + 1, 2, 3, ps_t)
                    elif at == (2, "y0"):
                        scale_product(b + 1, 3, 3, ps_l)
                        stats1(b + 1, 2, link)
                        stats1(b + 1, 3, link)
                    elif at == (2, "e0"):
                        split_u(b + 1, 0, after, ps_y)
                    elif at == (2, "z1"):
                        split_u(b + 1, 1, after, ps_t)
                        stats2(b + 1, 2, link)
                        stats2(b + 1, 3, link)
                    elif at == (2, "y1"):
                        layernorm(b + 1, 2)
                        layernorm(b + 1, 3)
                    elif at == (2, "e1"):
                        rl2(b + 1, 2, after, link)
                        rl2(b + 1, 3, after, link)
                    elif at == (2, "y2"):
                        split_u(b + 1, 2, after, ps_t)
                    elif at == (2, "e2"):
                        split_u(b + 1, 3, after, ps_l)
                    elif at == (3, "h"):
                        w_amax(b + 2, 0)
                        w_amax(b + 2, 1)
                    elif at == (3, "z0"):
                        w_scale(b + 2, 0, n_w, link)
                        w_scale(b + 2, 1, n_w + 1, link)
                    elif at == (3, "y0"):
                        step(n_w, 0, link)
                        step(n_w + 1, 1, link)
                    elif at == (3, "z1"):
                        w_amax(b + 2, 2)
                        w_amax(b + 2, 3)
                    elif at == (3, "y1"):
                        w_scale(b + 2, 2, n_w + 2, link)
                        w_scale(b + 2, 3, n_w + 3, link)
                    elif at == (3, "e1"):
                        step(n_w + 2, 0, link)
                        step(n_w + 3, 1, link)

                for g in range(NG):
                    if g == NG - 1:
                        dve.wait_ge(e_sum_done, b * E + E)
                        nc.vector.tensor_copy(mass_sum[:, :, :], mass[:, bass.ds(this * NT, NT), :]).then_inc(mass_sum_done, 1)
                        nc.vector.tensor_reduce(z_row[:, :], mass[:, bass.ds(this * NT, NT), :], AX_X, ALU.add).then_inc(zr_done, 1)
                        dve.wait_ge(zr_done, b * 3 + 1)
                        nc.vector.reciprocal(z_inv[:, :], z_row[:, :]).then_inc(zr_done, 1)
                        dve.wait_ge(zr_done, b * 3 + 2)
                        nc.vector.tensor_scalar(z_inv[:, :], z_inv[:, :], tgf[:, :], None, ALU.mult).then_inc(zr_done, 1)
                    group(b, g, follows or g < NG - 1, after if g == NG - 1 else this, aside)
                assert not follows or link.count == DVE_LINKS, link.count
                dve.wait_ge(sums_done, b + 1)
                for t in range(NT):
                    dve.wait_ge(last_in[t], b * 16 + 16)
                    nc.vector.scalar_tensor_tensor(last[:, t, :], acc[t][:, :], z_inv[:, t:t + 1], last[:, t, :], ALU.mult,
                                                   ALU.add).then_inc(out_ready, 1)

            link = Chain(dve, dve_early)
            dve.wait_ge(tanh_done, 2)
            for t in range(0, NT, 2):
                for i in (t, t + 1):
                    w_amax(0, i)
                for i in (t, t + 1):
                    w_scale(0, i, i, link)
                for i in (t, t + 1):
                    step(i, i % 2, link)
            for t in range(0, NT, 2):
                for i in (t, t + 1):
                    x_stats(0, i, link)
                for i in (t, t + 1):
                    x_scale(0, i, NT + i, link)
                for i in (t, t + 1):
                    step(NT + i, i % 2, link)
            w = Chain(dve, dve_w1)
            for k in range(KD):
                dve.wait_ge(w1_in[k], 16)
                w.then(nc.vector.tensor_reduce(w1_max[:, k:k + 1], w1_raw[:, k, :], AX_X, ALU.max, apply_absolute_value=True))
            w.then(nc.vector.tensor_reduce(w1_unit[:, 0:1], w1_max[:, :], AX_X, ALU.max))
            dve.wait_ge(w1_all_max, 1)
            w.then(nc.vector.tensor_scalar(w1_unit[:, 2:3].bitcast(I32), w1_unit[:, 1:2].bitcast(I32), EXP_MASK, None, ALU.bitwise_and))
            w.then(nc.vector.tensor_scalar(w1_unit[:, 2:3], w1_unit[:, 2:3], 2.0 ** -100, 2.0 ** -14, ALU.max, ALU.mult))
            w.then(nc.vector.reciprocal(w1_unit[:, 3:4], w1_unit[:, 2:3]))
            w.then(nc.vector.tensor_scalar(w1_unit[:, 4:5], w1_unit[:, 2:3], 1.0 / UNIT, None, ALU.mult))
            assert w.count == W1_LINKS
            dve.wait_ge(mu_summed, KD)
            nc.vector.tensor_scalar(mu_norm[:, 0, :], ps_l[:, 0:E], L2_EPS * L2_EPS, None, ALU.max).then_inc(mu_clamped, 1)
            dve.wait_ge(mu_rooted, 1)
            for e in range(E):
                if e >= 2:
                    dve.wait_ge(mu_spread, e - 1)
                nc.vector.tensor_scalar(diag[:, e % 2, :], ident[:, :], mu_norm[:, 1, e:e + 1], UNIT, ALU.mult, ALU.mult).then_inc(mu_diag, 1)
            dve.wait_ge(mu_spread, E)
            for k in range(KD):
                for i in range(NT):
                    cols = slice(i * W, (i + 1) * W)
                    ins = nc.vector.tensor_tensor(mu_raw[:, k, cols], mu_raw[:, k, cols], acc[i][:, :], ALU.mult)
                ins.then_inc(mu_scaled, 1)
                dve.wait_ge(w1_hi_done, k + 1)
                nc.vector.scalar_tensor_tensor(w1_lo[:, k, :], w1_raw[:, k, :], w1_unit[:, 3:4], w1_hi[:, k, :], ALU.mult,
                                               ALU.subtract).then_inc(w1_lo_done, 1)
            s = Chain(dve, dve_small)
            s.then(nc.vector.tensor_scalar(logit_scale[:, :], sc_in[:, :], 1.0 / (UNIT * UNIT), None, ALU.mult))
            s.then(nc.vector.tensor_reduce(shift[:, :], sc_in[:, :], AX_X, ALU.max, apply_absolute_value=True))
            s.then(nc.vector.tensor_scalar(shift[:, :], shift[:, :], LOGIT_ROOM, None, ALU.subtract))
            s.then(nc.vector.tensor_scalar(shift[:, :], shift[:, :], 0.0, -1.0, ALU.max, ALU.mult))
            dve.wait_ge(b2_in, 16)
            s.then(nc.vector.tensor_copy(b2_hi[:, :], b2_raw))
            s.then(nc.vector.tensor_tensor(b2_lo[:, :], b2_raw, b2_hi[:, :].bitcast(F32), ALU.subtract))
            for t in range(0, NT, 2):
                for i in (t, t + 1):
                    dequants(i, link)
                for kb in range(KD):
                    for i in (t, t + 1):
                        scale_product(0, i, kb, EARLY_BANKS[(2 * kb + i % 2) % 4], first=(i < 2 and kb == 0))
                for i in (t, t + 1):
                    stats1(0, i, link)
                for i in (t, t + 1):
                    stats2(0, i, link)
                for i in (t, t + 1):
                    layernorm(0, i)
                for i in (t, t + 1):
                    rl2(0, i, 0, link)
                split_u(0, t, 0, ps_t)
                split_u(0, t + 1, 0, ps_y)
            for j in range(G):
                split_y(0, j, 0)
                split_eT(0, j, False)
                split_e(0, 0, j, 0)
            for t in range(0, NT, 2):
                for i in (t, t + 1):
                    w_amax(1, i)
                for i in (t, t + 1):
                    w_scale(1, i, 2 * NT + i, link)
                for i in (t, t + 1):
                    step(2 * NT + i, i % 2, link)
            with dve.Fori(0, B - 1) as b:
                batch(b, True)
            batch(B - 1, False)

        @block.tensor
        def _(pe):
            def three(out, terms, start=True, stop=True, check=True):
                todo = []
                for a_hi, a_lo, b_hi, b_lo in terms:
                    todo += [(a_hi, b_hi), (a_hi, b_lo), (a_lo, b_hi)]
                for n, (a, c) in enumerate(todo):
                    ins = nc.tensor.matmul(out, a, c, start=start and n == 0, stop=stop and n == len(todo) - 1,
                                           skip_group_check=not check)
                return ins

            def turn_q(n, w, bank):
                pe.wait_ge(q_done, n + 1)
                for kb in range(KD):
                    ins = nc.tensor.transpose(banks16(bank)[:, kb * P:(kb + 1) * P], q16[:, w, kb * P:(kb + 1) * P], ident16[:, :])
                ins.then_inc(q_turned, 1)

            def product(b, t, kb, bank, n_q):
                pe.wait_ge(q_copied, n_q)
                nc.tensor.matmul(bank[:, :], qT[:, t, kb, :], wT[:, kb, :], start=True, stop=True).then_inc(prod_done, 1)

            def turn_u(b, t, bank):
                pe.wait_ge(unit_done, nth(b, t) + 1)
                for kb in range(KD):
                    ins = nc.tensor.transpose(bank[:, kb * P:(kb + 1) * P], work[:, t % 2, 0, kb * P:(kb + 1) * P], ident[:, :])
                ins.then_inc(unit_turned, 1)

            u_reg = pe.alloc_register("u_reg")

            def u_base(par):
                pe.reg_mov(u_reg, par * (KD * N))
                return pe.snap(u_reg, min_val=0, max_val=KD * N)

            def logits(i, j, g, par):
                cols = bass.ds(g * W + j * S, S)
                base = u_base(par)
                three(ps_l[:, :], [(mu_hi[:, k, cols], mu_lo[:, k, cols], uT_hi[:, bass.ds(base + k * N, N)],
                                    uT_lo[:, bass.ds(base + k * N, N)]) for k in range(KD)]).then_inc(l_done, 1)

            def project(i, j, g, par):
                cols = bass.ds(g * W, W)
                base = u_base(par)
                three(ps_y[:, :], [(uT_hi[:, bass.ds(base + (k * N + j * P), P)], uT_lo[:, bass.ds(base + (k * N + j * P), P)],
                                    w1_hi[:, k, cols], w1_lo[:, k, cols]) for k in range(KD)]).then_inc(y_done, 1)

            def turn(i, j):
                pe.wait_ge(exp_done, i + j + 1)
                for t in range(NT):
                    ins = nc.tensor.transpose(ps_t[:, t * P:(t + 1) * P], eT[:, j, t * P:(t + 1) * P], ident[:, :])
                ins.then_inc(t_done, 1)

            def slots(i):
                pe.wait_ge(e_lo_done, i + G)
                pe.wait_ge(y_lo_done, i + G)
                for j in range(G):
                    ins = three(ps_zh[:, j * H:(j + 1) * H], [(e_hi[:, j, t, :], e_lo[:, j, t, :], y_hi[:, t, j * H:(j + 1) * H],
                                                               y_lo[:, t, j * H:(j + 1) * H]) for t in range(NT)])
                ins.then_inc(h_done, 1)

            def combine(i, j, n):
                if j == 0:
                    pe.wait_ge(h_lo_done, n)
                else:
                    pe.wait_ge(z_lo_done, i + j)
                pe.wait_ge(eT_lo_done, i + j + 1)
                three(ps_zh[:, :], [(h_hi[:, j, :], h_lo[:, j, :], eT_hi[:, j, :], eT_lo[:, j, :])]).then_inc(z_done, 1)

            def expand(i, j, first=False):
                pe.wait_ge(z_lo_done, i + j + 1)
                pe.wait_ge(w2_split, i + j + 1)
                for t in range(NT):
                    rows = slice(t * P, (t + 1) * P)
                    ins = three(acc[t][:, :], [(z_hi[:, rows], z_lo[:, rows], w2_hi[:, j % 2, :], w2_lo[:, j % 2, :])], start=first,
                                stop=False, check=False)
                ins.then_inc(f_done, 1)

            def batch(b, follows):
                n_x, n_w = b * (2 * NT) + FIRST_Q, b * (2 * NT) + (FIRST_Q + NT)
                this, after = b % 2, (b + 1) % 2
                plan = {
                    (0, "c1"): ("x", 0), (0, "b1"): ("x", 1), (0, "a2"): ("p", 0, 0), (0, "c2"): ("p", 1, 0), (0, "b2"): ("p", 0, 1),
                    (0, "b3"): ("p", 1, 1), (0, "c3"): ("p", 0, 2),
                    (1, "a0"): ("x", 2), (1, "c0"): ("x", 3), (1, "b0"): ("p", 1, 2), (1, "a1"): ("p", 0, 3), (1, "c1"): ("p", 1, 3),
                    (1, "b1"): ("p", 2, 0), (1, "a2"): ("p", 3, 0), (1, "c2"): ("p", 2, 1), (1, "b2"): ("p", 3, 1), (1, "b3"): ("p", 2, 2),
                    (1, "c3"): ("p", 3, 2),
                    (2, "a0"): ("p", 2, 3), (2, "c0"): ("p", 3, 3), (2, "b0"): ("u", 0), (2, "a1"): ("u", 1), (2, "a2"): ("u", 2),
                    (2, "c2"): ("u", 3),
                    (3, "c1"): ("w", 0), (3, "b1"): ("w", 1), (3, "c2"): ("w", 2), (3, "b2"): ("w", 3),
                } if follows else {}
                plan[(3, "a1")] = ("m",)
                bank_of = {"a": ps_t, "b": ps_y, "c": ps_l}

                def read(g, place):
                    what = plan.get((g % NG, place))
                    if what is None:
                        return
                    kind = what[0]
                    if kind == "x":
                        pe.wait_ge(q_copied, n_x + what[1] + 1)
                    elif kind == "w":
                        pe.wait_ge(q_copied, n_w + what[1] + 1)
                    elif kind == "p":
                        pe.wait_ge(prod_scaled, nth_product(b + 1, what[1], what[2]) + 1)
                    elif kind == "u":
                        pe.wait_ge(uT_lo_done, nth(b + 1, what[1]) + 1)
                    else:
                        pe.wait_ge(mass_split, b * 2 + 2)

                def aside(g, place, i):
                    what = plan.get((g, place))
                    if what is None:
                        return
                    kind, bank, j = what[0], bank_of[place[0]], int(place[1])
                    if place[0] == "a":
                        pe.wait_ge(e_sum_done, i + j if follows else i)
                    elif place[0] == "c":
                        pe.wait_ge(exp_done, i + min(j + 2, G))
                    else:
                        pe.wait_ge(y_lo_done, i + min(j + 2, G))
                    if place == "b3":
                        read(g, "b2")
                    if place == "c3":
                        read(g, "c2")
                    if kind == "x":
                        turn_q(n_x + what[1], what[1] % 2, bank)
                    elif kind == "w":
                        turn_q(n_w + what[1], what[1] % 2, bank)
                    elif kind == "p":
                        product(b + 1, what[1], what[2], bank, n_x + what[1] + 1)
                    elif kind == "u":
                        turn_u(b + 1, what[1], bank)
                    else:
                        pe.wait_ge(mass_sum_done, b + 1)
                        for t in range(NT):
                            ins = nc.tensor.transpose(ps_t[0:E, t * P:(t + 1) * P], mass_sum[:, t, :], ident[:, :])
                        ins.then_inc(mass_turned, 1)

                for g in range(NG):
                    i, n = b * E + g * G, b * NG + g + 1
                    more = follows or g < NG - 1
                    par, nxt = (after, 0) if g == NG - 1 else (this, g + 1)
                    slots(i)
                    if more:
                        if g > 0:
                            read(g - 1, "c3")
                        if g == NG - 1:
                            pe.wait_ge(uT_lo_done, b * NT + 2 * NT)
                        pe.wait_ge(exp_done, i + G)
                        logits(i + G, 0, nxt, par)
                        if g > 0:
                            read(g - 1, "b3")
                        pe.wait_ge(y_lo_done, i + G)
                        project(i + G, 0, nxt, par)
                    for j in range(G):
                        combine(i, j, n)
                        if more and j + 1 < G:
                            pe.wait_ge(exp_done, i + G + j + 1)
                            if j >= 1:
                                read(g, f"c{j - 1}")
                            logits(i + G, j + 1, nxt, par)
                        if j + 1 < G:
                            aside(g, f"a{j}", i + G)
                        if more and j + 1 < G:
                            pe.wait_ge(y_lo_done, i + G + j + 1)
                            if j >= 1:
                                read(g, f"b{j - 1}")
                            project(i + G, j + 1, nxt, par)
                        if j + 1 < G:
                            aside(g, f"c{j}", i + G)
                        if j + 1 < G:
                            expand(i, j, first=(g == 0 and j == 0))
                        aside(g, f"b{j}", i + G)
                        if more:
                            if j >= 1:
                                pe.wait_ge(e_sum_done, i + G + j)
                            if j + 1 < G:
                                read(g, f"a{j}")
                            turn(i + G, j)
                        if j + 1 == G:
                            aside(g, f"c{j}", i + G)
                            expand(i, j)
                pe.wait_ge(mass_split, b * 2 + 2)
                for t in range(NT):
                    rows = slice(t * P, (t + 1) * P)
                    ins = three(acc[t][:, :], [(massT_hi[:, rows], massT_lo[:, rows], b2_hi[:, :], b2_lo[:, :])], start=False, check=False)
                ins.then_inc(sums_done, 1)

            pe.wait_ge(pool_const, 5)
            for n in range(2 * NT):
                if n >= 2:
                    pe.wait_ge(q_copied, n - 1)
                turn_q(n, n % 2, (ps_t, ps_y)[n % 2])
            pe.wait_ge(ones_done, 1)
            for k in range(KD):
                pe.wait_ge(mu_squared, k + 1)
                for e in range(E):
                    ins = nc.tensor.matmul(ps_l[:, e:e + 1], flat(eT[:, :, :])[:, e * S:(e + 1) * S], ones[:, 0:1], start=(k == 0 and e == 0),
                                           stop=(k == KD - 1), skip_group_check=True)
                ins.then_inc(mu_summed, 1)
            for e in range(E):
                pe.wait_ge(mu_diag, e + 1)
                nc.tensor.matmul(acc[e // G][:, e % G * S:(e % G + 1) * S], ones, diag[:, e % 2, :], start=True, stop=True).then_inc(mu_spread, 1)
            pe.wait_ge(dve_small, 6)
            pe.wait_ge(mu_scaled, KD)
            for t in range(0, NT, 2):
                for kb in range(KD):
                    for i in (t, t + 1):
                        at = nth_product(0, i, kb)
                        if at >= 4:
                            pe.wait_ge(prod_scaled, at - 3)
                        else:
                            pe.wait_ge(q_copied, 2 * NT)
                        if t and kb < 2:
                            pe.wait_ge(uT_lo_done, t)
                        product(0, i, kb, EARLY_BANKS[(2 * kb + i % 2) % 4], 2 * NT)
                for i in (t, t + 1):
                    pe.wait_ge(prod_scaled, nth_product(0, t + 1, KD - 1) + 1)
                    turn_u(0, i, (ps_t, ps_y)[i % 2])
            pe.sem_inc(f_done, 2)
            pe.wait_ge(uT_lo_done, NT)
            pe.wait_ge(mu_lo_done, KD)
            pe.wait_ge(w1_lo_done, KD)
            for j in range(G):
                if j >= 1:
                    pe.wait_ge(exp_done, j)
                logits(0, j, 0, 0)
                if j >= 1:
                    pe.wait_ge(y_lo_done, j)
                project(0, j, 0, 0)
                if j >= 1:
                    pe.wait_ge(e_sum_done, j)
                turn(0, j)
            pe.wait_ge(exp_done, G)
            pe.wait_ge(y_lo_done, G)
            for n in range(2 * NT, 3 * NT):
                if n >= 2 * NT + 2:
                    pe.wait_ge(q_copied, n - 1)
                turn_q(n, n % 2, (ps_l, ps_y)[n % 2])
            pe.wait_ge(q_copied, 3 * NT)
            with pe.Fori(0, B - 1) as b:
                batch(b, True)
            batch(B - 1, False)


_INS = ["x", "ctx_2048", "g_xattn", "g_ffn", "L0_ffn_gamma", "L0_ffn_beta", "L0_ffn_mu", "L0_ffn_scale",
        "L0_ffn_W1", "L0_ffn_b1", "L0_ffn_W2", "L0_ffn_b2"]


def kernel(**inputs):
    import numpy as _np
    import concourse.bacc as _bacc
    from concourse import mybir as _mybir
    from concourse.bass_utils import run_bass_kernel_spmd as _run

    nc = _bacc.Bacc("TRN2", target_bir_lowering=False, num_devices=1)
    arrays, args = {}, []
    for name in _INS:
        a = _np.ascontiguousarray(inputs[name])
        arrays[f"in_{name}_dram"] = a
        args.append(nc.dram_tensor(f"in_{name}_dram", a.shape, _mybir.dt.from_np(a.dtype), kind="ExternalInput").ap())
    args.append(nc.dram_tensor("out_dram", arrays["in_x_dram"].shape, _mybir.dt.float32, kind="ExternalOutput").ap())
    flamingo_block(nc, *args)
    r = _run(nc, [arrays], core_ids=[0])
    return r.results[0]["out_dram"]
```

```python
from contextlib import ExitStack

import concourse.bass as bass
from concourse import mybir

ALU = mybir.AluOpType
ACT = mybir.ActivationFunctionType
AX_X = mybir.AxisListType.X
F32 = mybir.dt.float32
F32R = mybir.dt.float32r
F16 = mybir.dt.float16
BF16 = mybir.dt.bfloat16
I32 = mybir.dt.int32

P = 128
FP8_MAX = 448.0
ACT_EPS, W_EPS = 1e-4, 1e-6
LN_EPS, L2_EPS = 1e-5, 1e-12
EXP_MASK = 0x7F800000
UNIT = 2.0 ** 13
LOGIT_ROOM = 60.0


def flamingo_block(nc, x, ctx_w, g_xattn, g_ffn, gamma, beta, mu, scale, w1, b1, w2, b2, out):
    B, N, D = x.shape
    _, E, S = mu.shape
    H = w1.shape[2]
    KD = D // P
    NT = N // P
    G = 4
    NG = E // G
    W = G * S
    assert S == P and H == P and N == 512 and D == 512 and W == 512 and NG == 4 and NT == 4 and KD == 4

    x_rows = x.rearrange("b n d -> (b n) d")
    ctx_rows = ctx_w.rearrange("b n d -> (b n) d")
    out_rows = out.rearrange("b n d -> (b n) d")
    mu_dram = mu.rearrange("(k p) e s -> p k (e s)", p=P)
    w1_dram = w1.rearrange("e (k p) h -> p k e h", p=P)
    w2_dram = w2.rearrange("e h d -> h e d")
    b1_flat = b1.rearrange("e h -> (e h)")

    with ExitStack() as es:
        def sb(name, shape, dt=F32):
            return es.enter_context(nc.sbuf_tensor(name, shape, dt))

        def sem(name):
            return es.enter_context(nc.semaphore(name))

        acc = [es.enter_context(nc.psum_tensor(f"acc{t}", [P, D], F32)) for t in range(NT)]
        ps_l = es.enter_context(nc.psum_tensor("ps_l", [P, N], F32))
        ps_zh = es.enter_context(nc.psum_tensor("ps_zh", [P, N], F32))
        ps_t = es.enter_context(nc.psum_tensor("ps_t", [P, N], F32))
        ps_y = es.enter_context(nc.psum_tensor("ps_y", [P, N], F32))

        ident = sb("ident", [P, P])
        ident16 = sb("ident16", [P, P], BF16)
        gx = sb("gx", [P, 1])
        gf = sb("gf", [P, 1])
        sc_in = sb("sc_in", [P, 1])
        tgx = sb("tgx", [P, 1])
        tgf = sb("tgf", [P, 1])
        half = sb("half", [P, 1])
        mhalf = sb("mhalf", [P, E])
        logit_scale = sb("logit_scale", [P, 1])
        shift = sb("shift", [P, 1])
        gam = sb("gam", [P, D])
        bet = sb("bet", [P, D])
        b1_bc = sb("b1_bc", [P, W])
        b2_hi = sb("b2_hi", [E, D], F32R)
        b2_lo = sb("b2_lo", [E, D], F32R)
        mu_hi = sb("mu_hi", [P, KD, E * S], F16)
        mu_lo = sb("mu_lo", [P, KD, E * S], F16)
        mu_norm = sb("mu_norm", [P, 2, E])
        w1_hi = sb("w1_hi", [P, KD, E * H], F16)
        w1_lo = sb("w1_lo", [P, KD, E * H], F16)
        w1_max = sb("w1_max", [P, KD])
        w1_unit = sb("w1_unit", [P, 5])
        w2_raw = sb("w2_raw", [P, D])
        w2_hi = sb("w2_hi", [P, 2, D], F32R)
        w2_lo = sb("w2_lo", [P, 2, D], F32R)

        work = sb("work", [P, 2, 2, D])
        q16 = sb("q16", [P, 2, D], BF16)
        qT = sb("qT", [P, NT, KD, P], BF16)
        wT = sb("wT", [P, KD, N], BF16)
        x1 = sb("x1", [P, NT, D])
        stat = sb("stat", [P, 2, 8])
        norm = sb("norm", [P, 2, 6])
        amax = sb("amax", [P, 2, 4])
        amax_all = sb("amax_all", [P, 2, 4])
        quant = sb("quant", [P, 2, 4])
        x_dequant = sb("x_dequant", [P, NT, 4])
        w_dequant = sb("w_dequant", [P, KD, NT])
        dequant = sb("dequant", [P, 2, KD, NT])
        uT_hi = sb("uT_hi", [P, 2 * KD * N], F16)
        uT_lo = sb("uT_lo", [P, 2 * KD * N], F16)
        y_scale = sb("y_scale", [P, 2 * NT])

        eT = sb("eT", [P, G, N])
        den = sb("den", [P, G])
        rden = sb("rden", [P, G])
        hn = sb("hn", [P, G, H])
        mass = sb("mass", [P, 2 * NT, E])
        mass_sum = sb("mass_sum", [P, NT, E])
        z_row = sb("z_row", [P, NT])
        z_inv = sb("z_inv", [P, NT])
        with nc.sbuf_tensor("prod", [P, 2, D], F32) as prod:
            pass
        massT_hi = sb("massT_hi", [E, N], F32R)
        massT_lo = sb("massT_lo", [E, N], F32R)
        b2_raw, diag, ones = prod[0:E, 0, :], eT[:, 0, 0:2 * P].rearrange("p (a c) -> p a c", c=P), hn[:, 0, :]

        with nc.sbuf_tensor("mu_raw", [P, KD, E * S], F32) as mu_raw, nc.sbuf_tensor("w1_raw", [P, KD, E * H], F32) as w1_raw:
            pass
        e_hi = sb("e_hi", [P, G, NT, S], F32R)
        e_lo = sb("e_lo", [P, G, NT, S], F32R)
        y_hi = sb("y_hi", [P, NT, W], F32R)
        y_lo = sb("y_lo", [P, NT, W], F32R)
        eT_hi = sb("eT_hi", [P, G, N], F32R)
        eT_lo = sb("eT_lo", [P, G, N], F32R)
        h_hi = sb("h_hi", [P, G, H], F32R)
        h_lo = sb("h_lo", [P, G, H], F32R)
        z_hi = sb("z_hi", [P, N], F32R)
        z_lo = sb("z_lo", [P, N], F32R)
        last = sb("last", [P, NT, D])

        x1_dram = nc.dram_tensor("x1_dram", [B * N, D], F32, kind="Internal").ap()

        consts_in, b2_in, b1_in = sem("consts_in"), sem("b2_in"), sem("b1_in")
        mu_in = [sem(f"mu_in{i}") for i in range(KD)]
        w1_in = [sem(f"w1_in{i}") for i in range(KD)]
        w2_in = sem("w2_in")
        x_in = [sem(f"x_in{t}") for t in range(NT)]
        ctx_in = [sem(f"ctx_in{i}") for i in range(2)]
        x1_stored = [sem(f"x1_stored{t}") for t in range(NT)]
        last_in = [sem(f"last_in{t}") for t in range(NT)]
        out_written = [sem(f"out_written{t}") for t in range(NT)]
        pool_const, ones_done = sem("pool_const"), sem("ones_done")
        tanh_done, dve_small, dve_w1 = sem("tanh_done"), sem("dve_small"), sem("dve_w1")
        mu_squared, mu_summed, mu_clamped, mu_rooted = sem("mu_squared"), sem("mu_summed"), sem("mu_clamped"), sem("mu_rooted")
        mu_diag, mu_spread, mu_scaled, mu_hi_done, mu_lo_done = sem("mu_diag"), sem("mu_spread"), sem("mu_scaled"), sem("mu_hi_done"), sem("mu_lo_done")
        w1_all_max, w1_hi_done, w1_lo_done = sem("w1_all_max"), sem("w1_hi_done"), sem("w1_lo_done")
        w_amax_done, w_amax_all = sem("w_amax_done"), sem("w_amax_all")
        x_var_done, x_rstd_done = sem("x_var_done"), sem("x_rstd_done")
        q_scale_done, q_scaled, q_step_done = sem("q_scale_done"), sem("q_scaled"), sem("q_step_done")
        q_done, q_turned, q_copied = sem("q_done"), sem("q_turned"), sem("q_copied")
        prod_done, prod_scaled, prod_added = sem("prod_done"), sem("prod_scaled"), sem("prod_added")
        var1_done, rstd1_done, var2_done, rstd2_done = sem("var1_done"), sem("rstd1_done"), sem("var2_done"), sem("rstd2_done")
        ln_done, affine_done, squares_done, l2_done = sem("ln_done"), sem("affine_done"), sem("squares_done"), sem("l2_done")
        rl2_done, unit_done, unit_turned, uT_hi_done, uT_lo_done = (sem("rl2_done"), sem("unit_done"), sem("unit_turned"),
                                                                    sem("uT_hi_done"), sem("uT_lo_done"))
        dve_early, dve_link, pool_early, pool_link = sem("dve_early"), sem("dve_link"), sem("pool_early"), sem("pool_link")
        w2_half, w2_split, held = sem("w2_half"), sem("w2_split"), sem("held")
        l_done, y_done, h_done, z_done, t_done, f_done = (sem("l_done"), sem("y_done"), sem("h_done"), sem("z_done"),
                                                          sem("t_done"), sem("f_done"))
        exp_done, gelu_done, y_hi_done, z_hi_done, e_hi_done = (sem("exp_done"), sem("gelu_done"), sem("y_hi_done"),
                                                                sem("z_hi_done"), sem("e_hi_done"))
        rden_done, hn_done, hb_done, h_hi_done, h_lo_done = (sem("rden_done"), sem("hn_done"), sem("hb_done"),
                                                             sem("h_hi_done"), sem("h_lo_done"))
        y_lo_done, z_lo_done, eT_hi_done, eT_lo_done = sem("y_lo_done"), sem("z_lo_done"), sem("eT_hi_done"), sem("eT_lo_done")
        e_lo_done, e_sum_done = sem("e_lo_done"), sem("e_sum_done")
        mass_sum_done, mass_turned, mass_split, zr_done = (sem("mass_sum_done"), sem("mass_turned"), sem("mass_split"),
                                                            sem("zr_done"))
        sums_done, out_ready = sem("sums_done"), sem("out_ready")

        W1_LINKS, DVE_LINKS, POOL_LINKS = KD + 5, 72, 12
        EARLY_BANKS = (ps_y, ps_l, ps_zh, ps_t)
        FIRST_Q = 3 * NT

        class Chain:

            def __init__(self, engine, semaphore, start=0):
                self.engine, self.semaphore, self.start, self.count = engine, semaphore, start, 0

            def then(self, instruction):
                self.count += 1
                instruction.then_inc(self.semaphore, 1)
                self.engine.wait_ge(self.semaphore, self.start + self.count)

        def hold(engine):
            engine.sem_inc(held, 1)

        def by_block(ap):
            return ap.rearrange("p (k c) -> p k c", c=P)

        def spread(ap, n=P):
            return ap.rearrange("p (k a) -> p k a", a=1).to_broadcast([P, 4, n])

        def flat(ap):
            return ap.rearrange("p a b -> p (a b)")

        def nth(b, t):
            return b * NT + t

        def nth_product(b, t, kb):
            return b * (NT * KD) + ((t // 2) * 2 * KD + 2 * kb + t % 2)

        def banks16(bank):
            return bank[:, 0:D // 2].bitcast(BF16)

        def u_view(u, par, t):
            return u[:, :].rearrange("p (a k n) -> p a k n", a=2, k=KD)[:, bass.ds(par, 1), :, t * P:(t + 1) * P].rearrange(
                "p a k n -> p (a k) n")

        block = es.enter_context(nc.Block())

        @block.sync
        def _(sp):
            def load_ctx(b, t, n, later):
                if later:
                    sp.wait_ge(q_done, n - 1)
                sp.dma_start(work[:, t % 2, 0, :], ctx_rows[bass.ds((b % B) * N + t * P, P), :]).then_inc(ctx_in[t % 2], 16)

            def load_x(b, t):
                sp.dma_start(x1[:, t, :], x_rows[bass.ds((b % B) * N + t * P, P), :]).then_inc(x_in[t], 16)

            def store_x1(b, t):
                sp.wait_ge(prod_added, nth_product(b, t, KD - 1) + 1)
                sp.dma_start(x1_dram[bass.ds(b * N + t * P, P), :], x1[:, t, :]).then_inc(x1_stored[t], 16)

            def load_b1(n, g):
                if n is not None:
                    sp.wait_ge(hb_done, n)
                sp.dma_start(b1_bc[:, :], b1_flat[bass.ds(g * W, W)].partition_broadcast(P)).then_inc(b1_in, 16)

            def outputs(b):
                for t in range(NT):
                    sp.wait_ge(out_written[t], (b + 1) * 16)
                    hold(sp)
                    sp.wait_ge(x1_stored[t], b * 16 + 16)
                    sp.dma_start(last[:, t, :], x1_dram[bass.ds(b * N + t * P, P), :]).then_inc(last_in[t], 16)
                for t in range(NT):
                    sp.wait_ge(out_ready, nth(b, t) + 1)
                    sp.dma_start(out_rows[bass.ds(b * N + t * P, P), :], last[:, t, :]).then_inc(out_written[t], 16)

            for t in range(NT):
                sp.sem_inc(out_written[t], 16)
            for t in range(2):
                load_ctx(0, t, t, False)
            for dst, src in ((gx, g_xattn), (gf, g_ffn), (sc_in, scale), (gam, gamma), (bet, beta)):
                sp.dma_start(dst[:, :], src.partition_broadcast(P)).then_inc(consts_in, 16)
            for t in range(NT):
                load_x(0, t)
            sp.dma_start(mu_raw[:, 0, :], mu_dram[:, 0]).then_inc(mu_in[0], 16)
            for t in range(2, NT):
                load_ctx(0, t, t, True)
            for k in range(1, KD):
                sp.dma_start(mu_raw[:, k, :], mu_dram[:, k]).then_inc(mu_in[k], 16)
            for k in range(KD):
                sp.dma_start(w1_raw[:, k, :].rearrange("p (c h) -> p c h", h=H), w1_dram[:, k]).then_inc(w1_in[k], 16)
            sp.dma_start(b2_raw, b2).then_inc(b2_in, 16)
            load_b1(None, 0)
            for t in range(NT):
                store_x1(0, t)
            sp.wait_ge(unit_turned, NT)
            for t in range(NT):
                load_ctx(1, t, 2 * NT + t, True)
                sp.wait_ge(x1_stored[t], 16)
                load_x(1, t)
            with sp.Fori(0, B - 1) as b:
                load_b1(b * NG + 1, 1)
                load_b1(b * NG + 2, 2)
                store_x1(b + 1, 0)
                store_x1(b + 1, 1)
                load_b1(b * NG + 3, 3)
                store_x1(b + 1, 2)
                store_x1(b + 1, 3)
                sp.wait_ge(unit_turned, nth(b + 1, NT - 1) + 1)
                n = b * (2 * NT) + (FIRST_Q + NT)
                load_ctx(b + 2, 0, n, True)
                load_ctx(b + 2, 1, n + 1, True)
                for t in range(NT):
                    sp.wait_ge(x1_stored[t], b * 16 + 32)
                    load_x(b + 2, t)
                load_b1(b * NG + 4, 0)
                load_ctx(b + 2, 2, n + 2, True)
                load_ctx(b + 2, 3, n + 3, True)
                outputs(b)
            for g in range(1, NG):
                load_b1((B - 1) * NG + g, g)
            outputs(B - 1)
            for t in range(NT):
                sp.wait_ge(out_written[t], 16 * B + 16)

        @block.gpsimd
        def _(pool):
            def reduce_weights(b, t):
                w = t % 2
                pool.wait_ge(w_amax_done, nth(b, t) + 1)
                hold(pool)
                nc.gpsimd.partition_all_reduce(amax_all[:, w, :], amax[:, w, :], P, bass.bass_isa.ReduceOp.max).then_inc(w_amax_all, 1)

            def root(b, t, col_in, waits, col_out, exponent, done):
                w = t % 2
                pool.wait_ge(waits, nth(b, t) + 1)
                src = stat[:, w, 7:8] if col_in is None else norm[:, w, col_in:col_in + 1]
                nc.gpsimd.tensor_tensor(norm[:, w, col_out:col_out + 1], src, exponent, ALU.pow).then_inc(done, 1)

            def x_rstd(b, t):
                root(b, t, None, x_var_done, 0, mhalf[:, 0:1], x_rstd_done)

            def rstd1(b, t):
                root(b, t, None, var1_done, 1, mhalf[:, 0:1], rstd1_done)

            def rstd2(b, t):
                root(b, t, None, var2_done, 2, mhalf[:, 0:1], rstd2_done)

            def l2(b, t):
                root(b, t, 3, squares_done, 4, half[:, :], l2_done)

            def round_(n, w, link, first=False):
                a, m = work[:, w, 0, :], work[:, w, 1, :]
                pool.wait_ge(q_step_done, n + 1)
                link.then(nc.gpsimd.tensor_tensor(a, a, m, ALU.add))
                if not first:
                    pool.wait_ge(q_turned, n - 1)
                nc.gpsimd.tensor_tensor(q16[:, w, :], a, m, ALU.subtract).then_inc(q_done, 1)

            def add(b, t, kb):
                pool.wait_ge(prod_scaled, nth_product(b, t, kb) + 1)
                nc.gpsimd.tensor_tensor(x1[:, t, :], x1[:, t, :], prod[:, t % 2, :], ALU.add).then_inc(prod_added, 1)

            def affine(b, t, link):
                y = work[:, t % 2, 0, :]
                pool.wait_ge(ln_done, nth(b, t) + 1)
                link.then(nc.gpsimd.tensor_tensor(y, y, gam[:, :], ALU.mult))
                nc.gpsimd.tensor_tensor(y, y, bet[:, :], ALU.add).then_inc(affine_done, 1)

            def load_w2(b, e):
                hold(pool)
                pool.dma_start(w2_raw[:, :], w2_dram[:, e, :]).then_inc(w2_in, 16)

            def split_w2(b, e):
                i, s = b * E + e, e % 2
                pool.wait_ge(w2_in, i * 16 + 16)
                pool.wait_ge(f_done, i + 1)
                hold(pool)
                nc.gpsimd.tensor_scalar(w2_hi[:, s, :], w2_raw[:, :], 1.0, 1.0, ALU.mult, ALU.mult).then_inc(w2_half, 1)
                pool.wait_ge(w2_half, i + 1)
                nc.gpsimd.tensor_tensor(w2_lo[:, s, :], w2_raw[:, :], w2_hi[:, s, :].bitcast(F32), ALU.subtract).then_inc(w2_split, 1)
                pool.wait_ge(w2_split, i + 1)
                load_w2(b, (e + 1) % E)

            c = Chain(pool, pool_const)
            c.then(nc.gpsimd.memset(mhalf[:, :], -0.5))
            c.then(nc.gpsimd.memset(half[:, :], 0.5))
            c.then(nc.gpsimd.memset(ident[:, :], 0.0))
            c.then(nc.gpsimd.affine_select(out=ident[:, :], in_=ident[:, :], compare_op=ALU.not_equal, fill=1.0,
                                           base=0, pattern=[[-1, P]], channel_multiplier=1))
            c.then(nc.gpsimd.tensor_copy(ident16[:, :], ident[:, :]))
            nc.gpsimd.memset(ones, 1.0).then_inc(ones_done, 1)
            load_w2(0, 0)
            link = Chain(pool, pool_early)
            for t in range(0, NT, 2):
                for i in (t, t + 1):
                    reduce_weights(0, i)
                for i in (t, t + 1):
                    round_(i, i % 2, link, first=(i < 2))
            for t in range(0, NT, 2):
                for i in (t, t + 1):
                    x_rstd(0, i)
                for i in (t, t + 1):
                    round_(NT + i, i % 2, link)
            pool.wait_ge(dve_w1, KD + 1)
            nc.gpsimd.partition_all_reduce(w1_unit[:, 1:2], w1_unit[:, 0:1], P, bass.bass_isa.ReduceOp.max).then_inc(w1_all_max, 1)
            for kb in (0, 1):
                for i in (0, 1):
                    add(0, i, kb)
            pool.wait_ge(mu_clamped, 1)
            nc.gpsimd.tensor_tensor(mu_norm[:, 1, :], mu_norm[:, 0, :], mhalf[:, :], ALU.pow).then_inc(mu_rooted, 1)
            for kb in (2, 3):
                for i in (0, 1):
                    add(0, i, kb)

            def both(stage, t):
                stage(0, t)
                stage(0, t + 1)

            def low_mu(k):
                pool.wait_ge(mu_hi_done, k + 1)
                nc.gpsimd.tensor_tensor(mu_lo[:, k, :], mu_raw[:, k, :], mu_hi[:, k, :], ALU.subtract).then_inc(mu_lo_done, 1)

            both(rstd1, 0)
            both(lambda b, i: add(b, i, 0), 2)
            both(lambda b, i: add(b, i, 1), 2)
            both(rstd2, 0)
            both(lambda b, i: add(b, i, 2), 2)
            both(lambda b, i: affine(b, i, link), 0)
            both(lambda b, i: add(b, i, 3), 2)
            both(rstd1, 2)
            both(l2, 0)
            low_mu(0)
            both(rstd2, 2)
            low_mu(1)
            both(lambda b, i: affine(b, i, link), 2)
            low_mu(2)
            both(l2, 2)
            low_mu(3)
            for t in range(0, NT, 2):
                for i in (t, t + 1):
                    reduce_weights(1, i)
                for i in (t, t + 1):
                    round_(2 * NT + i, i % 2, link)

            def batch(b, aside):
                link = Chain(pool, pool_link, b * POOL_LINKS)
                n_x, n_w = b * (2 * NT) + FIRST_Q, b * (2 * NT) + (FIRST_Q + NT)
                if not aside:
                    for e in range(E):
                        split_w2(b, e)
                    return
                x_rstd(b + 1, 0)
                split_w2(b, 0)
                x_rstd(b + 1, 1)
                split_w2(b, 1)
                round_(n_x, 0, link)
                round_(n_x + 1, 1, link)
                split_w2(b, 2)
                x_rstd(b + 1, 2)
                x_rstd(b + 1, 3)
                split_w2(b, 3)
                add(b + 1, 0, 0)
                round_(n_x + 2, 0, link)
                add(b + 1, 1, 0)
                round_(n_x + 3, 1, link)
                add(b + 1, 0, 1)
                add(b + 1, 1, 1)
                split_w2(b, 4)
                split_w2(b, 5)
                add(b + 1, 0, 2)
                add(b + 1, 1, 2)
                split_w2(b, 6)
                add(b + 1, 0, 3)
                add(b + 1, 1, 3)
                rstd1(b + 1, 0)
                add(b + 1, 2, 0)
                rstd1(b + 1, 1)
                split_w2(b, 7)
                add(b + 1, 3, 0)
                rstd2(b + 1, 0)
                add(b + 1, 2, 1)
                add(b + 1, 3, 1)
                rstd2(b + 1, 1)
                add(b + 1, 2, 2)
                affine(b + 1, 0, link)
                add(b + 1, 3, 2)
                add(b + 1, 2, 3)
                affine(b + 1, 1, link)
                add(b + 1, 3, 3)
                rstd1(b + 1, 2)
                l2(b + 1, 0)
                rstd1(b + 1, 3)
                split_w2(b, 8)
                l2(b + 1, 1)
                split_w2(b, 9)
                rstd2(b + 1, 2)
                split_w2(b, 10)
                rstd2(b + 1, 3)
                affine(b + 1, 2, link)
                affine(b + 1, 3, link)
                l2(b + 1, 2)
                l2(b + 1, 3)
                split_w2(b, 11)
                reduce_weights(b + 2, 0)
                reduce_weights(b + 2, 1)
                split_w2(b, 12)
                split_w2(b, 13)
                round_(n_w, 0, link)
                round_(n_w + 1, 1, link)
                reduce_weights(b + 2, 2)
                reduce_weights(b + 2, 3)
                split_w2(b, 14)
                round_(n_w + 2, 0, link)
                round_(n_w + 3, 1, link)
                split_w2(b, 15)
                assert link.count == POOL_LINKS, link.count

            with pool.Fori(0, B - 1) as b:
                batch(b, True)
            batch(B - 1, False)

        @block.scalar
        def _(act):
            def scale_blocks(n, w):
                act.wait_ge(q_scale_done, n + 1)
                a = work[:, w, 0, :]
                for kb in range(KD):
                    cols = slice(kb * P, (kb + 1) * P)
                    ins = nc.scalar.activation(a[:, cols], a[:, cols], ACT.Copy, scale=quant[:, w, kb:kb + 1])
                ins.then_inc(q_scaled, 1)

            def keep_w(n, t, bank):
                act.wait_ge(q_turned, n + 1)
                nc.scalar.activation(wT[:, :, t * P:(t + 1) * P], by_block(banks16(bank)), ACT.Copy).then_inc(q_copied, 1)

            def keep_x(n, t, bank):
                act.wait_ge(q_turned, n + 1)
                nc.scalar.activation(qT[:, t, :, :], by_block(banks16(bank)), ACT.Copy).then_inc(q_copied, 1)

            def squares(b, t):
                act.wait_ge(affine_done, nth(b, t) + 1)
                w = t % 2
                nc.scalar.activation(work[:, w, 1, :], work[:, w, 0, :], ACT.Square, accum_out=norm[:, w, 3:4]).then_inc(squares_done, 1)

            def unit(b, t):
                act.wait_ge(rl2_done, nth(b, t) + 1)
                w = t % 2
                nc.scalar.activation(work[:, w, 0, :], work[:, w, 0, :], ACT.Copy, scale=norm[:, w, 5:6]).then_inc(unit_done, 1)

            def keep_u(b, t, par, bank):
                act.wait_ge(unit_turned, nth(b, t) + 1)
                hold(act)
                nc.scalar.activation(u_view(uT_hi, par, t), by_block(bank[:, :]), ACT.Copy).then_inc(uT_hi_done, 1)

            def exp(i, j, reused):
                act.wait_ge(l_done, i + j + 1)
                if reused:
                    act.wait_ge(t_done, i + j - 3)
                    act.wait_ge(eT_lo_done, i + j - 3)
                nc.scalar.activation(eT[:, j, :], ps_l[:, :], ACT.Exp, bias=shift[:, :], scale=logit_scale[:, :],
                                     accum_out=den[:, j:j + 1]).then_inc(exp_done, 1)

            def split_y(i, j, par):
                act.wait_ge(y_done, i + j + 1)
                hold(act)
                nc.scalar.activation(y_hi[:, j, :], ps_y[:, :], ACT.Copy, scale=y_scale[:, bass.ds(par * NT + j, 1)]).then_inc(y_hi_done, 1)

            def split_e(i, j):
                act.wait_ge(t_done, i + j + 1)
                nc.scalar.activation(e_hi[:, j, :, :], ps_t[:, :].rearrange("p (t s) -> p t s", s=S), ACT.Copy).then_inc(e_hi_done, 1)

            def split_z(i, j):
                act.wait_ge(z_done, i + j + 1)
                nc.scalar.activation(z_hi[:, :], ps_zh[:, :], ACT.Copy).then_inc(z_hi_done, 1)

            def group(b, g, follows, par, aside):
                i = b * E + g * G
                aside(g, "s")
                act.wait_ge(hb_done, b * NG + g + 1)
                nc.scalar.activation(hn[:, :, :], hn[:, :, :], ACT.Gelu).then_inc(gelu_done, 1)
                aside(g, "h")
                for j in range(G):
                    if follows and j == 0:
                        exp(i + G, 0, True)
                        split_y(i + G, 0, par)
                        aside(g, "y-")
                    split_z(i, j)
                    if follows and j + 1 < G:
                        exp(i + G, j + 1, True)
                    aside(g, f"z{j}")
                    if follows and j + 1 < G:
                        split_y(i + G, j + 1, par)
                    aside(g, f"y{j}")
                    if follows:
                        split_e(i + G, j)
                    aside(g, f"e{j}")

            def batch(b, follows):
                n_x, n_w = b * (2 * NT) + FIRST_Q, b * (2 * NT) + (FIRST_Q + NT)
                this, after = b % 2, (b + 1) % 2

                def aside(g, at):
                    if not follows:
                        return
                    at = (g, at)
                    if at == (0, "z0"):
                        scale_blocks(n_x, 0)
                    elif at == (0, "y0"):
                        scale_blocks(n_x + 1, 1)
                    elif at == (0, "y1"):
                        keep_x(n_x, 0, ps_l)
                    elif at == (0, "e1"):
                        keep_x(n_x + 1, 1, ps_y)
                        scale_blocks(n_x + 2, 0)
                    elif at == (0, "z2"):
                        scale_blocks(n_x + 3, 1)
                    elif at == (1, "s"):
                        keep_x(n_x + 2, 2, ps_y)
                    elif at == (1, "h"):
                        keep_x(n_x + 3, 3, ps_t)
                    elif at == (2, "h"):
                        squares(b + 1, 0)
                    elif at == (2, "y-"):
                        squares(b + 1, 1)
                    elif at == (2, "z0"):
                        unit(b + 1, 0)
                        unit(b + 1, 1)
                    elif at == (2, "y0"):
                        keep_u(b + 1, 0, after, ps_l)
                    elif at == (2, "e0"):
                        keep_u(b + 1, 1, after, ps_y)
                    elif at == (2, "y1"):
                        squares(b + 1, 2)
                    elif at == (2, "e1"):
                        squares(b + 1, 3)
                    elif at == (2, "z2"):
                        unit(b + 1, 2)
                        unit(b + 1, 3)
                    elif at == (2, "y2"):
                        keep_u(b + 1, 2, after, ps_l)
                    elif at == (2, "e2"):
                        keep_u(b + 1, 3, after, ps_y)
                    elif at == (3, "z0"):
                        scale_blocks(n_w, 0)
                        scale_blocks(n_w + 1, 1)
                    elif at == (3, "y1"):
                        keep_w(n_w, 0, ps_l)
                        scale_blocks(n_w + 2, 0)
                        scale_blocks(n_w + 3, 1)
                    elif at == (3, "e1"):
                        keep_w(n_w + 1, 1, ps_y)
                    elif at == (3, "e2"):
                        keep_w(n_w + 2, 2, ps_y)
                    elif at == (3, "e3"):
                        keep_w(n_w + 3, 3, ps_l)

                for g in range(NG):
                    group(b, g, follows or g < NG - 1, after if g == NG - 1 else this, aside)

            act.wait_ge(consts_in, 16 * 5)
            nc.scalar.activation(tgx[:, :], gx[:, :], ACT.Tanh).then_inc(tanh_done, 1)
            nc.scalar.activation(tgf[:, :], gf[:, :], ACT.Tanh).then_inc(tanh_done, 1)
            for k in range(KD):
                n = 2 * k
                keep = keep_w if n < NT else keep_x
                scale_blocks(n, 0)
                scale_blocks(n + 1, 1)
                keep(n, n % NT, ps_t)
                keep(n + 1, n % NT + 1, ps_y)
                act.wait_ge(mu_in[k], 16)
                if k >= 1:
                    act.wait_ge(mu_summed, k)
                nc.scalar.activation(flat(eT[:, :, :]), mu_raw[:, k, :], ACT.Square).then_inc(mu_squared, 1)

            def high_w1(k):
                act.wait_ge(w1_in[k], 16)
                if k == 0:
                    act.wait_ge(dve_w1, W1_LINKS)
                nc.scalar.activation(w1_hi[:, k, :], w1_raw[:, k, :], ACT.Copy, scale=w1_unit[:, 3:4]).then_inc(w1_hi_done, 1)

            def high_mu(k):
                act.wait_ge(mu_scaled, k + 1)
                nc.scalar.activation(mu_hi[:, k, :], mu_raw[:, k, :], ACT.Copy).then_inc(mu_hi_done, 1)

            def both(stage, t):
                stage(0, t)
                stage(0, t + 1)

            high_w1(0)
            high_w1(1)
            high_mu(0)
            high_w1(2)
            high_mu(1)
            both(squares, 0)
            high_mu(2)
            both(unit, 0)
            high_w1(3)
            keep_u(0, 0, 0, ps_t)
            keep_u(0, 1, 0, ps_y)
            high_mu(3)
            both(squares, 2)
            both(unit, 2)
            keep_u(0, 2, 0, ps_l)
            keep_u(0, 3, 0, ps_zh)
            for j in range(G):
                exp(0, j, False)
                split_y(0, j, 0)
                if j % 2 == 1:
                    scale_blocks(2 * NT + j - 1, 0)
                    scale_blocks(2 * NT + j, 1)
                if j == 2:
                    keep_w(2 * NT, 0, acc[0])
                    keep_w(2 * NT + 1, 1, acc[1])
                split_e(0, j)
            keep_w(2 * NT + 2, 2, acc[2])
            keep_w(2 * NT + 3, 3, acc[3])
            with act.Fori(0, B - 1) as b:
                batch(b, True)
            batch(B - 1, False)

        @block.vector
        def _(dve):
            def statistics(src, w, link, done):
                link.then(nc.vector.bn_stats(stat[:, w, 0:6], src))
                hold(dve)
                link.then(nc.vector.bn_aggr(stat[:, w, 6:8], stat[:, w, 0:6]))
                nc.vector.tensor_scalar(stat[:, w, 7:8], stat[:, w, 7:8], LN_EPS, None, ALU.add).then_inc(done, 1)

            def standardise(dst, src, w, col, waits, n):
                dve.wait_ge(waits, n + 1)
                return nc.vector.tensor_scalar(dst, src, stat[:, w, 6:7], norm[:, w, col:col + 1], ALU.subtract, ALU.mult)

            def w_amax(b, t):
                dve.wait_ge(ctx_in[t % 2], b * 32 + (t // 2) * 16 + 16)
                nc.vector.tensor_reduce(amax[:, t % 2, :], by_block(work[:, t % 2, 0, :]), AX_X, ALU.max,
                                        apply_absolute_value=True).then_inc(w_amax_done, 1)

            def w_scale(b, t, n, link):
                w = t % 2
                dve.wait_ge(w_amax_all, nth(b, t) + 1)
                link.then(nc.vector.tensor_scalar(w_dequant[:, :, t], amax_all[:, w, :], W_EPS, 1.0 / FP8_MAX, ALU.max, ALU.mult))
                nc.vector.reciprocal(quant[:, w, :], w_dequant[:, :, t]).then_inc(q_scale_done, 1)

            def x_stats(b, t, link):
                dve.wait_ge(x_in[t], b * 16 + 16)
                statistics(x1[:, t, :], t % 2, link, x_var_done)

            def x_scale(b, t, n, link, first=False):
                w = t % 2
                a = work[:, w, 0, :]
                dve.wait_ge(q_done, n - 1)
                link.then(standardise(a, x1[:, t, :], w, 0, x_rstd_done, nth(b, t)))
                link.then(nc.vector.tensor_reduce(amax[:, w, :], by_block(a), AX_X, ALU.max, apply_absolute_value=True))
                link.then(nc.vector.tensor_scalar(x_dequant[:, t, :], amax[:, w, :], ACT_EPS, 1.0 / FP8_MAX, ALU.max, ALU.mult))
                link.then(nc.vector.reciprocal(quant[:, w, :], x_dequant[:, t, :]))
                nc.vector.tensor_scalar(x_dequant[:, t, :], x_dequant[:, t, :], tgx[:, :], None, ALU.mult).then_inc(q_scale_done, 1)

            def step(n, w, link):
                a, m = work[:, w, 0, :], work[:, w, 1, :]
                dve.wait_ge(q_scaled, n + 1)
                link.then(nc.vector.tensor_scalar(m.bitcast(I32), a.bitcast(I32), EXP_MASK, None, ALU.bitwise_and))
                nc.vector.tensor_scalar(m, m, 2.0 ** -6, 1.5 * 2.0 ** 20, ALU.max, ALU.mult).then_inc(q_step_done, 1)

            def dequants(t, link):
                link.then(nc.vector.tensor_tensor(dequant[:, t % 2, :, :], spread(x_dequant[:, t, :], NT), w_dequant[:, :, :], ALU.mult))

            def scale_product(b, t, kb, bank, first=False):
                n, w = nth_product(b, t, kb), t % 2
                dve.wait_ge(prod_done, n + 1)
                if not first:
                    dve.wait_ge(prod_added, n - 1)
                nc.vector.tensor_tensor(by_block(prod[:, w, :]), by_block(bank[:, :]), spread(dequant[:, w, kb, :]), ALU.mult).then_inc(prod_scaled, 1)

            def stats1(b, t, link):
                dve.wait_ge(prod_added, nth_product(b, t, KD - 1) + 1)
                statistics(x1[:, t, :], t % 2, link, var1_done)

            def stats2(b, t, link):
                y = work[:, t % 2, 0, :]
                if t >= 2:
                    dve.wait_ge(unit_turned, nth(b, t) - 1)
                link.then(standardise(y, x1[:, t, :], t % 2, 1, rstd1_done, nth(b, t)))
                statistics(y, t % 2, link, var2_done)

            def layernorm(b, t):
                y = work[:, t % 2, 0, :]
                standardise(y, y, t % 2, 2, rstd2_done, nth(b, t)).then_inc(ln_done, 1)

            def rl2(b, t, par, link):
                w = t % 2
                dve.wait_ge(l2_done, nth(b, t) + 1)
                link.then(nc.vector.tensor_scalar(norm[:, w, 4:5], norm[:, w, 4:5], L2_EPS, None, ALU.max))
                link.then(nc.vector.tensor_scalar(y_scale[:, bass.ds(par * NT + t, 1)], norm[:, w, 4:5], w1_unit[:, 4:5], None, ALU.mult))
                link.then(nc.vector.reciprocal(norm[:, w, 5:6], norm[:, w, 4:5]))
                nc.vector.tensor_scalar(norm[:, w, 5:6], norm[:, w, 5:6], UNIT, None, ALU.mult).then_inc(rl2_done, 1)

            def split_u(b, t, par, bank):
                dve.wait_ge(uT_hi_done, nth(b, t) + 1)
                nc.vector.tensor_tensor(u_view(uT_lo, par, t), by_block(bank[:, :]), u_view(uT_hi, par, t), ALU.subtract).then_inc(uT_lo_done, 1)

            def split_y(i, j, par):
                dve.wait_ge(y_hi_done, i + j + 1)
                nc.vector.scalar_tensor_tensor(y_lo[:, j, :], ps_y[:, :], y_scale[:, bass.ds(par * NT + j, 1)], y_hi[:, j, :].bitcast(F32),
                                               ALU.mult, ALU.subtract).then_inc(y_lo_done, 1)

            def split_z(i, j):
                dve.wait_ge(z_hi_done, i + j + 1)
                nc.vector.tensor_tensor(z_lo[:, :], ps_zh[:, :], z_hi[:, :].bitcast(F32), ALU.subtract).then_inc(z_lo_done, 1)

            def split_eT(i, j, reused):
                dve.wait_ge(exp_done, i + j + 1)
                if reused:
                    dve.wait_ge(z_done, i + j - 3)
                nc.vector.tensor_copy(eT_hi[:, j, :], eT[:, j, :]).then_inc(eT_hi_done, 1)
                dve.wait_ge(eT_hi_done, i + j + 1)
                nc.vector.tensor_tensor(eT_lo[:, j, :], eT[:, j, :], eT_hi[:, j, :].bitcast(F32), ALU.subtract).then_inc(eT_lo_done, 1)

            def split_e(i, e, j, par):
                dve.wait_ge(e_hi_done, i + j + 1)
                nc.vector.tensor_tensor(e_lo[:, j, :, :].rearrange("p t s -> p (t s)"), ps_t[:, :],
                                        e_hi[:, j, :, :].rearrange("p t s -> p (t s)").bitcast(F32), ALU.subtract).then_inc(e_lo_done, 1)
                nc.vector.tensor_reduce(mass[:, bass.ds(par * NT, NT), e + j], ps_t[:, :].rearrange("p (t s) -> p t s", s=S), AX_X,
                                        ALU.add).then_inc(e_sum_done, 1)

            def group(b, g, follows, par, aside):
                i, n = b * E + g * G, b * NG + g + 1
                aside(g, "s")
                dve.wait_ge(exp_done, i + G)
                nc.vector.reciprocal(rden[:, :], den[:, :]).then_inc(rden_done, 1)
                dve.wait_ge(rden_done, n)
                dve.wait_ge(h_done, n)
                nc.vector.tensor_tensor(hn[:, :, :], by_block(ps_zh[:, :]), spread(rden[:, :]), ALU.mult).then_inc(hn_done, 1)
                dve.wait_ge(hn_done, n)
                dve.wait_ge(b1_in, n * 16)
                nc.vector.tensor_tensor(hn[:, :, :], hn[:, :, :], by_block(b1_bc[:, :]), ALU.add).then_inc(hb_done, 1)
                dve.wait_ge(gelu_done, n)
                nc.vector.tensor_copy(h_hi[:, :, :], hn[:, :, :]).then_inc(h_hi_done, 1)
                dve.wait_ge(h_hi_done, n)
                nc.vector.tensor_tensor(h_lo[:, :, :], hn[:, :, :], h_hi[:, :, :].bitcast(F32), ALU.subtract).then_inc(h_lo_done, 1)
                aside(g, "h")
                if follows:
                    split_y(i + G, 0, par)
                for j in range(G):
                    split_z(i, j)
                    if follows and j + 1 < G:
                        split_eT(i + G, j, True)
                    aside(g, f"z{j}")
                    if follows and j + 1 < G:
                        split_y(i + G, j + 1, par)
                    aside(g, f"y{j}")
                    if follows:
                        split_e(i + G, (g + 1) % NG * G, j, par)
                        if j + 1 == G:
                            split_eT(i + G, j, True)
                    aside(g, f"e{j}")

            def batch(b, follows):
                n_x, n_w = b * (2 * NT) + FIRST_Q, b * (2 * NT) + (FIRST_Q + NT)
                this, after = b % 2, (b + 1) % 2
                link = Chain(dve, dve_link, b * DVE_LINKS)

                def aside(g, at):
                    at = (g, at)
                    if at == (NG - 1, "z1"):
                        dve.wait_ge(mass_turned, b + 1)
                        nc.vector.tensor_copy(massT_hi[:, :], ps_t[0:E, :]).then_inc(mass_split, 1)
                        dve.wait_ge(mass_split, b * 2 + 1)
                        nc.vector.tensor_tensor(massT_lo[:, :], ps_t[0:E, :], massT_hi[:, :].bitcast(F32), ALU.subtract).then_inc(mass_split, 1)
                    if not follows:
                        return
                    if at == (0, "s"):
                        x_stats(b + 1, 0, link)
                    elif at == (0, "h"):
                        x_stats(b + 1, 1, link)
                        x_scale(b + 1, 0, n_x, link)
                    elif at == (0, "z0"):
                        x_scale(b + 1, 1, n_x + 1, link)
                    elif at == (0, "y0"):
                        step(n_x, 0, link)
                    elif at == (0, "e0"):
                        step(n_x + 1, 1, link)
                    elif at == (0, "z1"):
                        x_stats(b + 1, 2, link)
                        x_stats(b + 1, 3, link)
                    elif at == (0, "y1"):
                        x_scale(b + 1, 2, n_x + 2, link)
                    elif at == (0, "e1"):
                        x_scale(b + 1, 3, n_x + 3, link)
                    elif at == (0, "z2"):
                        dequants(0, link)
                        dequants(1, link)
                        scale_product(b + 1, 0, 0, ps_t)
                        step(n_x + 2, 0, link)
                    elif at == (0, "y2"):
                        scale_product(b + 1, 1, 0, ps_l)
                        step(n_x + 3, 1, link)
                    elif at == (0, "e2"):
                        scale_product(b + 1, 0, 1, ps_y)
                    elif at == (0, "e3"):
                        scale_product(b + 1, 1, 1, ps_l)
                    elif at == (1, "z0"):
                        scale_product(b + 1, 0, 2, ps_t)
                    elif at == (1, "y0"):
                        scale_product(b + 1, 1, 2, ps_l)
                    elif at == (1, "e0"):
                        scale_product(b + 1, 0, 3, ps_y)
                    elif at == (1, "z1"):
                        scale_product(b + 1, 1, 3, ps_t)
                        stats1(b + 1, 0, link)
                        dequants(2, link)
                        dequants(3, link)
                    elif at == (1, "y1"):
                        scale_product(b + 1, 2, 0, ps_l)
                        stats1(b + 1, 1, link)
                    elif at == (1, "e1"):
                        scale_product(b + 1, 3, 0, ps_y)
                    elif at == (1, "z2"):
                        scale_product(b + 1, 2, 1, ps_t)
                        stats2(b + 1, 0, link)
                    elif at == (1, "y2"):
                        scale_product(b + 1, 3, 1, ps_l)
                    elif at == (1, "e2"):
                        scale_product(b + 1, 2, 2, ps_y)
                        stats2(b + 1, 1, link)
                    elif at == (1, "e3"):
                        layernorm(b + 1, 0)
                        scale_product(b + 1, 3, 2, ps_l)
                        layernorm(b + 1, 1)
                    elif at == (2, "s"):
                        scale_product(b + 1, 2, 3, ps_y)
                        scale_product(b + 1, 3, 3, ps_t)
                    elif at == (2, "h"):
                        stats1(b + 1, 2, link)
                        stats1(b + 1, 3, link)
                    elif at == (2, "z0"):
                        rl2(b + 1, 0, after, link)
                        rl2(b + 1, 1, after, link)
                    elif at == (2, "y0"):
                        split_u(b + 1, 0, after, ps_l)
                        stats2(b + 1, 2, link)
                    elif at == (2, "e0"):
                        split_u(b + 1, 1, after, ps_y)
                        stats2(b + 1, 3, link)
                    elif at == (2, "z1"):
                        layernorm(b + 1, 2)
                    elif at == (2, "y1"):
                        layernorm(b + 1, 3)
                    elif at == (2, "e1"):
                        rl2(b + 1, 2, after, link)
                    elif at == (2, "z2"):
                        rl2(b + 1, 3, after, link)
                    elif at == (2, "y2"):
                        split_u(b + 1, 2, after, ps_l)
                    elif at == (2, "e2"):
                        split_u(b + 1, 3, after, ps_y)
                    elif at == (3, "s"):
                        w_amax(b + 2, 0)
                        w_amax(b + 2, 1)
                    elif at == (3, "z0"):
                        w_scale(b + 2, 0, n_w, link)
                        w_scale(b + 2, 1, n_w + 1, link)
                    elif at == (3, "y0"):
                        step(n_w, 0, link)
                        step(n_w + 1, 1, link)
                    elif at == (3, "z1"):
                        w_amax(b + 2, 2)
                        w_amax(b + 2, 3)
                    elif at == (3, "y1"):
                        w_scale(b + 2, 2, n_w + 2, link)
                        w_scale(b + 2, 3, n_w + 3, link)
                    elif at == (3, "e1"):
                        step(n_w + 2, 0, link)
                        step(n_w + 3, 1, link)

                for g in range(NG):
                    if g == NG - 1:
                        dve.wait_ge(e_sum_done, b * E + E)
                        nc.vector.tensor_copy(mass_sum[:, :, :], mass[:, bass.ds(this * NT, NT), :]).then_inc(mass_sum_done, 1)
                        nc.vector.tensor_reduce(z_row[:, :], mass[:, bass.ds(this * NT, NT), :], AX_X, ALU.add).then_inc(zr_done, 1)
                        dve.wait_ge(zr_done, b * 3 + 1)
                        nc.vector.reciprocal(z_inv[:, :], z_row[:, :]).then_inc(zr_done, 1)
                        dve.wait_ge(zr_done, b * 3 + 2)
                        nc.vector.tensor_scalar(z_inv[:, :], z_inv[:, :], tgf[:, :], None, ALU.mult).then_inc(zr_done, 1)
                    group(b, g, follows or g < NG - 1, after if g == NG - 1 else this, aside)
                assert not follows or link.count == DVE_LINKS, link.count
                dve.wait_ge(sums_done, b + 1)
                for t in range(NT):
                    dve.wait_ge(last_in[t], b * 16 + 16)
                    nc.vector.scalar_tensor_tensor(last[:, t, :], acc[t][:, :], z_inv[:, t:t + 1], last[:, t, :], ALU.mult,
                                                   ALU.add).then_inc(out_ready, 1)

            link, w = Chain(dve, dve_early), Chain(dve, dve_w1)

            def w1_largest(k):
                dve.wait_ge(w1_in[k], 16)
                w.then(nc.vector.tensor_reduce(w1_max[:, k:k + 1], w1_raw[:, k, :], AX_X, ALU.max, apply_absolute_value=True))

            def both(stage, t):
                stage(0, t)
                stage(0, t + 1)

            def products(t, kb):
                for i in (t, t + 1):
                    scale_product(0, i, kb, EARLY_BANKS[(2 * kb + i % 2) % 4], first=(i < 2 and kb == 0))

            def scale_mu(k):
                for i in range(NT):
                    cols = slice(i * W, (i + 1) * W)
                    ins = nc.vector.tensor_tensor(mu_raw[:, k, cols], mu_raw[:, k, cols], acc[i][:, :], ALU.mult)
                ins.then_inc(mu_scaled, 1)

            def low_w1(k):
                dve.wait_ge(w1_hi_done, k + 1)
                nc.vector.scalar_tensor_tensor(w1_lo[:, k, :], w1_raw[:, k, :], w1_unit[:, 3:4], w1_hi[:, k, :], ALU.mult,
                                               ALU.subtract).then_inc(w1_lo_done, 1)

            for t in range(0, NT, 2):
                for i in (t, t + 1):
                    w_amax(0, i)
                for i in (t, t + 1):
                    w_scale(0, i, i, link)
                for i in (t, t + 1):
                    step(i, i % 2, link)
            dve.wait_ge(tanh_done, 2)
            for t in range(0, NT, 2):
                for i in (t, t + 1):
                    x_stats(0, i, link)
                for i in (t, t + 1):
                    x_scale(0, i, NT + i, link)
                for i in (t, t + 1):
                    step(NT + i, i % 2, link)
                w1_largest(t)
                w1_largest(t + 1)
            w.then(nc.vector.tensor_reduce(w1_unit[:, 0:1], w1_max[:, :], AX_X, ALU.max))
            dve.wait_ge(w1_all_max, 1)
            w.then(nc.vector.tensor_scalar(w1_unit[:, 2:3].bitcast(I32), w1_unit[:, 1:2].bitcast(I32), EXP_MASK, None, ALU.bitwise_and))
            w.then(nc.vector.tensor_scalar(w1_unit[:, 2:3], w1_unit[:, 2:3], 2.0 ** -100, 2.0 ** -14, ALU.max, ALU.mult))
            w.then(nc.vector.reciprocal(w1_unit[:, 3:4], w1_unit[:, 2:3]))
            w.then(nc.vector.tensor_scalar(w1_unit[:, 4:5], w1_unit[:, 2:3], 1.0 / UNIT, None, ALU.mult))
            assert w.count == W1_LINKS
            s = Chain(dve, dve_small)
            s.then(nc.vector.tensor_scalar(logit_scale[:, :], sc_in[:, :], 1.0 / (UNIT * UNIT), None, ALU.mult))
            s.then(nc.vector.tensor_reduce(shift[:, :], sc_in[:, :], AX_X, ALU.max, apply_absolute_value=True))
            s.then(nc.vector.tensor_scalar(shift[:, :], shift[:, :], LOGIT_ROOM, None, ALU.subtract))
            s.then(nc.vector.tensor_scalar(shift[:, :], shift[:, :], 0.0, -1.0, ALU.max, ALU.mult))
            dve.wait_ge(b2_in, 16)
            s.then(nc.vector.tensor_copy(b2_hi[:, :], b2_raw))
            s.then(nc.vector.tensor_tensor(b2_lo[:, :], b2_raw, b2_hi[:, :].bitcast(F32), ALU.subtract))
            dequants(0, link)
            dequants(1, link)
            products(0, 0)
            products(0, 1)
            dve.wait_ge(mu_summed, KD)
            nc.vector.tensor_scalar(mu_norm[:, 0, :], acc[0][:, 0:E], L2_EPS * L2_EPS, None, ALU.max).then_inc(mu_clamped, 1)
            products(0, 2)
            products(0, 3)
            dve.wait_ge(mu_rooted, 1)
            for e in range(E):
                if e >= 2:
                    dve.wait_ge(mu_spread, e - 1)
                nc.vector.tensor_scalar(diag[:, e % 2, :], ident[:, :], mu_norm[:, 1, e:e + 1], UNIT, ALU.mult, ALU.mult).then_inc(mu_diag, 1)
            both(lambda b, i: stats1(b, i, link), 0)
            dequants(2, link)
            dequants(3, link)
            products(2, 0)
            dve.wait_ge(mu_spread, E)
            scale_mu(0)
            products(2, 1)
            both(lambda b, i: stats2(b, i, link), 0)
            products(2, 2)
            scale_mu(1)
            both(layernorm, 0)
            products(2, 3)
            scale_mu(2)
            both(lambda b, i: stats1(b, i, link), 2)
            scale_mu(3)
            both(lambda b, i: rl2(b, i, 0, link), 0)
            split_u(0, 0, 0, ps_t)
            split_u(0, 1, 0, ps_y)
            both(lambda b, i: stats2(b, i, link), 2)
            low_w1(0)
            both(layernorm, 2)
            low_w1(1)
            low_w1(2)
            both(lambda b, i: rl2(b, i, 0, link), 2)
            split_u(0, 2, 0, ps_l)
            split_u(0, 3, 0, ps_zh)
            low_w1(3)
            for j in range(G):
                split_y(0, j, 0)
                for i in (j // 2 * 2, j // 2 * 2 + 1):
                    if j % 2 == 0:
                        w_amax(1, i)
                    else:
                        w_scale(1, i, 2 * NT + i, link)
                split_eT(0, j, False)
                if j % 2 == 1:
                    step(2 * NT + j - 1, 0, link)
                    step(2 * NT + j, 1, link)
                split_e(0, 0, j, 0)
            with dve.Fori(0, B - 1) as b:
                batch(b, True)
            batch(B - 1, False)

        @block.tensor
        def _(pe):
            def three(out, terms, start=True, stop=True, check=True):
                todo = []
                for a_hi, a_lo, b_hi, b_lo in terms:
                    todo += [(a_hi, b_hi), (a_hi, b_lo), (a_lo, b_hi)]
                for n, (a, c) in enumerate(todo):
                    ins = nc.tensor.matmul(out, a, c, start=start and n == 0, stop=stop and n == len(todo) - 1,
                                           skip_group_check=not check)
                return ins

            def turn_q(n, w, bank):
                pe.wait_ge(q_done, n + 1)
                for kb in range(KD):
                    ins = nc.tensor.transpose(banks16(bank)[:, kb * P:(kb + 1) * P], q16[:, w, kb * P:(kb + 1) * P], ident16[:, :])
                ins.then_inc(q_turned, 1)

            def product(b, t, kb, bank, n_q):
                pe.wait_ge(q_copied, n_q)
                nc.tensor.matmul(bank[:, :], qT[:, t, kb, :], wT[:, kb, :], start=True, stop=True).then_inc(prod_done, 1)

            def turn_u(b, t, bank):
                pe.wait_ge(unit_done, nth(b, t) + 1)
                for kb in range(KD):
                    ins = nc.tensor.transpose(bank[:, kb * P:(kb + 1) * P], work[:, t % 2, 0, kb * P:(kb + 1) * P], ident[:, :])
                ins.then_inc(unit_turned, 1)

            u_reg = pe.alloc_register("u_reg")

            def u_base(par):
                pe.reg_mov(u_reg, par * (KD * N))
                return pe.snap(u_reg, min_val=0, max_val=KD * N)

            def logits(i, j, g, par):
                cols = bass.ds(g * W + j * S, S)
                base = u_base(par)
                three(ps_l[:, :], [(mu_hi[:, k, cols], mu_lo[:, k, cols], uT_hi[:, bass.ds(base + k * N, N)],
                                    uT_lo[:, bass.ds(base + k * N, N)]) for k in range(KD)]).then_inc(l_done, 1)

            def project(i, j, g, par):
                cols = bass.ds(g * W, W)
                base = u_base(par)
                three(ps_y[:, :], [(uT_hi[:, bass.ds(base + (k * N + j * P), P)], uT_lo[:, bass.ds(base + (k * N + j * P), P)],
                                    w1_hi[:, k, cols], w1_lo[:, k, cols]) for k in range(KD)]).then_inc(y_done, 1)

            def turn(i, j):
                pe.wait_ge(exp_done, i + j + 1)
                for t in range(NT):
                    ins = nc.tensor.transpose(ps_t[:, t * P:(t + 1) * P], eT[:, j, t * P:(t + 1) * P], ident[:, :])
                ins.then_inc(t_done, 1)

            def slots(i):
                pe.wait_ge(e_lo_done, i + G)
                pe.wait_ge(y_lo_done, i + G)
                for j in range(G):
                    ins = three(ps_zh[:, j * H:(j + 1) * H], [(e_hi[:, j, t, :], e_lo[:, j, t, :], y_hi[:, t, j * H:(j + 1) * H],
                                                               y_lo[:, t, j * H:(j + 1) * H]) for t in range(NT)])
                ins.then_inc(h_done, 1)

            def combine(i, j, n):
                if j == 0:
                    pe.wait_ge(h_lo_done, n)
                else:
                    pe.wait_ge(z_lo_done, i + j)
                pe.wait_ge(eT_lo_done, i + j + 1)
                three(ps_zh[:, :], [(h_hi[:, j, :], h_lo[:, j, :], eT_hi[:, j, :], eT_lo[:, j, :])]).then_inc(z_done, 1)

            def expand(i, j, first=False):
                pe.wait_ge(z_lo_done, i + j + 1)
                pe.wait_ge(w2_split, i + j + 1)
                for t in range(NT):
                    rows = slice(t * P, (t + 1) * P)
                    ins = three(acc[t][:, :], [(z_hi[:, rows], z_lo[:, rows], w2_hi[:, j % 2, :], w2_lo[:, j % 2, :])], start=first,
                                stop=False, check=False)
                ins.then_inc(f_done, 1)

            def batch(b, follows):
                n_x, n_w = b * (2 * NT) + FIRST_Q, b * (2 * NT) + (FIRST_Q + NT)
                this, after = b % 2, (b + 1) % 2
                plan = {
                    (0, "c1"): ("x", 0), (0, "b1"): ("x", 1), (0, "a2"): ("p", 0, 0), (0, "c2"): ("p", 1, 0), (0, "b2"): ("p", 0, 1),
                    (0, "c3"): ("p", 1, 1),
                    (1, "bs"): ("x", 2), (1, "as"): ("x", 3), (1, "a0"): ("p", 0, 2), (1, "c0"): ("p", 1, 2), (1, "b0"): ("p", 0, 3),
                    (1, "a1"): ("p", 1, 3), (1, "c1"): ("p", 2, 0), (1, "b1"): ("p", 3, 0), (1, "a2"): ("p", 2, 1), (1, "c2"): ("p", 3, 1),
                    (1, "b2"): ("p", 2, 2), (1, "c3"): ("p", 3, 2),
                    (2, "bs"): ("p", 2, 3), (2, "as"): ("p", 3, 3),
                    (2, "c0"): ("u", 0), (2, "b0"): ("u", 1), (2, "c2"): ("u", 2), (2, "b2"): ("u", 3),
                    (3, "c1"): ("w", 0), (3, "b1"): ("w", 1), (3, "b2"): ("w", 2), (3, "c3"): ("w", 3),
                } if follows else {}
                plan[(3, "a1")] = ("m",)
                bank_of = {"a": ps_t, "b": ps_y, "c": ps_l}

                def read(g, place):
                    what = plan.get((g % NG, place))
                    if what is None:
                        return
                    kind = what[0]
                    if kind == "x":
                        pe.wait_ge(q_copied, n_x + what[1] + 1)
                    elif kind == "w":
                        pe.wait_ge(q_copied, n_w + what[1] + 1)
                    elif kind == "p":
                        pe.wait_ge(prod_scaled, nth_product(b + 1, what[1], what[2]) + 1)
                    elif kind == "u":
                        pe.wait_ge(uT_lo_done, nth(b + 1, what[1]) + 1)
                    else:
                        pe.wait_ge(mass_split, b * 2 + 2)

                def aside(g, place, i):
                    what = plan.get((g, place))
                    if what is None:
                        return
                    kind, bank = what[0], bank_of[place[0]]
                    j = 0 if place[1] == "s" else int(place[1])
                    if place[0] == "a":
                        pe.wait_ge(e_sum_done, i + j if follows else i)
                    elif place[0] == "c":
                        pe.wait_ge(exp_done, i + min(j + 2, G))
                    elif place != "bs":
                        pe.wait_ge(y_lo_done, i + min(j + 2, G))
                    if place == "bs":
                        read(g - 1, "b2")
                    if place == "a0":
                        read(g, "as")
                    if place == "c3":
                        read(g, "c2")
                    if kind == "x":
                        turn_q(n_x + what[1], what[1] % 2, bank)
                    elif kind == "w":
                        turn_q(n_w + what[1], what[1] % 2, bank)
                    elif kind == "p":
                        product(b + 1, what[1], what[2], bank, n_x + (what[1] + 1 if g == 0 else NT))
                    elif kind == "u":
                        turn_u(b + 1, what[1], bank)
                    else:
                        pe.wait_ge(mass_sum_done, b + 1)
                        for t in range(NT):
                            ins = nc.tensor.transpose(ps_t[0:E, t * P:(t + 1) * P], mass_sum[:, t, :], ident[:, :])
                        ins.then_inc(mass_turned, 1)

                for g in range(NG):
                    i, n = b * E + g * G, b * NG + g + 1
                    more = follows or g < NG - 1
                    par, nxt = (after, 0) if g == NG - 1 else (this, g + 1)
                    slots(i)
                    aside(g, "bs", i + G)
                    aside(g, "as", i + G)
                    if more:
                        if g > 0:
                            read(g - 1, "c3")
                        else:
                            pe.wait_ge(q_copied, n_x)
                        if g == NG - 1:
                            pe.wait_ge(uT_lo_done, b * NT + 2 * NT)
                        pe.wait_ge(exp_done, i + G)
                        logits(i + G, 0, nxt, par)
                        if g > 0:
                            read(g - 1, "b2")
                        read(g, "bs")
                        pe.wait_ge(y_lo_done, i + G)
                        project(i + G, 0, nxt, par)
                    for j in range(G):
                        combine(i, j, n)
                        if j + 1 < G:
                            aside(g, f"a{j}", i + G)
                        if more and j + 1 < G:
                            pe.wait_ge(exp_done, i + G + j + 1)
                            if j >= 1:
                                read(g, f"c{j - 1}")
                            logits(i + G, j + 1, nxt, par)
                            pe.wait_ge(y_lo_done, i + G + j + 1)
                            if j >= 1:
                                read(g, f"b{j - 1}")
                            project(i + G, j + 1, nxt, par)
                        if j + 1 < G:
                            aside(g, f"c{j}", i + G)
                        if more:
                            if j >= 1:
                                pe.wait_ge(e_sum_done, i + G + j)
                            if j + 1 < G:
                                read(g, f"a{j}")
                            if j == 0:
                                read(g, "as")
                            turn(i + G, j)
                        if j + 1 == G:
                            aside(g, f"c{j}", i + G)
                        expand(i, j, first=(g == 0 and j == 0))
                        if j + 1 < G:
                            aside(g, f"b{j}", i + G)
                pe.wait_ge(mass_split, b * 2 + 2)
                for t in range(NT):
                    rows = slice(t * P, (t + 1) * P)
                    ins = three(acc[t][:, :], [(massT_hi[:, rows], massT_lo[:, rows], b2_hi[:, :], b2_lo[:, :])], start=False, check=False)
                ins.then_inc(sums_done, 1)

            def early_product(i, kb):
                at = nth_product(0, i, kb)
                if at >= 4:
                    pe.wait_ge(prod_scaled, at - 3)
                product(0, i, kb, EARLY_BANKS[(2 * kb + i % 2) % 4], 2 * NT)

            pe.wait_ge(pool_const, 5)
            pe.wait_ge(ones_done, 1)
            for k in range(KD):
                for n in (2 * k, 2 * k + 1):
                    if n >= 2:
                        pe.wait_ge(q_copied, n - 1)
                    turn_q(n, n % 2, (ps_t, ps_y)[n % 2])
                if k == KD - 1:
                    pe.wait_ge(q_copied, 2 * NT)
                    pe.wait_ge(dve_small, 6)
                    for kb in (0, 1):
                        early_product(0, kb)
                        early_product(1, kb)
                pe.wait_ge(mu_squared, k + 1)
                for e in range(E):
                    ins = nc.tensor.matmul(acc[0][:, e:e + 1], flat(eT[:, :, :])[:, e * S:(e + 1) * S], ones[:, 0:1], start=(k == 0 and e == 0),
                                           stop=(k == KD - 1), skip_group_check=True)
                ins.then_inc(mu_summed, 1)
            for kb in (2, 3):
                early_product(0, kb)
                early_product(1, kb)
            for e in range(E):
                pe.wait_ge(mu_diag, e + 1)
                nc.tensor.matmul(acc[e // G][:, e % G * S:(e % G + 1) * S], ones, diag[:, e % 2, :], start=True, stop=True).then_inc(mu_spread, 1)
            for kb in range(KD):
                early_product(2, kb)
                early_product(3, kb)
            pe.wait_ge(prod_scaled, NT * KD)
            for t, bank in enumerate((ps_t, ps_y, ps_l, ps_zh)):
                turn_u(0, t, bank)
            pe.sem_inc(f_done, 2)
            pe.wait_ge(uT_lo_done, NT)
            pe.wait_ge(mu_lo_done, KD)
            pe.wait_ge(w1_lo_done, KD)
            for j in range(G):
                if j >= 1:
                    pe.wait_ge(exp_done, j)
                logits(0, j, 0, 0)
                if j >= 1:
                    pe.wait_ge(y_lo_done, j)
                project(0, j, 0, 0)
                if j >= 1:
                    pe.wait_ge(e_sum_done, j)
                turn(0, j)
                if j >= 2:
                    for n in (2 * j - 4, 2 * j - 3):
                        turn_q(2 * NT + n, n % 2, acc[n])
            pe.wait_ge(exp_done, G)
            pe.wait_ge(y_lo_done, G)
            with pe.Fori(0, B - 1) as b:
                batch(b, True)
            batch(B - 1, False)


_INS = ["x", "ctx_2048", "g_xattn", "g_ffn", "L0_ffn_gamma", "L0_ffn_beta", "L0_ffn_mu", "L0_ffn_scale",
        "L0_ffn_W1", "L0_ffn_b1", "L0_ffn_W2", "L0_ffn_b2"]


def kernel(**inputs):
    import numpy as _np
    import concourse.bacc as _bacc
    from concourse import mybir as _mybir
    from concourse.bass_utils import run_bass_kernel_spmd as _run

    nc = _bacc.Bacc("TRN2", target_bir_lowering=False, num_devices=1)
    arrays, args = {}, []
    for name in _INS:
        a = _np.ascontiguousarray(inputs[name])
        arrays[f"in_{name}_dram"] = a
        args.append(nc.dram_tensor(f"in_{name}_dram", a.shape, _mybir.dt.from_np(a.dtype), kind="ExternalInput").ap())
    args.append(nc.dram_tensor("out_dram", arrays["in_x_dram"].shape, _mybir.dt.float32, kind="ExternalOutput").ap())
    flamingo_block(nc, *args)
    r = _run(nc, [arrays], core_ids=[0])
    return r.results[0]["out_dram"]
```

```python
from contextlib import ExitStack

import concourse.bass as bass
from concourse import mybir

ALU = mybir.AluOpType
ACT = mybir.ActivationFunctionType
AX_X = mybir.AxisListType.X
F32 = mybir.dt.float32
F32R = mybir.dt.float32r
F16 = mybir.dt.float16
BF16 = mybir.dt.bfloat16
I32 = mybir.dt.int32

P = 128
FP8_MAX = 448.0
ACT_EPS, W_EPS = 1e-4, 1e-6
LN_EPS, L2_EPS = 1e-5, 1e-12
EXP_MASK = 0x7F800000
UNIT = 2.0 ** 13
LOGIT_ROOM = 60.0


def flamingo_block(nc, x, ctx_w, g_xattn, g_ffn, gamma, beta, mu, scale, w1, b1, w2, b2, out):
    B, N, D = x.shape
    _, E, S = mu.shape
    H = w1.shape[2]
    KD = D // P
    NT = N // P
    G = 4
    NG = E // G
    W = G * S
    assert S == P and H == P and N == 512 and D == 512 and W == 512 and NG == 4 and NT == 4 and KD == 4

    x_rows = x.rearrange("b n d -> (b n) d")
    ctx_rows = ctx_w.rearrange("b n d -> (b n) d")
    out_rows = out.rearrange("b n d -> (b n) d")
    mu_dram = mu.rearrange("(k p) e s -> p k (e s)", p=P)
    w1_dram = w1.rearrange("e (k p) h -> p k e h", p=P)
    w2_dram = w2.rearrange("e h d -> h e d")
    b1_flat = b1.rearrange("e h -> (e h)")

    with ExitStack() as es:
        def sb(name, shape, dt=F32):
            return es.enter_context(nc.sbuf_tensor(name, shape, dt))

        def sem(name):
            return es.enter_context(nc.semaphore(name))

        acc = [es.enter_context(nc.psum_tensor(f"acc{t}", [P, D], F32)) for t in range(NT)]
        ps_l = es.enter_context(nc.psum_tensor("ps_l", [P, N], F32))
        ps_zh = es.enter_context(nc.psum_tensor("ps_zh", [P, N], F32))
        ps_t = es.enter_context(nc.psum_tensor("ps_t", [P, N], F32))
        ps_y = es.enter_context(nc.psum_tensor("ps_y", [P, N], F32))

        ident = sb("ident", [P, P])
        ident16 = sb("ident16", [P, P], BF16)
        gx = sb("gx", [P, 1])
        gf = sb("gf", [P, 1])
        sc_in = sb("sc_in", [P, 1])
        tgx = sb("tgx", [P, 1])
        tgf = sb("tgf", [P, 1])
        half = sb("half", [P, 1])
        mhalf = sb("mhalf", [P, E])
        logit_scale = sb("logit_scale", [P, 1])
        shift = sb("shift", [P, 1])
        gam = sb("gam", [P, D])
        bet = sb("bet", [P, D])
        b1_bc = sb("b1_bc", [P, W])
        b2_hi = sb("b2_hi", [E, D], F32R)
        b2_lo = sb("b2_lo", [E, D], F32R)
        mu_hi = sb("mu_hi", [P, KD, E * S], F16)
        mu_lo = sb("mu_lo", [P, KD, E * S], F16)
        mu_norm = sb("mu_norm", [P, 2, E])
        w1_hi = sb("w1_hi", [P, KD, E * H], F16)
        w1_lo = sb("w1_lo", [P, KD, E * H], F16)
        w1_max = sb("w1_max", [P, KD])
        w1_unit = sb("w1_unit", [P, 5])
        w2_raw = sb("w2_raw", [P, D])
        w2_hi = sb("w2_hi", [P, 2, D], F32R)
        w2_lo = sb("w2_lo", [P, 2, D], F32R)

        work = sb("work", [P, 2, 2, D])
        q16 = sb("q16", [P, 2, D], BF16)
        qT = sb("qT", [P, NT, KD, P], BF16)
        wT = sb("wT", [P, KD, N], BF16)
        x1 = sb("x1", [P, NT, D])
        stat = sb("stat", [P, 2, 8])
        norm = sb("norm", [P, 2, 6])
        amax = sb("amax", [P, 2, 4])
        amax_all = sb("amax_all", [P, 2, 4])
        quant = sb("quant", [P, 2, 4])
        x_dequant = sb("x_dequant", [P, NT, 4])
        w_dequant = sb("w_dequant", [P, KD, NT])
        dequant = sb("dequant", [P, 2, KD, NT])
        uT_hi = sb("uT_hi", [P, 2 * KD * N], F16)
        uT_lo = sb("uT_lo", [P, 2 * KD * N], F16)
        y_scale = sb("y_scale", [P, 2 * NT])

        eT = sb("eT", [P, G, N])
        den = sb("den", [P, G])
        rden = sb("rden", [P, G])
        hn = sb("hn", [P, G, H])
        mass = sb("mass", [P, 2 * NT, E])
        mass_sum = sb("mass_sum", [P, NT, E])
        z_row = sb("z_row", [P, NT])
        z_inv = sb("z_inv", [P, NT])

        def by_block(ap):
            return ap.rearrange("p (k c) -> p k c", c=P)

        with nc.sbuf_tensor("prod", [P, 2, D], F32) as prod:
            pass
        massT_hi = sb("massT_hi", [E, N], F32R)
        massT_lo = sb("massT_lo", [E, N], F32R)
        b2_raw, diag, ones = prod[0:E, 0, :], by_block(eT[:, 0, :]), hn[:, 0, :]

        with nc.sbuf_tensor("mu_raw", [P, KD, E * S], F32) as mu_raw, nc.sbuf_tensor("w1_raw", [P, KD, E * H], F32) as w1_raw:
            pass
        e_hi = sb("e_hi", [P, G, NT, S], F32R)
        e_lo = sb("e_lo", [P, G, NT, S], F32R)
        y_hi = sb("y_hi", [P, NT, W], F32R)
        y_lo = sb("y_lo", [P, NT, W], F32R)
        eT_hi = sb("eT_hi", [P, G, N], F32R)
        eT_lo = sb("eT_lo", [P, G, N], F32R)
        h_hi = sb("h_hi", [P, G, H], F32R)
        h_lo = sb("h_lo", [P, G, H], F32R)
        z_hi = sb("z_hi", [P, N], F32R)
        z_lo = sb("z_lo", [P, N], F32R)
        last = sb("last", [P, NT, D])

        x1_dram = nc.dram_tensor("x1_dram", [B * N, D], F32, kind="Internal").ap()

        consts_in, b2_in, b1_in = sem("consts_in"), sem("b2_in"), sem("b1_in")
        mu_in = [sem(f"mu_in{i}") for i in range(KD)]
        w1_in = [sem(f"w1_in{i}") for i in range(KD)]
        w2_in = sem("w2_in")
        x_in = [sem(f"x_in{t}") for t in range(NT)]
        ctx_in = [sem(f"ctx_in{t}") for t in range(NT)]
        x1_stored = [sem(f"x1_stored{t}") for t in range(NT)]
        last_in = [sem(f"last_in{t}") for t in range(NT)]
        out_written = [sem(f"out_written{t}") for t in range(NT)]
        pool_const, ones_done = sem("pool_const"), sem("ones_done")
        tanh_done, dve_small, dve_w1 = sem("tanh_done"), sem("dve_small"), sem("dve_w1")
        mu_squared, mu_summed, mu_clamped, mu_rooted = sem("mu_squared"), sem("mu_summed"), sem("mu_clamped"), sem("mu_rooted")
        mu_added = sem("mu_added")
        mu_diag, mu_spread, mu_scaled, mu_hi_done, mu_lo_done = sem("mu_diag"), sem("mu_spread"), sem("mu_scaled"), sem("mu_hi_done"), sem("mu_lo_done")
        w1_all_max, w1_hi_done, w1_lo_done = sem("w1_all_max"), sem("w1_hi_done"), sem("w1_lo_done")
        w_amax_done, w_amax_all = sem("w_amax_done"), sem("w_amax_all")
        x_var_done, x_rstd_done = sem("x_var_done"), sem("x_rstd_done")
        q_scale_done, q_scaled, q_step_done = sem("q_scale_done"), sem("q_scaled"), sem("q_step_done")
        q_done, q_turned, q_copied = sem("q_done"), sem("q_turned"), sem("q_copied")
        prod_done, prod_scaled, prod_added = sem("prod_done"), sem("prod_scaled"), sem("prod_added")
        var1_done, rstd1_done, var2_done, rstd2_done = sem("var1_done"), sem("rstd1_done"), sem("var2_done"), sem("rstd2_done")
        ln_done, affine_done, squares_done, l2_done = sem("ln_done"), sem("affine_done"), sem("squares_done"), sem("l2_done")
        rl2_done, unit_done, unit_turned, uT_hi_done, uT_lo_done = (sem("rl2_done"), sem("unit_done"), sem("unit_turned"),
                                                                    sem("uT_hi_done"), sem("uT_lo_done"))
        dve_early, dve_link, pool_early, pool_link = sem("dve_early"), sem("dve_link"), sem("pool_early"), sem("pool_link")
        w2_half, w2_split, held = sem("w2_half"), sem("w2_split"), sem("held")
        l_done, y_done, h_done, z_done, t_done, f_done = (sem("l_done"), sem("y_done"), sem("h_done"), sem("z_done"),
                                                          sem("t_done"), sem("f_done"))
        exp_done, gelu_done, y_hi_done, z_hi_done, e_hi_done = (sem("exp_done"), sem("gelu_done"), sem("y_hi_done"),
                                                                sem("z_hi_done"), sem("e_hi_done"))
        rden_done, hn_done, hb_done, h_hi_done, h_lo_done = (sem("rden_done"), sem("hn_done"), sem("hb_done"),
                                                             sem("h_hi_done"), sem("h_lo_done"))
        y_lo_done, z_lo_done, eT_hi_done, eT_lo_done = sem("y_lo_done"), sem("z_lo_done"), sem("eT_hi_done"), sem("eT_lo_done")
        e_lo_done, e_sum_done = sem("e_lo_done"), sem("e_sum_done")
        mass_sum_done, mass_turned, mass_split, zr_done = (sem("mass_sum_done"), sem("mass_turned"), sem("mass_split"),
                                                            sem("zr_done"))
        sums_done, out_ready = sem("sums_done"), sem("out_ready")

        W1_LINKS, DVE_LINKS, POOL_LINKS = KD + 5, 72, 12
        EARLY_BANKS = (ps_y, ps_l, ps_zh, ps_t)
        FIRST_Q = 3 * NT

        class Chain:

            def __init__(self, engine, semaphore, start=0):
                self.engine, self.semaphore, self.start, self.count = engine, semaphore, start, 0

            def then(self, instruction):
                self.count += 1
                instruction.then_inc(self.semaphore, 1)
                self.engine.wait_ge(self.semaphore, self.start + self.count)

        def hold(engine):
            engine.sem_inc(held, 1)

        def spread(ap, n=P):
            return ap.rearrange("p (k a) -> p k a", a=1).to_broadcast([P, 4, n])

        def flat(ap):
            return ap.rearrange("p a b -> p (a b)")

        def nth(b, t):
            return b * NT + t

        def nth_product(b, t, kb):
            return b * (NT * KD) + ((t // 2) * 2 * KD + 2 * kb + t % 2)

        def banks16(bank):
            return bank[:, 0:D // 2].bitcast(BF16)

        def u_view(u, par, t):
            return u[:, :].rearrange("p (a k n) -> p a k n", a=2, k=KD)[:, bass.ds(par, 1), :, t * P:(t + 1) * P].rearrange(
                "p a k n -> p (a k) n")

        mu_squares = [flat(eT[:, :, :])] + [flat(half_of[:, k:k + 2, :]).bitcast(F32) for half_of, k in ((mu_hi, 0), (mu_hi, 2), (mu_lo, 0))]

        def z_place(j, final):
            if final:
                return (ps_zh, ps_l, ps_y, ps_zh)[j], y_hi[:, j, :], y_lo[:, j, :]
            return ps_zh, z_hi[:, :], z_lo[:, :]

        def ctx_place(b, t):
            return prod[:, t % 2, :] if isinstance(b, int) and b == 0 and t >= 2 else work[:, t % 2, 0, :]

        def y_of(b, t):
            return work[:, t % 2, t // 2 if isinstance(b, int) else 0, :]

        block = es.enter_context(nc.Block())

        @block.sync
        def _(sp):
            def load_ctx(b, t, n, later):
                if later:
                    sp.wait_ge(q_done, n - 1)
                sp.dma_start(ctx_place(b, t), ctx_rows[bass.ds((b % B) * N + t * P, P), :]).then_inc(ctx_in[t], 16)

            def load_x(b, t):
                sp.dma_start(x1[:, t, :], x_rows[bass.ds((b % B) * N + t * P, P), :]).then_inc(x_in[t], 16)

            def store_x1(b, t):
                sp.wait_ge(prod_added, nth_product(b, t, KD - 1) + 1)
                sp.dma_start(x1_dram[bass.ds(b * N + t * P, P), :], x1[:, t, :]).then_inc(x1_stored[t], 16)

            def load_b1(n, g):
                if n is not None:
                    sp.wait_ge(hb_done, n)
                sp.dma_start(b1_bc[:, :], b1_flat[bass.ds(g * W, W)].partition_broadcast(P)).then_inc(b1_in, 16)

            def load_w2(b, *experts):
                for e in experts:
                    sp.wait_ge(w2_split, b * E + e)
                    sp.dma_start(w2_raw[:, :], w2_dram[:, e % E, :]).then_inc(w2_in, 16)

            def outputs(b):
                for t in range(NT):
                    sp.wait_ge(out_written[t], (b + 1) * 16)
                    hold(sp)
                    sp.wait_ge(x1_stored[t], b * 16 + 16)
                    sp.dma_start(last[:, t, :], x1_dram[bass.ds(b * N + t * P, P), :]).then_inc(last_in[t], 16)
                for t in range(NT):
                    sp.wait_ge(out_ready, nth(b, t) + 1)
                    sp.dma_start(out_rows[bass.ds(b * N + t * P, P), :], last[:, t, :]).then_inc(out_written[t], 16)

            for t in range(NT):
                sp.sem_inc(out_written[t], 16)
            for t in range(NT):
                load_ctx(0, t, t, False)
            for dst, src in ((gx, g_xattn), (gf, g_ffn), (sc_in, scale), (gam, gamma), (bet, beta)):
                sp.dma_start(dst[:, :], src.partition_broadcast(P)).then_inc(consts_in, 16)
            for t in range(NT):
                load_x(0, t)
            for k in range(KD):
                sp.dma_start(mu_raw[:, k, :], mu_dram[:, k]).then_inc(mu_in[k], 16)
            for k in range(KD):
                sp.dma_start(w1_raw[:, k, :].rearrange("p (c h) -> p c h", h=H), w1_dram[:, k]).then_inc(w1_in[k], 16)
            sp.wait_ge(q_scaled, NT)
            sp.dma_start(b2_raw, b2).then_inc(b2_in, 16)
            load_b1(None, 0)
            sp.dma_start(w2_raw[:, :], w2_dram[:, 0, :]).then_inc(w2_in, 16)
            for t in range(NT):
                store_x1(0, t)
            sp.wait_ge(unit_turned, NT)
            for t in range(NT):
                load_ctx(1, t, 2 * NT + t, True)
                sp.wait_ge(x1_stored[t], 16)
                load_x(1, t)
            with sp.Fori(0, B - 1) as b:
                load_b1(b * NG + 1, 1)
                load_w2(b, 1, 2, 3, 4)
                load_b1(b * NG + 2, 2)
                load_w2(b, 5, 6, 7)
                store_x1(b + 1, 0)
                store_x1(b + 1, 1)
                load_w2(b, 8, 9)
                load_b1(b * NG + 3, 3)
                store_x1(b + 1, 2)
                store_x1(b + 1, 3)
                load_w2(b, 10, 11)
                sp.wait_ge(unit_turned, nth(b + 1, NT - 1) + 1)
                n = b * (2 * NT) + (FIRST_Q + NT)
                load_ctx(b + 2, 0, n, True)
                load_ctx(b + 2, 1, n + 1, True)
                load_w2(b, 12)
                for t in range(NT):
                    sp.wait_ge(x1_stored[t], b * 16 + 32)
                    load_x(b + 2, t)
                load_b1(b * NG + 4, 0)
                load_w2(b, 13)
                load_ctx(b + 2, 2, n + 2, True)
                load_ctx(b + 2, 3, n + 3, True)
                load_w2(b, 14, 15, 16)
                outputs(b)
            for g in range(1, NG):
                load_b1((B - 1) * NG + g, g)
                load_w2(B - 1, *range(g * G - 3, g * G + 1))
            load_w2(B - 1, *range(E - 3, E))
            outputs(B - 1)
            for t in range(NT):
                sp.wait_ge(out_written[t], 16 * B + 16)

        @block.gpsimd
        def _(pool):
            def reduce_weights(b, t):
                w = t % 2
                pool.wait_ge(w_amax_done, nth(b, t) + 1)
                hold(pool)
                nc.gpsimd.partition_all_reduce(amax_all[:, w, :], amax[:, w, :], P, bass.bass_isa.ReduceOp.max).then_inc(w_amax_all, 1)

            def root(b, t, col_in, waits, col_out, exponent, done):
                w = t % 2
                pool.wait_ge(waits, nth(b, t) + 1)
                src = stat[:, w, 7:8] if col_in is None else norm[:, w, col_in:col_in + 1]
                nc.gpsimd.tensor_tensor(norm[:, w, col_out:col_out + 1], src, exponent, ALU.pow).then_inc(done, 1)

            def x_rstd(b, t):
                root(b, t, None, x_var_done, 0, mhalf[:, 0:1], x_rstd_done)

            def rstd1(b, t):
                root(b, t, None, var1_done, 1, mhalf[:, 0:1], rstd1_done)

            def rstd2(b, t):
                root(b, t, None, var2_done, 2, mhalf[:, 0:1], rstd2_done)

            def l2(b, t):
                root(b, t, 3, squares_done, 4, half[:, :], l2_done)

            def round_(n, w, link):
                a, m = work[:, w, 0, :], work[:, w, 1, :]
                pool.wait_ge(q_step_done, n + 1)
                link.then(nc.gpsimd.tensor_tensor(a, a, m, ALU.add))
                pool.wait_ge(q_turned, n - 1)
                nc.gpsimd.tensor_tensor(q16[:, w, :], a, m, ALU.subtract).then_inc(q_done, 1)

            def add(b, t, kb):
                pool.wait_ge(prod_scaled, nth_product(b, t, kb) + 1)
                nc.gpsimd.tensor_tensor(x1[:, t, :], x1[:, t, :], prod[:, t % 2, :], ALU.add).then_inc(prod_added, 1)

            def affine(b, t, link):
                y = y_of(b, t)
                pool.wait_ge(ln_done, nth(b, t) + 1)
                link.then(nc.gpsimd.tensor_tensor(y, y, gam[:, :], ALU.mult))
                nc.gpsimd.tensor_tensor(y, y, bet[:, :], ALU.add).then_inc(affine_done, 1)

            def split_w2(b, e):
                i, s = b * E + e, e % 2
                pool.wait_ge(w2_in, i * 16 + 16)
                pool.wait_ge(f_done, i + 1)
                hold(pool)
                nc.gpsimd.tensor_scalar(w2_hi[:, s, :], w2_raw[:, :], 1.0, 1.0, ALU.mult, ALU.mult).then_inc(w2_half, 1)
                pool.wait_ge(w2_half, i + 1)
                nc.gpsimd.tensor_tensor(w2_lo[:, s, :], w2_raw[:, :], w2_hi[:, s, :].bitcast(F32), ALU.subtract).then_inc(w2_split, 1)

            c = Chain(pool, pool_const)
            c.then(nc.gpsimd.memset(mhalf[:, :], -0.5))
            c.then(nc.gpsimd.memset(half[:, :], 0.5))
            c.then(nc.gpsimd.memset(ident[:, :], 0.0))
            c.then(nc.gpsimd.affine_select(out=ident[:, :], in_=ident[:, :], compare_op=ALU.not_equal, fill=1.0,
                                           base=0, pattern=[[-1, P]], channel_multiplier=1))
            c.then(nc.gpsimd.tensor_copy(ident16[:, :], ident[:, :]))
            nc.gpsimd.memset(ones, 1.0).then_inc(ones_done, 1)
            link, total = Chain(pool, pool_early), Chain(pool, mu_added)

            def add_squares(k):
                pool.wait_ge(mu_squared, k + 1)
                total.then(nc.gpsimd.tensor_tensor(mu_squares[0], mu_squares[0], mu_squares[k], ALU.add))

            for i in range(NT):
                reduce_weights(0, i)
            x_rstd(0, 0)
            x_rstd(0, 1)
            add_squares(1)
            add_squares(2)
            x_rstd(0, 2)
            x_rstd(0, 3)
            add_squares(3)
            for kb in (0, 1):
                for i in (0, 1):
                    add(0, i, kb)
            pool.wait_ge(mu_clamped, 1)
            nc.gpsimd.tensor_tensor(mu_norm[:, 1, :], mu_norm[:, 0, :], mhalf[:, :], ALU.pow).then_inc(mu_rooted, 1)
            for kb in (2, 3):
                for i in (0, 1):
                    add(0, i, kb)

            def both(stage, t):
                stage(0, t)
                stage(0, t + 1)

            def low_mu(k):
                pool.wait_ge(mu_hi_done, k + 1)
                nc.gpsimd.tensor_tensor(mu_lo[:, k, :], mu_raw[:, k, :], mu_hi[:, k, :], ALU.subtract).then_inc(mu_lo_done, 1)

            both(rstd1, 0)
            both(lambda b, i: add(b, i, 0), 2)
            both(lambda b, i: add(b, i, 1), 2)
            both(rstd2, 0)
            both(lambda b, i: add(b, i, 2), 2)
            both(lambda b, i: affine(b, i, link), 0)
            both(lambda b, i: add(b, i, 3), 2)
            both(rstd1, 2)
            both(l2, 0)
            pool.wait_ge(dve_w1, KD + 1)
            nc.gpsimd.partition_all_reduce(w1_unit[:, 1:2], w1_unit[:, 0:1], P, bass.bass_isa.ReduceOp.max).then_inc(w1_all_max, 1)
            both(rstd2, 2)
            low_mu(0)
            both(lambda b, i: affine(b, i, link), 2)
            low_mu(1)
            both(l2, 2)
            low_mu(2)
            for i in range(NT):
                reduce_weights(1, i)

            def batch(b, aside):
                link = Chain(pool, pool_link, b * POOL_LINKS)
                n_x, n_w = b * (2 * NT) + FIRST_Q, b * (2 * NT) + (FIRST_Q + NT)
                if not aside:
                    for e in range(E):
                        split_w2(b, e)
                    return
                x_rstd(b + 1, 0)
                split_w2(b, 0)
                x_rstd(b + 1, 1)
                split_w2(b, 1)
                round_(n_x, 0, link)
                round_(n_x + 1, 1, link)
                split_w2(b, 2)
                x_rstd(b + 1, 2)
                x_rstd(b + 1, 3)
                split_w2(b, 3)
                add(b + 1, 0, 0)
                round_(n_x + 2, 0, link)
                add(b + 1, 1, 0)
                round_(n_x + 3, 1, link)
                add(b + 1, 0, 1)
                add(b + 1, 1, 1)
                split_w2(b, 4)
                split_w2(b, 5)
                add(b + 1, 0, 2)
                add(b + 1, 1, 2)
                split_w2(b, 6)
                add(b + 1, 0, 3)
                add(b + 1, 1, 3)
                rstd1(b + 1, 0)
                add(b + 1, 2, 0)
                rstd1(b + 1, 1)
                split_w2(b, 7)
                add(b + 1, 3, 0)
                rstd2(b + 1, 0)
                add(b + 1, 2, 1)
                add(b + 1, 3, 1)
                rstd2(b + 1, 1)
                add(b + 1, 2, 2)
                split_w2(b, 8)
                affine(b + 1, 0, link)
                add(b + 1, 3, 2)
                add(b + 1, 2, 3)
                affine(b + 1, 1, link)
                add(b + 1, 3, 3)
                l2(b + 1, 0)
                l2(b + 1, 1)
                split_w2(b, 9)
                rstd1(b + 1, 2)
                split_w2(b, 10)
                rstd1(b + 1, 3)
                rstd2(b + 1, 2)
                affine(b + 1, 2, link)
                rstd2(b + 1, 3)
                l2(b + 1, 2)
                affine(b + 1, 3, link)
                l2(b + 1, 3)
                split_w2(b, 11)
                reduce_weights(b + 2, 0)
                reduce_weights(b + 2, 1)
                split_w2(b, 12)
                round_(n_w, 0, link)
                round_(n_w + 1, 1, link)
                split_w2(b, 13)
                reduce_weights(b + 2, 2)
                reduce_weights(b + 2, 3)
                split_w2(b, 14)
                round_(n_w + 2, 0, link)
                round_(n_w + 3, 1, link)
                split_w2(b, 15)
                assert link.count == POOL_LINKS, link.count

            with pool.Fori(0, B - 1) as b:
                batch(b, True)
            batch(B - 1, False)

        @block.scalar
        def _(act):
            def scale_blocks(n, w):
                act.wait_ge(q_scale_done, n + 1)
                a = source = work[:, w, 0, :]
                if isinstance(n, int) and 2 <= n < NT:
                    source = ctx_place(0, n)
                    act.wait_ge(q_done, n - 1)
                for kb in range(KD):
                    cols = slice(kb * P, (kb + 1) * P)
                    ins = nc.scalar.activation(a[:, cols], source[:, cols], ACT.Copy, scale=quant[:, w, kb:kb + 1])
                ins.then_inc(q_scaled, 1)

            def keep_w(n, t, bank):
                act.wait_ge(q_turned, n + 1)
                nc.scalar.activation(wT[:, :, t * P:(t + 1) * P], by_block(banks16(bank)), ACT.Copy).then_inc(q_copied, 1)

            def keep_x(n, t, bank):
                act.wait_ge(q_turned, n + 1)
                nc.scalar.activation(qT[:, t, :, :], by_block(banks16(bank)), ACT.Copy).then_inc(q_copied, 1)

            def squares(b, t):
                act.wait_ge(affine_done, nth(b, t) + 1)
                w = t % 2
                scratch = eT[:, t, :] if isinstance(b, int) else work[:, w, 1, :]
                nc.scalar.activation(scratch, y_of(b, t), ACT.Square, accum_out=norm[:, w, 3:4]).then_inc(squares_done, 1)

            def unit(b, t):
                act.wait_ge(rl2_done, nth(b, t) + 1)
                nc.scalar.activation(y_of(b, t), y_of(b, t), ACT.Copy, scale=norm[:, t % 2, 5:6]).then_inc(unit_done, 1)

            def keep_u(b, t, par, bank):
                act.wait_ge(unit_turned, nth(b, t) + 1)
                hold(act)
                nc.scalar.activation(u_view(uT_hi, par, t), by_block(bank[:, :]), ACT.Copy).then_inc(uT_hi_done, 1)

            def exp(i, j, reused):
                act.wait_ge(l_done, i + j + 1)
                if reused:
                    act.wait_ge(t_done, i + j - 3)
                    act.wait_ge(eT_lo_done, i + j - 3)
                nc.scalar.activation(eT[:, j, :], ps_l[:, :], ACT.Exp, bias=shift[:, :], scale=logit_scale[:, :],
                                     accum_out=den[:, j:j + 1]).then_inc(exp_done, 1)

            def split_y(i, j, par):
                act.wait_ge(y_done, i + j + 1)
                hold(act)
                nc.scalar.activation(y_hi[:, j, :], ps_y[:, :], ACT.Copy, scale=y_scale[:, bass.ds(par * NT + j, 1)]).then_inc(y_hi_done, 1)

            def split_e(i, j):
                act.wait_ge(t_done, i + j + 1)
                nc.scalar.activation(e_hi[:, j, :, :], ps_t[:, :].rearrange("p (t s) -> p t s", s=S), ACT.Copy).then_inc(e_hi_done, 1)

            def split_z(i, j, final):
                bank, hi, _ = z_place(j, final)
                act.wait_ge(z_done, i + j + 1)
                nc.scalar.activation(hi, bank[:, :], ACT.Copy).then_inc(z_hi_done, 1)

            def group(b, g, follows, par, aside):
                i = b * E + g * G
                aside(g, "s")
                act.wait_ge(hb_done, b * NG + g + 1)
                nc.scalar.activation(hn[:, :, :], hn[:, :, :], ACT.Gelu).then_inc(gelu_done, 1)
                aside(g, "h")
                for j in range(G):
                    if follows and j == 0:
                        exp(i + G, 0, True)
                        split_y(i + G, 0, par)
                    split_z(i, j, not follows)
                    aside(g, f"x{j}")
                    if follows and j + 1 < G:
                        exp(i + G, j + 1, True)
                    aside(g, f"z{j}")
                    if follows and j + 1 < G:
                        split_y(i + G, j + 1, par)
                    aside(g, f"y{j}")
                    if follows:
                        split_e(i + G, j)
                    aside(g, f"e{j}")

            def batch(b, follows):
                n_x, n_w = b * (2 * NT) + FIRST_Q, b * (2 * NT) + (FIRST_Q + NT)
                this, after = b % 2, (b + 1) % 2

                def aside(g, at):
                    if not follows:
                        return
                    at = (g, at)
                    if at == (0, "z0"):
                        scale_blocks(n_x, 0)
                    elif at == (0, "y0"):
                        scale_blocks(n_x + 1, 1)
                    elif at == (0, "y1"):
                        keep_x(n_x, 0, ps_l)
                    elif at == (0, "e1"):
                        keep_x(n_x + 1, 1, ps_y)
                        scale_blocks(n_x + 2, 0)
                    elif at == (0, "z2"):
                        scale_blocks(n_x + 3, 1)
                    elif at == (1, "s"):
                        keep_x(n_x + 2, 2, ps_zh)
                    elif at == (1, "z0"):
                        keep_x(n_x + 3, 3, ps_t)
                    elif at == (2, "x0"):
                        squares(b + 1, 0)
                    elif at == (2, "z0"):
                        squares(b + 1, 1)
                        unit(b + 1, 0)
                    elif at == (2, "y0"):
                        unit(b + 1, 1)
                    elif at == (2, "e0"):
                        keep_u(b + 1, 0, after, ps_y)
                    elif at == (2, "y1"):
                        keep_u(b + 1, 1, after, ps_l)
                    elif at == (2, "e1"):
                        squares(b + 1, 2)
                    elif at == (2, "z2"):
                        unit(b + 1, 2)
                        squares(b + 1, 3)
                    elif at == (2, "y2"):
                        keep_u(b + 1, 2, after, ps_l)
                    elif at == (2, "e2"):
                        unit(b + 1, 3)
                    elif at == (2, "e3"):
                        keep_u(b + 1, 3, after, ps_l)
                    elif at == (3, "x0"):
                        scale_blocks(n_w, 0)
                        scale_blocks(n_w + 1, 1)
                    elif at == (3, "y1"):
                        keep_w(n_w, 0, ps_l)
                    elif at == (3, "e1"):
                        scale_blocks(n_w + 2, 0)
                        scale_blocks(n_w + 3, 1)
                        keep_w(n_w + 1, 1, ps_y)
                    elif at == (3, "e2"):
                        keep_w(n_w + 2, 2, ps_y)
                    elif at == (3, "e3"):
                        keep_w(n_w + 3, 3, ps_l)

                for g in range(NG):
                    group(b, g, follows or g < NG - 1, after if g == NG - 1 else this, aside)

            act.wait_ge(consts_in, 16 * 5)
            nc.scalar.activation(tgx[:, :], gx[:, :], ACT.Tanh).then_inc(tanh_done, 1)
            nc.scalar.activation(tgf[:, :], gf[:, :], ACT.Tanh).then_inc(tanh_done, 1)
            for k in range(KD):
                n = 2 * k
                keep = keep_w if n < NT else keep_x
                scale_blocks(n, 0)
                scale_blocks(n + 1, 1)
                keep(n, n % NT, ps_t)
                keep(n + 1, n % NT + 1, ps_y)
                for i in ((0,), (1, 2), (3,), ())[k]:
                    act.wait_ge(mu_in[i], 16)
                    nc.scalar.activation(mu_squares[i], mu_raw[:, i, :], ACT.Square).then_inc(mu_squared, 1)

            def high_w1(k):
                act.wait_ge(w1_in[k], 16)
                if k == 0:
                    act.wait_ge(dve_w1, W1_LINKS)
                nc.scalar.activation(w1_hi[:, k, :], w1_raw[:, k, :], ACT.Copy, scale=w1_unit[:, 3:4]).then_inc(w1_hi_done, 1)

            def high_mu(k):
                act.wait_ge(mu_scaled, k + 1)
                nc.scalar.activation(mu_hi[:, k, :], mu_raw[:, k, :], ACT.Copy).then_inc(mu_hi_done, 1)

            def both(stage, t):
                stage(0, t)
                stage(0, t + 1)

            high_mu(0)
            high_mu(1)
            both(squares, 0)
            high_w1(0)
            high_mu(2)
            both(unit, 0)
            high_w1(1)
            keep_u(0, 0, 0, ps_t)
            keep_u(0, 1, 0, ps_y)
            high_mu(3)
            high_w1(2)
            both(squares, 2)
            high_w1(3)
            both(unit, 2)
            keep_u(0, 2, 0, ps_l)
            keep_u(0, 3, 0, ps_zh)
            for j in range(G):
                exp(0, j, False)
                split_y(0, j, 0)
                n = 2 * NT + j
                if j % 2 == 0:
                    scale_blocks(n, 0)
                    scale_blocks(n + 1, 1)
                split_e(0, j)
                if j >= 2:
                    n = 2 * NT + 2 * (j - 2)
                    keep_w(n, n % NT, acc[n % NT])
                    keep_w(n + 1, n % NT + 1, acc[n % NT + 1])
            with act.Fori(0, B - 1) as b:
                batch(b, True)
            batch(B - 1, False)

        @block.vector
        def _(dve):
            def statistics(src, w, link, done):
                link.then(nc.vector.bn_stats(stat[:, w, 0:6], src))
                hold(dve)
                link.then(nc.vector.bn_aggr(stat[:, w, 6:8], stat[:, w, 0:6]))
                nc.vector.tensor_scalar(stat[:, w, 7:8], stat[:, w, 7:8], LN_EPS, None, ALU.add).then_inc(done, 1)

            def standardise(dst, src, w, col, waits, n):
                dve.wait_ge(waits, n + 1)
                return nc.vector.tensor_scalar(dst, src, stat[:, w, 6:7], norm[:, w, col:col + 1], ALU.subtract, ALU.mult)

            def w_amax(b, t):
                dve.wait_ge(ctx_in[t], b * 16 + 16)
                nc.vector.tensor_reduce(amax[:, t % 2, :], by_block(ctx_place(b, t)), AX_X, ALU.max,
                                        apply_absolute_value=True).then_inc(w_amax_done, 1)

            def w_scale(b, t, n, link):
                w = t % 2
                dve.wait_ge(w_amax_all, nth(b, t) + 1)
                link.then(nc.vector.tensor_scalar(w_dequant[:, :, t], amax_all[:, w, :], W_EPS, 1.0 / FP8_MAX, ALU.max, ALU.mult))
                nc.vector.reciprocal(quant[:, w, :], w_dequant[:, :, t]).then_inc(q_scale_done, 1)

            def x_stats(b, t, link):
                dve.wait_ge(x_in[t], b * 16 + 16)
                statistics(x1[:, t, :], t % 2, link, x_var_done)

            def x_scale(b, t, n, link):
                w = t % 2
                a = work[:, w, 0, :]
                dve.wait_ge(q_done, n - 1)
                link.then(standardise(a, x1[:, t, :], w, 0, x_rstd_done, nth(b, t)))
                link.then(nc.vector.tensor_reduce(amax[:, w, :], by_block(a), AX_X, ALU.max, apply_absolute_value=True))
                link.then(nc.vector.tensor_scalar(x_dequant[:, t, :], amax[:, w, :], ACT_EPS, 1.0 / FP8_MAX, ALU.max, ALU.mult))
                link.then(nc.vector.reciprocal(quant[:, w, :], x_dequant[:, t, :]))
                nc.vector.tensor_scalar(x_dequant[:, t, :], x_dequant[:, t, :], tgx[:, :], None, ALU.mult).then_inc(q_scale_done, 1)

            def step(n, w, link):
                a, m = work[:, w, 0, :], work[:, w, 1, :]
                dve.wait_ge(q_scaled, n + 1)
                link.then(nc.vector.tensor_scalar(m.bitcast(I32), a.bitcast(I32), EXP_MASK, None, ALU.bitwise_and))
                nc.vector.tensor_scalar(m, m, 2.0 ** -6, 1.5 * 2.0 ** 20, ALU.max, ALU.mult).then_inc(q_step_done, 1)

            def early_round(n, w, link):
                a, m = work[:, w, 0, :], work[:, w, 1, :]
                dve.wait_ge(q_step_done, n + 1)
                link.then(nc.vector.tensor_tensor(a, a, m, ALU.add))
                if n >= 2:
                    dve.wait_ge(q_turned, n - 1)
                nc.vector.tensor_tensor(q16[:, w, :], a, m, ALU.subtract).then_inc(q_done, 1)

            def dequants(t, link):
                link.then(nc.vector.tensor_tensor(dequant[:, t % 2, :, :], spread(x_dequant[:, t, :], NT), w_dequant[:, :, :], ALU.mult))

            def scale_product(b, t, kb, bank, first=False):
                n, w = nth_product(b, t, kb), t % 2
                dve.wait_ge(prod_done, n + 1)
                if not first:
                    dve.wait_ge(prod_added, n - 1)
                nc.vector.tensor_tensor(by_block(prod[:, w, :]), by_block(bank[:, :]), spread(dequant[:, w, kb, :]), ALU.mult).then_inc(prod_scaled, 1)

            def stats1(b, t, link):
                dve.wait_ge(prod_added, nth_product(b, t, KD - 1) + 1)
                statistics(x1[:, t, :], t % 2, link, var1_done)

            def stats2(b, t, link):
                y = y_of(b, t)
                if t >= 2 and not isinstance(b, int):
                    dve.wait_ge(unit_turned, nth(b, t) - 1)
                link.then(standardise(y, x1[:, t, :], t % 2, 1, rstd1_done, nth(b, t)))
                statistics(y, t % 2, link, var2_done)

            def layernorm(b, t):
                y = y_of(b, t)
                standardise(y, y, t % 2, 2, rstd2_done, nth(b, t)).then_inc(ln_done, 1)

            def rl2(b, t, par, link):
                w = t % 2
                dve.wait_ge(l2_done, nth(b, t) + 1)
                link.then(nc.vector.tensor_scalar(norm[:, w, 4:5], norm[:, w, 4:5], L2_EPS, None, ALU.max))
                link.then(nc.vector.tensor_scalar(y_scale[:, bass.ds(par * NT + t, 1)], norm[:, w, 4:5], w1_unit[:, 4:5], None, ALU.mult))
                link.then(nc.vector.reciprocal(norm[:, w, 5:6], norm[:, w, 4:5]))
                nc.vector.tensor_scalar(norm[:, w, 5:6], norm[:, w, 5:6], UNIT, None, ALU.mult).then_inc(rl2_done, 1)

            def split_u(b, t, par, bank):
                dve.wait_ge(uT_hi_done, nth(b, t) + 1)
                nc.vector.tensor_tensor(u_view(uT_lo, par, t), by_block(bank[:, :]), u_view(uT_hi, par, t), ALU.subtract).then_inc(uT_lo_done, 1)

            def split_y(i, j, par):
                dve.wait_ge(y_hi_done, i + j + 1)
                nc.vector.scalar_tensor_tensor(y_lo[:, j, :], ps_y[:, :], y_scale[:, bass.ds(par * NT + j, 1)], y_hi[:, j, :].bitcast(F32),
                                               ALU.mult, ALU.subtract).then_inc(y_lo_done, 1)

            def split_z(i, j, final):
                bank, hi, lo = z_place(j, final)
                dve.wait_ge(z_hi_done, i + j + 1)
                nc.vector.tensor_tensor(lo, bank[:, :], hi.bitcast(F32), ALU.subtract).then_inc(z_lo_done, 1)

            def split_eT(i, j, reused):
                dve.wait_ge(exp_done, i + j + 1)
                if reused:
                    dve.wait_ge(z_done, i + j - 3)
                nc.vector.tensor_copy(eT_hi[:, j, :], eT[:, j, :]).then_inc(eT_hi_done, 1)
                dve.wait_ge(eT_hi_done, i + j + 1)
                nc.vector.tensor_tensor(eT_lo[:, j, :], eT[:, j, :], eT_hi[:, j, :].bitcast(F32), ALU.subtract).then_inc(eT_lo_done, 1)

            def split_e(i, e, j, par):
                dve.wait_ge(e_hi_done, i + j + 1)
                nc.vector.tensor_tensor(e_lo[:, j, :, :].rearrange("p t s -> p (t s)"), ps_t[:, :],
                                        e_hi[:, j, :, :].rearrange("p t s -> p (t s)").bitcast(F32), ALU.subtract).then_inc(e_lo_done, 1)
                nc.vector.tensor_reduce(mass[:, bass.ds(par * NT, NT), e + j], ps_t[:, :].rearrange("p (t s) -> p t s", s=S), AX_X,
                                        ALU.add).then_inc(e_sum_done, 1)

            def group(b, g, follows, par, aside):
                i, n = b * E + g * G, b * NG + g + 1
                aside(g, "s")
                dve.wait_ge(exp_done, i + G)
                nc.vector.reciprocal(rden[:, :], den[:, :]).then_inc(rden_done, 1)
                dve.wait_ge(rden_done, n)
                dve.wait_ge(h_done, n)
                nc.vector.tensor_tensor(hn[:, :, :], by_block(ps_y[:, :]), spread(rden[:, :]), ALU.mult).then_inc(hn_done, 1)
                dve.wait_ge(hn_done, n)
                dve.wait_ge(b1_in, n * 16)
                nc.vector.tensor_tensor(hn[:, :, :], hn[:, :, :], by_block(b1_bc[:, :]), ALU.add).then_inc(hb_done, 1)
                aside(g, "n")
                dve.wait_ge(gelu_done, n)
                nc.vector.tensor_copy(h_hi[:, :, :], hn[:, :, :]).then_inc(h_hi_done, 1)
                dve.wait_ge(h_hi_done, n)
                nc.vector.tensor_tensor(h_lo[:, :, :], hn[:, :, :], h_hi[:, :, :].bitcast(F32), ALU.subtract).then_inc(h_lo_done, 1)
                aside(g, "h")
                if follows:
                    split_y(i + G, 0, par)
                for j in range(G):
                    split_z(i, j, not follows)
                    if follows and j + 1 < G:
                        split_eT(i + G, j, True)
                    aside(g, f"z{j}")
                    if follows and j + 1 < G:
                        split_y(i + G, j + 1, par)
                    aside(g, f"y{j}")
                    if follows:
                        split_e(i + G, (g + 1) % NG * G, j, par)
                        if j + 1 == G:
                            split_eT(i + G, j, True)
                    aside(g, f"e{j}")

            def batch(b, follows):
                n_x, n_w = b * (2 * NT) + FIRST_Q, b * (2 * NT) + (FIRST_Q + NT)
                this, after = b % 2, (b + 1) % 2
                link = Chain(dve, dve_link, b * DVE_LINKS)

                def aside(g, at):
                    at = (g, at)
                    if at == (NG - 1, "z1" if follows else "s"):
                        dve.wait_ge(mass_turned, b + 1)
                        nc.vector.tensor_copy(massT_hi[:, :], ps_t[0:E, :]).then_inc(mass_split, 1)
                        dve.wait_ge(mass_split, b * 2 + 1)
                        nc.vector.tensor_tensor(massT_lo[:, :], ps_t[0:E, :], massT_hi[:, :].bitcast(F32), ALU.subtract).then_inc(mass_split, 1)
                    if not follows:
                        return
                    if at == (0, "n"):
                        x_stats(b + 1, 0, link)
                    elif at == (0, "h"):
                        x_scale(b + 1, 0, n_x, link)
                    elif at == (0, "z0"):
                        x_stats(b + 1, 1, link)
                        x_scale(b + 1, 1, n_x + 1, link)
                    elif at == (0, "y0"):
                        step(n_x, 0, link)
                    elif at == (0, "e0"):
                        step(n_x + 1, 1, link)
                    elif at == (0, "z1"):
                        x_stats(b + 1, 2, link)
                        x_stats(b + 1, 3, link)
                    elif at == (0, "e1"):
                        x_scale(b + 1, 2, n_x + 2, link)
                        x_scale(b + 1, 3, n_x + 3, link)
                    elif at == (0, "z2"):
                        dequants(0, link)
                        dequants(1, link)
                        scale_product(b + 1, 0, 0, ps_t)
                    elif at == (0, "y2"):
                        scale_product(b + 1, 1, 0, ps_l)
                    elif at == (0, "e2"):
                        step(n_x + 2, 0, link)
                        scale_product(b + 1, 0, 1, ps_y)
                    elif at == (0, "e3"):
                        step(n_x + 3, 1, link)
                        scale_product(b + 1, 1, 1, ps_l)
                    elif at == (1, "n"):
                        scale_product(b + 1, 0, 2, ps_t)
                    elif at == (1, "y0"):
                        scale_product(b + 1, 1, 2, ps_l)
                    elif at == (1, "e0"):
                        scale_product(b + 1, 0, 3, ps_y)
                    elif at == (1, "z1"):
                        scale_product(b + 1, 1, 3, ps_t)
                        stats1(b + 1, 0, link)
                        dequants(2, link)
                        dequants(3, link)
                    elif at == (1, "y1"):
                        scale_product(b + 1, 2, 0, ps_l)
                    elif at == (1, "e1"):
                        stats1(b + 1, 1, link)
                        scale_product(b + 1, 3, 0, ps_y)
                    elif at == (1, "z2"):
                        scale_product(b + 1, 2, 1, ps_t)
                        stats2(b + 1, 0, link)
                    elif at == (1, "y2"):
                        scale_product(b + 1, 3, 1, ps_l)
                    elif at == (1, "e2"):
                        scale_product(b + 1, 2, 2, ps_y)
                    elif at == (1, "e3"):
                        scale_product(b + 1, 3, 2, ps_l)
                        stats2(b + 1, 1, link)
                        layernorm(b + 1, 0)
                    elif at == (2, "n"):
                        scale_product(b + 1, 2, 3, ps_zh)
                    elif at == (2, "h"):
                        scale_product(b + 1, 3, 3, ps_t)
                        layernorm(b + 1, 1)
                    elif at == (2, "z0"):
                        rl2(b + 1, 0, after, link)
                        rl2(b + 1, 1, after, link)
                    elif at == (2, "y0"):
                        stats1(b + 1, 2, link)
                    elif at == (2, "e0"):
                        split_u(b + 1, 0, after, ps_y)
                        stats1(b + 1, 3, link)
                        stats2(b + 1, 2, link)
                    elif at == (2, "z1"):
                        layernorm(b + 1, 2)
                    elif at == (2, "y1"):
                        split_u(b + 1, 1, after, ps_l)
                        stats2(b + 1, 3, link)
                    elif at == (2, "e1"):
                        layernorm(b + 1, 3)
                    elif at == (2, "z2"):
                        rl2(b + 1, 2, after, link)
                    elif at == (2, "y2"):
                        split_u(b + 1, 2, after, ps_l)
                    elif at == (2, "e2"):
                        rl2(b + 1, 3, after, link)
                    elif at == (2, "e3"):
                        split_u(b + 1, 3, after, ps_l)
                    elif at == (3, "s"):
                        w_amax(b + 2, 0)
                        w_amax(b + 2, 1)
                    elif at == (3, "n"):
                        w_scale(b + 2, 0, n_w, link)
                        w_scale(b + 2, 1, n_w + 1, link)
                    elif at == (3, "z0"):
                        step(n_w, 0, link)
                        step(n_w + 1, 1, link)
                    elif at == (3, "z1"):
                        w_amax(b + 2, 2)
                        w_amax(b + 2, 3)
                    elif at == (3, "y1"):
                        w_scale(b + 2, 2, n_w + 2, link)
                        w_scale(b + 2, 3, n_w + 3, link)
                    elif at == (3, "e1"):
                        step(n_w + 2, 0, link)
                        step(n_w + 3, 1, link)

                for g in range(NG):
                    if g == NG - 1:
                        dve.wait_ge(e_sum_done, b * E + E)
                        nc.vector.tensor_copy(mass_sum[:, :, :], mass[:, bass.ds(this * NT, NT), :]).then_inc(mass_sum_done, 1)
                        nc.vector.tensor_reduce(z_row[:, :], mass[:, bass.ds(this * NT, NT), :], AX_X, ALU.add).then_inc(zr_done, 1)
                        dve.wait_ge(zr_done, b * 3 + 1)
                        nc.vector.reciprocal(z_inv[:, :], z_row[:, :]).then_inc(zr_done, 1)
                        dve.wait_ge(zr_done, b * 3 + 2)
                        nc.vector.tensor_scalar(z_inv[:, :], z_inv[:, :], tgf[:, :], None, ALU.mult).then_inc(zr_done, 1)
                    group(b, g, follows or g < NG - 1, after if g == NG - 1 else this, aside)
                assert not follows or link.count == DVE_LINKS, link.count
                if follows:
                    dve.wait_ge(sums_done, b + 1)
                else:
                    dve.wait_ge(f_done, B * E + 2)
                for t in range(NT):
                    dve.wait_ge(last_in[t], b * 16 + 16)
                    nc.vector.scalar_tensor_tensor(last[:, t, :], acc[t][:, :], z_inv[:, t:t + 1], last[:, t, :], ALU.mult,
                                                   ALU.add).then_inc(out_ready, 1)

            link, w = Chain(dve, dve_early), Chain(dve, dve_w1)

            def w1_largest(k):
                dve.wait_ge(w1_in[k], 16)
                w.then(nc.vector.tensor_reduce(w1_max[:, k:k + 1], w1_raw[:, k, :], AX_X, ALU.max, apply_absolute_value=True))

            def both(stage, t):
                stage(0, t)
                stage(0, t + 1)

            def products(t, kb):
                for i in (t, t + 1):
                    scale_product(0, i, kb, EARLY_BANKS[(2 * kb + i % 2) % 4], first=(i < 2 and kb == 0))

            def scale_mu(k):
                for i in range(NT):
                    cols = slice(i * W, (i + 1) * W)
                    ins = nc.vector.tensor_tensor(mu_raw[:, k, cols], mu_raw[:, k, cols], acc[i][:, :], ALU.mult)
                ins.then_inc(mu_scaled, 1)

            def low_w1(k):
                dve.wait_ge(w1_hi_done, k + 1)
                nc.vector.scalar_tensor_tensor(w1_lo[:, k, :], w1_raw[:, k, :], w1_unit[:, 3:4], w1_hi[:, k, :], ALU.mult,
                                               ALU.subtract).then_inc(w1_lo_done, 1)

            def step_and_round(n):
                for i in (n, n + 1):
                    step(i, i % 2, link)
                for i in (n, n + 1):
                    early_round(i, i % 2, link)

            for t in range(0, NT, 2):
                for i in (t, t + 1):
                    w_amax(0, i)
                for i in (t, t + 1):
                    w_scale(0, i, i, link)
                if t > 0:
                    for i in (0, 1):
                        x_stats(0, i, link)
                step_and_round(t)
            dve.wait_ge(tanh_done, 2)
            for t in range(0, NT, 2):
                for i in (t, t + 1):
                    if t > 0:
                        x_stats(0, i, link)
                for i in (t, t + 1):
                    x_scale(0, i, NT + i, link)
                step_and_round(NT + t)
            s = Chain(dve, dve_small)
            s.then(nc.vector.tensor_scalar(logit_scale[:, :], sc_in[:, :], 1.0 / (UNIT * UNIT), None, ALU.mult))
            s.then(nc.vector.tensor_reduce(shift[:, :], sc_in[:, :], AX_X, ALU.max, apply_absolute_value=True))
            s.then(nc.vector.tensor_scalar(shift[:, :], shift[:, :], LOGIT_ROOM, None, ALU.subtract))
            s.then(nc.vector.tensor_scalar(shift[:, :], shift[:, :], 0.0, -1.0, ALU.max, ALU.mult))
            dve.wait_ge(b2_in, 16)
            s.then(nc.vector.tensor_copy(b2_hi[:, :], b2_raw))
            s.then(nc.vector.tensor_tensor(b2_lo[:, :], b2_raw, b2_hi[:, :].bitcast(F32), ALU.subtract))
            dequants(0, link)
            dequants(1, link)
            products(0, 0)
            products(0, 1)
            w1_largest(0)
            dve.wait_ge(mu_summed, 1)
            nc.vector.tensor_scalar(mu_norm[:, 0, :], acc[0][:, 0:E], L2_EPS * L2_EPS, None, ALU.max).then_inc(mu_clamped, 1)
            products(0, 2)
            w1_largest(1)
            products(0, 3)
            dve.wait_ge(mu_rooted, 1)
            for e in range(E):
                if e >= 4:
                    dve.wait_ge(mu_spread, e - 3)
                nc.vector.tensor_scalar(diag[:, e % 4, :], ident[:, :], mu_norm[:, 1, e:e + 1], UNIT, ALU.mult, ALU.mult).then_inc(mu_diag, 1)
            both(lambda b, i: stats1(b, i, link), 0)
            dequants(2, link)
            dequants(3, link)
            products(2, 0)
            both(lambda b, i: stats2(b, i, link), 0)
            products(2, 1)
            dve.wait_ge(mu_spread, E)
            scale_mu(0)
            both(layernorm, 0)
            products(2, 2)
            scale_mu(1)
            products(2, 3)
            w1_largest(2)
            both(lambda b, i: stats1(b, i, link), 2)
            w1_largest(3)
            w.then(nc.vector.tensor_reduce(w1_unit[:, 0:1], w1_max[:, :], AX_X, ALU.max))
            dve.wait_ge(w1_all_max, 1)
            w.then(nc.vector.tensor_scalar(w1_unit[:, 2:3].bitcast(I32), w1_unit[:, 1:2].bitcast(I32), EXP_MASK, None, ALU.bitwise_and))
            w.then(nc.vector.tensor_scalar(w1_unit[:, 2:3], w1_unit[:, 2:3], 2.0 ** -100, 2.0 ** -14, ALU.max, ALU.mult))
            w.then(nc.vector.reciprocal(w1_unit[:, 3:4], w1_unit[:, 2:3]))
            w.then(nc.vector.tensor_scalar(w1_unit[:, 4:5], w1_unit[:, 2:3], 1.0 / UNIT, None, ALU.mult))
            assert w.count == W1_LINKS
            scale_mu(2)
            both(lambda b, i: stats2(b, i, link), 2)
            both(lambda b, i: rl2(b, i, 0, link), 0)
            both(layernorm, 2)
            scale_mu(3)
            split_u(0, 0, 0, ps_t)
            split_u(0, 1, 0, ps_y)
            low_w1(0)
            low_w1(1)
            dve.wait_ge(mu_hi_done, KD)
            nc.vector.tensor_tensor(mu_lo[:, KD - 1, :], mu_raw[:, KD - 1, :], mu_hi[:, KD - 1, :], ALU.subtract).then_inc(mu_lo_done, 1)
            both(lambda b, i: rl2(b, i, 0, link), 2)
            low_w1(2)
            low_w1(3)
            split_u(0, 2, 0, ps_l)
            split_u(0, 3, 0, ps_zh)

            def amax_and_scale(t):
                for i in (t, t + 1):
                    w_amax(1, i)
                for i in (t, t + 1):
                    w_scale(1, i, 2 * NT + i, link)

            for j in range(G):
                if j == 0:
                    amax_and_scale(0)
                split_y(0, j, 0)
                split_eT(0, j, False)
                split_e(0, 0, j, 0)
                if j == 0:
                    step_and_round(2 * NT)
                elif j == 1:
                    amax_and_scale(2)
                elif j == G - 1:
                    step_and_round(2 * NT + 2)
            with dve.Fori(0, B - 1) as b:
                batch(b, True)
            batch(B - 1, False)

        @block.tensor
        def _(pe):
            def three(out, terms, start=True, stop=True, check=True):
                todo = []
                for a_hi, a_lo, b_hi, b_lo in terms:
                    todo += [(a_hi, b_hi), (a_hi, b_lo), (a_lo, b_hi)]
                for n, (a, c) in enumerate(todo):
                    ins = nc.tensor.matmul(out, a, c, start=start and n == 0, stop=stop and n == len(todo) - 1,
                                           skip_group_check=not check)
                return ins

            def turn_q(n, w, bank):
                pe.wait_ge(q_done, n + 1)
                for kb in range(KD):
                    ins = nc.tensor.transpose(banks16(bank)[:, kb * P:(kb + 1) * P], q16[:, w, kb * P:(kb + 1) * P], ident16[:, :])
                ins.then_inc(q_turned, 1)

            def product(b, t, kb, bank, n_q):
                pe.wait_ge(q_copied, n_q)
                nc.tensor.matmul(bank[:, :], qT[:, t, kb, :], wT[:, kb, :], start=True, stop=True).then_inc(prod_done, 1)

            def turn_u(b, t, bank):
                pe.wait_ge(unit_done, nth(b, t) + 1)
                for kb in range(KD):
                    ins = nc.tensor.transpose(bank[:, kb * P:(kb + 1) * P], y_of(b, t)[:, kb * P:(kb + 1) * P], ident[:, :])
                ins.then_inc(unit_turned, 1)

            u_reg = pe.alloc_register("u_reg")

            def u_base(par):
                pe.reg_mov(u_reg, par * (KD * N))
                return pe.snap(u_reg, min_val=0, max_val=KD * N)

            def logits(i, j, g, par):
                cols = bass.ds(g * W + j * S, S)
                base = u_base(par)
                three(ps_l[:, :], [(mu_hi[:, k, cols], mu_lo[:, k, cols], uT_hi[:, bass.ds(base + k * N, N)],
                                    uT_lo[:, bass.ds(base + k * N, N)]) for k in range(KD)]).then_inc(l_done, 1)

            def project(i, j, g, par):
                cols = bass.ds(g * W, W)
                base = u_base(par)
                three(ps_y[:, :], [(uT_hi[:, bass.ds(base + (k * N + j * P), P)], uT_lo[:, bass.ds(base + (k * N + j * P), P)],
                                    w1_hi[:, k, cols], w1_lo[:, k, cols]) for k in range(KD)]).then_inc(y_done, 1)

            def turn(i, j):
                pe.wait_ge(exp_done, i + j + 1)
                for t in range(NT):
                    ins = nc.tensor.transpose(ps_t[:, t * P:(t + 1) * P], eT[:, j, t * P:(t + 1) * P], ident[:, :])
                ins.then_inc(t_done, 1)

            def one(n, out, a_hi, a_lo, b_hi, b_lo, start, stop, check=True):
                return nc.tensor.matmul(out, a_lo if n == 2 else a_hi, b_lo if n == 1 else b_hi, start=start and n == 0,
                                        stop=stop and n == 2, skip_group_check=not check)

            def slot_pass(i, j, t, n):
                cols = slice(j * H, (j + 1) * H)
                return one(n, ps_y[:, cols], e_hi[:, j, t, :], e_lo[:, j, t, :], y_hi[:, t, cols], y_lo[:, t, cols], t == 0, t == NT - 1)

            def slots(i, j):
                pe.wait_ge(e_lo_done, i + j + 1)
                for t in range(NT):
                    for n in range(3):
                        ins = slot_pass(i, j, t, n)
                if j == G - 1:
                    ins.then_inc(h_done, 1)

            def combine(i, j, n, final=False):
                if j == 0:
                    pe.wait_ge(h_lo_done, n)
                elif not final:
                    pe.wait_ge(z_lo_done, i + j)
                elif j == G - 1:
                    pe.wait_ge(z_lo_done, i + 1)
                pe.wait_ge(eT_lo_done, i + j + 1)
                three(z_place(j, final)[0][:, :], [(h_hi[:, j, :], h_lo[:, j, :], eT_hi[:, j, :], eT_lo[:, j, :])]).then_inc(z_done, 1)

            def expand(i, j, first=False, final=False):
                pe.wait_ge(z_lo_done, i + j + 1)
                pe.wait_ge(w2_split, i + j + 1)
                for t in range(NT):
                    for n in range(3):
                        ins = expand_pass(j, t, n, first, final)
                ins.then_inc(f_done, 1)

            def expand_pass(j, t, n, first, final):
                _, hi, lo = z_place(j, final)
                rows = slice(t * P, (t + 1) * P)
                return one(n, acc[t][:, :], hi[:, rows], lo[:, rows], w2_hi[:, j % 2, :], w2_lo[:, j % 2, :], first, False, check=False)

            def batch(b, follows):
                n_x, n_w = b * (2 * NT) + FIRST_Q, b * (2 * NT) + (FIRST_Q + NT)
                this, after = b % 2, (b + 1) % 2
                plan = {
                    (0, "c1"): ("x", 0), (0, "b1"): ("x", 1), (0, "a2"): ("p", 0, 0), (0, "c2"): ("p", 1, 0), (0, "b2"): ("p", 0, 1),
                    (0, "c3"): ("p", 1, 1),
                    (1, "bs"): ("x", 2), (1, "as"): ("p", 0, 2), (1, "a0"): ("x", 3), (1, "c0"): ("p", 1, 2), (1, "b0"): ("p", 0, 3),
                    (1, "a1"): ("p", 1, 3), (1, "c1"): ("p", 2, 0), (1, "b1"): ("p", 3, 0), (1, "a2"): ("p", 2, 1), (1, "c2"): ("p", 3, 1),
                    (1, "b2"): ("p", 2, 2), (1, "c3"): ("p", 3, 2),
                    (2, "bs"): ("p", 2, 3), (2, "as"): ("p", 3, 3),
                    (2, "b0"): ("u", 0), (2, "c1"): ("u", 1), (2, "c2"): ("u", 2), (2, "c3"): ("u", 3),
                    (3, "c1"): ("w", 0), (3, "b1"): ("w", 1), (3, "b2"): ("w", 2), (3, "c3"): ("w", 3),
                } if follows else {}
                if follows:
                    plan[(3, "a1")] = ("m",)
                bank_of = {"a": ps_t, "b": ps_y, "c": ps_l}

                def read(g, place):
                    what = plan.get((g % NG, place))
                    if what is None:
                        return
                    kind = what[0]
                    if kind == "x":
                        pe.wait_ge(q_copied, n_x + what[1] + 1)
                    elif kind == "w":
                        pe.wait_ge(q_copied, n_w + what[1] + 1)
                    elif kind == "p":
                        pe.wait_ge(prod_scaled, nth_product(b + 1, what[1], what[2]) + 1)
                    elif kind == "u":
                        pe.wait_ge(uT_lo_done, nth(b + 1, what[1]) + 1)
                    else:
                        pe.wait_ge(mass_split, b * 2 + 2)

                def aside(g, place, i):
                    what = plan.get((g, place))
                    if what is None:
                        return
                    kind, bank = what[0], ps_zh if place == "bs" else bank_of[place[0]]
                    j = 0 if place[1] == "s" else int(place[1])
                    if place[0] == "a":
                        pe.wait_ge(e_sum_done, i + j if follows else i)
                    elif place[0] == "c":
                        pe.wait_ge(exp_done, i + min(j + 2, G))
                    elif place != "bs":
                        pe.wait_ge(y_lo_done, i + min(j + 2, G))
                    if place == "a0":
                        read(g, "as")
                    if place == "c3":
                        read(g, "c2")
                    if kind == "x":
                        turn_q(n_x + what[1], what[1] % 2, bank)
                    elif kind == "w":
                        turn_q(n_w + what[1], what[1] % 2, bank)
                    elif kind == "p":
                        product(b + 1, what[1], what[2], bank, n_x + (what[1] + 1 if what[1] < 2 else NT))
                    elif kind == "u":
                        turn_u(b + 1, what[1], bank)
                    else:
                        turn_masses()

                def turn_masses():
                    pe.wait_ge(mass_sum_done, b + 1)
                    for t in range(NT):
                        ins = nc.tensor.transpose(ps_t[0:E, t * P:(t + 1) * P], mass_sum[:, t, :], ident[:, :])
                    ins.then_inc(mass_turned, 1)

                def masses(*tiles):
                    pe.wait_ge(mass_split, b * 2 + 2)
                    for t in tiles:
                        for k in range(3):
                            ins = mass_pass(t, k)
                    return ins

                for g in range(NG):
                    i, n = b * E + g * G, b * NG + g + 1
                    more = follows or g < NG - 1
                    par, nxt = (after, 0) if g == NG - 1 else (this, g + 1)
                    aside(g, "bs", i + G)
                    aside(g, "as", i + G)
                    if more:
                        if g > 0:
                            read(g - 1, "c3")
                        else:
                            pe.wait_ge(q_copied, n_x)
                        if g == NG - 1:
                            pe.wait_ge(uT_lo_done, b * NT + 2 * NT)
                        pe.wait_ge(exp_done, i + G)
                        logits(i + G, 0, nxt, par)
                        pe.wait_ge(hn_done, n)
                        project(i + G, 0, nxt, par)
                    if not more:
                        masses(*range(NT))
                        combine(i, 0, n, final=True)
                        for j in range(G):
                            if j + 1 < G:
                                combine(i, j + 1, n, final=True)
                            expand(i, j, final=True)
                        break
                    for j in range(G):
                        if j == 0:
                            read(g, "bs")
                        combine(i, j, n)
                        if j + 1 < G:
                            aside(g, f"a{j}", i + G)
                        if more and j + 1 < G:
                            pe.wait_ge(exp_done, i + G + j + 1)
                            if j >= 1:
                                read(g, f"c{j - 1}")
                            logits(i + G, j + 1, nxt, par)
                            pe.wait_ge(y_lo_done, i + G + j + 1)
                            if j >= 1:
                                read(g, f"b{j - 1}")
                            project(i + G, j + 1, nxt, par)
                        if j + 1 < G:
                            aside(g, f"c{j}", i + G)
                        if more:
                            if j >= 1:
                                pe.wait_ge(e_sum_done, i + G + j)
                            if j + 1 < G:
                                read(g, f"a{j}")
                            if j == 0:
                                read(g, "as")
                            turn(i + G, j)
                        if j + 1 < G:
                            expand(i, j, first=(g == 0 and j == 0))
                            aside(g, f"b{j}", i + G)
                        if g == NG - 1 and j in (1, 2):
                            masses(j - 1)
                    aside(g, f"c{G - 1}", i + G)
                    pe.wait_ge(y_lo_done, i + 2 * G)
                    read(g, f"b{G - 2}")
                    slots(i + G, 0)
                    slots(i + G, 1)
                    expand(i, G - 1)
                    if g == NG - 1:
                        masses(2, 3).then_inc(sums_done, 1)
                    slots(i + G, 2)
                    if g == NG - 2 and not follows:
                        turn_masses()
                    slots(i + G, 3)

            def mass_pass(t, n):
                rows = slice(t * P, (t + 1) * P)
                return one(n, acc[t][:, :], massT_hi[:, rows], massT_lo[:, rows], b2_hi[:, :], b2_lo[:, :], False, True, check=False)

            def early_product(i, kb):
                at = nth_product(0, i, kb)
                if at >= 4:
                    pe.wait_ge(prod_scaled, at - 3)
                product(0, i, kb, EARLY_BANKS[(2 * kb + i % 2) % 4], 2 * NT)

            pe.wait_ge(pool_const, 5)
            pe.wait_ge(ones_done, 1)
            for n in range(2 * NT):
                if n >= 2:
                    pe.wait_ge(q_copied, n - 1)
                turn_q(n, n % 2, (ps_t, ps_y)[n % 2])
            pe.wait_ge(q_copied, 2 * NT)
            pe.wait_ge(dve_small, 6)
            for kb in (0, 1):
                early_product(0, kb)
                early_product(1, kb)
            pe.wait_ge(mu_added, KD - 1)
            for e in range(E):
                ins = nc.tensor.matmul(acc[0][:, e:e + 1], mu_squares[0][:, e * S:(e + 1) * S], ones[:, 0:1], start=True, stop=True)
            ins.then_inc(mu_summed, 1)
            for kb in (2, 3):
                early_product(0, kb)
                early_product(1, kb)
            for e in range(E):
                pe.wait_ge(mu_diag, e + 1)
                nc.tensor.matmul(acc[e // G][:, e % G * S:(e % G + 1) * S], ones, diag[:, e % 4, :], start=True, stop=True).then_inc(mu_spread, 1)
            for kb in range(KD):
                early_product(2, kb)
                early_product(3, kb)
            pe.wait_ge(prod_scaled, NT * KD)
            for t, bank in enumerate((ps_t, ps_y, ps_l, ps_zh)):
                turn_u(0, t, bank)
            pe.sem_inc(f_done, 2)
            pe.wait_ge(uT_lo_done, NT)
            pe.wait_ge(mu_lo_done, KD)
            for j in range(G):
                if j >= 1:
                    pe.wait_ge(exp_done, j)
                logits(0, j, 0, 0)
                if j == 0:
                    pe.wait_ge(w1_lo_done, KD)
                else:
                    pe.wait_ge(y_lo_done, j)
                project(0, j, 0, 0)
                if j >= 1:
                    pe.wait_ge(e_sum_done, j)
                turn(0, j)
                if j == 2:
                    for n in (0, 1):
                        turn_q(2 * NT + n, n % 2, acc[n])
            pe.wait_ge(exp_done, G)
            pe.wait_ge(y_lo_done, G)
            for j in range(G):
                slots(0, j)
            for n in (2, 3):
                turn_q(2 * NT + n, n % 2, acc[n])
            with pe.Fori(0, B - 1) as b:
                batch(b, True)
            batch(B - 1, False)


_INS = ["x", "ctx_2048", "g_xattn", "g_ffn", "L0_ffn_gamma", "L0_ffn_beta", "L0_ffn_mu", "L0_ffn_scale",
        "L0_ffn_W1", "L0_ffn_b1", "L0_ffn_W2", "L0_ffn_b2"]


def kernel(**inputs):
    import numpy as _np
    import concourse.bacc as _bacc
    from concourse import mybir as _mybir
    from concourse.bass_utils import run_bass_kernel_spmd as _run

    nc = _bacc.Bacc("TRN2", target_bir_lowering=False, num_devices=1)
    arrays, args = {}, []
    for name in _INS:
        a = _np.ascontiguousarray(inputs[name])
        arrays[f"in_{name}_dram"] = a
        args.append(nc.dram_tensor(f"in_{name}_dram", a.shape, _mybir.dt.from_np(a.dtype), kind="ExternalInput").ap())
    args.append(nc.dram_tensor("out_dram", arrays["in_x_dram"].shape, _mybir.dt.float32, kind="ExternalOutput").ap())
    flamingo_block(nc, *args)
    r = _run(nc, [arrays], core_ids=[0])
    return r.results[0]["out_dram"]
```
